# Optimizing a Trainium2 kernel written in Bass

```python
import numpy as np
import jax
import jax.numpy as jnp

def _softmax(x, axis=-1):
    return jax.nn.softmax(x, axis=axis)

def _gelu(x):
    return jax.nn.gelu(x, approximate=True)

def _silu(x):
    return jax.nn.silu(x)

def _sigmoid(x):
    return jax.nn.sigmoid(x)

def _layernorm(x, axis=-1, eps=1e-05):
    m = jnp.mean(x, axis=axis, keepdims=True)
    v = jnp.var(x, axis=axis, keepdims=True)
    return (x - m) / jnp.sqrt(v + eps)

def _scatter_add(tgt, idx, src, axis=0):
    return tgt.at[idx].add(src)

def _segment_sum(src, seg, n):
    return jax.ops.segment_sum(src, seg, n)
kernel_name = 'mk_seq_postln_d1_jaxref_r4_01a5a1'

def setup_inputs(seed: int=0):
    np.random.seed(seed)
    _w = jnp.asarray

    def _L0_attn_setup():
        import jax, jax.numpy as jnp
        import numpy as np
        B, S, D, L = (4, 512, 256, 4)

        def _retention(x, wkqv):
            d = x.shape[-1]
            k, q, v = jnp.split(x @ wkqv, 3, axis=-1)
            qkt = jnp.einsum('bid,bjd->bij', q, k) / jnp.sqrt(jnp.float32(d))
            s = x.shape[1]
            row_norm = 1.0 + jnp.sqrt(jnp.arange(s, dtype=x.dtype))[None, :, None]
            r = jnp.tril(qkt) / row_norm
            denom = jnp.clip(jnp.abs(r.sum(-1, keepdims=True)), 1.0, None)
            r = r / denom
            return jnp.einsum('bij,bjd->bid', r, v)

        def _groupnorm1(y, g, b, eps=1e-05):
            mu = y.mean(axis=(1, 2), keepdims=True)
            var = y.var(axis=(1, 2), keepdims=True)
            return (y - mu) / jnp.sqrt(var + eps) * g + b

        def _layernorm(y, g, b, eps=1e-05):
            mu = y.mean(-1, keepdims=True)
            var = y.var(-1, keepdims=True)
            return (y - mu) / jnp.sqrt(var + eps) * g + b
        key = jax.random.key(seed)
        ks = jax.random.split(key, 6)
        w = lambda k, shape: jax.random.normal(k, shape, jnp.float32) * 0.02
        return {'x': jax.random.normal(ks[0], (B, S, D), jnp.float32), 'Wkqv': w(ks[1], (L, D, 3 * D)), 'Wm1': w(ks[2], (L, D, 2 * D)), 'bm1': jnp.zeros((L, 2 * D), jnp.float32), 'Wm2': w(ks[3], (L, D, D)), 'bm2': jnp.zeros((L, D), jnp.float32), 'gn_g': jnp.ones((L, D), jnp.float32), 'gn_b': jnp.zeros((L, D), jnp.float32), 'Wf1': w(ks[4], (L, D, 2 * D)), 'bf1': jnp.zeros((L, 2 * D), jnp.float32), 'Wf2': w(ks[5], (L, 2 * D, D)), 'bf2': jnp.zeros((L, D), jnp.float32), 'ln_g': jnp.ones((L, D), jnp.float32), 'ln_b': jnp.zeros((L, D), jnp.float32)}
    _L0_attn_in = _L0_attn_setup()

    def _L0_ffn_setup():
        import jax, jax.numpy as jnp
        import numpy as np
        ALPHA = 1.5
        TEMP = 1.0
        N_ITER = 25
        THRESH = 1e-09

        def entmax_bisect(X, alpha=ALPHA, n_iter=N_ITER):
            d = X.shape[-1]
            inv_am1 = 1.0 / (alpha - 1.0)
            Xs = X * (alpha - 1.0)
            max_val = jnp.max(Xs, axis=-1, keepdims=True)
            tau_lo = max_val - 1.0
            tau_hi = max_val - (1.0 / d) ** (alpha - 1.0)
            f_lo = jnp.sum(jnp.maximum(Xs - tau_lo, 0.0) ** inv_am1, axis=-1, keepdims=True) - 1.0

            def body(i, carry):
                tau_lo, dm, _ = carry
                dm = dm * 0.5
                tau_m = tau_lo + dm
                f_m = jnp.sum(jnp.maximum(Xs - tau_m, 0.0) ** inv_am1, axis=-1, keepdims=True) - 1.0
                tau_lo = jnp.where(f_m * f_lo >= 0.0, tau_m, tau_lo)
                return (tau_lo, dm, tau_m)
            dm0 = tau_hi - tau_lo
            _, _, tau_m = jax.lax.fori_loop(0, n_iter, body, (tau_lo, dm0, tau_lo))
            p = jnp.maximum(Xs - tau_m, 0.0) ** inv_am1
            return p / jnp.sum(p, axis=-1, keepdims=True)
        key = jax.random.key(seed)
        ks = jax.random.split(key, 8)
        B, S, D, E = (2, 256, 256, 8)
        F = 4 * D
        return {'x': jax.random.normal(ks[0], (B, S, D), jnp.float32), 'Wr': jax.random.normal(ks[1], (D, E), jnp.float32) * 0.02, 'br': jnp.zeros((E,), jnp.float32), 'W1': jax.random.normal(ks[2], (E, D, F), jnp.float32) * 0.02, 'b1': jnp.zeros((E, F), jnp.float32), 'W2': jax.random.normal(ks[3], (E, F, D), jnp.float32) * 0.02, 'b2': jnp.zeros((E, D), jnp.float32)}
    _L0_ffn_in = _L0_ffn_setup()
    _d = {'L0_attn_x': _L0_attn_in['x'], 'L0_attn_Wkqv': _L0_attn_in['Wkqv'], 'L0_attn_Wm1': _L0_attn_in['Wm1'], 'L0_attn_bm1': _L0_attn_in['bm1'], 'L0_attn_Wm2': _L0_attn_in['Wm2'], 'L0_attn_bm2': _L0_attn_in['bm2'], 'L0_attn_gn_g': _L0_attn_in['gn_g'], 'L0_attn_gn_b': _L0_attn_in['gn_b'], 'L0_attn_Wf1': _L0_attn_in['Wf1'], 'L0_attn_bf1': _L0_attn_in['bf1'], 'L0_attn_Wf2': _L0_attn_in['Wf2'], 'L0_attn_bf2': _L0_attn_in['bf2'], 'L0_attn_ln_g': _L0_attn_in['ln_g'], 'L0_attn_ln_b': _L0_attn_in['ln_b'], 'L0_ffn_Wr': _L0_ffn_in['Wr'], 'L0_ffn_br': _L0_ffn_in['br'], 'L0_ffn_W1': _L0_ffn_in['W1'], 'L0_ffn_b1': _L0_ffn_in['b1'], 'L0_ffn_W2': _L0_ffn_in['W2'], 'L0_ffn_b2': _L0_ffn_in['b2']}
    _x0 = _d['L0_attn_x']
    _d['L0_attn_x'] = jax.random.normal(jax.random.fold_in(jax.random.key(seed), 1), (8, 512, 256), dtype=_x0.dtype)
    del _x0
    return _d

def reference(L0_attn_x, L0_attn_Wkqv, L0_attn_Wm1, L0_attn_bm1, L0_attn_Wm2, L0_attn_bm2, L0_attn_gn_g, L0_attn_gn_b, L0_attn_Wf1, L0_attn_bf1, L0_attn_Wf2, L0_attn_bf2, L0_attn_ln_g, L0_attn_ln_b, L0_ffn_Wr, L0_ffn_br, L0_ffn_W1, L0_ffn_b1, L0_ffn_W2, L0_ffn_b2):

    def _L0_attn_ref(x, Wkqv, Wm1, bm1, Wm2, bm2, gn_g, gn_b, Wf1, bf1, Wf2, bf2, ln_g, ln_b):
        import jax, jax.numpy as jnp
        import numpy as np
        B, S, D, L = (4, 512, 256, 4)

        def _retention(x, wkqv):
            d = x.shape[-1]
            k, q, v = jnp.split(x @ wkqv, 3, axis=-1)
            qkt = jnp.einsum('bid,bjd->bij', q, k) / jnp.sqrt(jnp.float32(d))
            s = x.shape[1]
            row_norm = 1.0 + jnp.sqrt(jnp.arange(s, dtype=x.dtype))[None, :, None]
            r = jnp.tril(qkt) / row_norm
            denom = jnp.clip(jnp.abs(r.sum(-1, keepdims=True)), 1.0, None)
            r = r / denom
            return jnp.einsum('bij,bjd->bid', r, v)

        def _groupnorm1(y, g, b, eps=1e-05):
            mu = y.mean(axis=(1, 2), keepdims=True)
            var = y.var(axis=(1, 2), keepdims=True)
            return (y - mu) / jnp.sqrt(var + eps) * g + b

        def _layernorm(y, g, b, eps=1e-05):
            mu = y.mean(-1, keepdims=True)
            var = y.var(-1, keepdims=True)
            return (y - mu) / jnp.sqrt(var + eps) * g + b

        def block(h, p):
            wk, w1, b1, w2, b2, gg, gb, wf1, bf1_, wf2, bf2_, lg, lb = p
            r = _retention(h, wk)
            m = r @ w1 + b1
            a, gate = jnp.split(m, 2, axis=-1)
            m = a * jax.nn.silu(gate) @ w2 + b2
            m = _groupnorm1(m, gg, gb)
            y = m + h
            f = jax.nn.gelu(y @ wf1 + bf1_, approximate=False) @ wf2 + bf2_
            return (_layernorm(f + y, lg, lb), None)
        params = (Wkqv, Wm1, bm1, Wm2, bm2, gn_g, gn_b, Wf1, bf1, Wf2, bf2, ln_g, ln_b)
        out, _ = jax.lax.scan(block, x, params)
        return out

    def _L0_ffn_ref(x, Wr, br, W1, b1, W2, b2):
        import jax, jax.numpy as jnp
        import numpy as np
        ALPHA = 1.5
        TEMP = 1.0
        N_ITER = 25
        THRESH = 1e-09

        def entmax_bisect(X, alpha=ALPHA, n_iter=N_ITER):
            d = X.shape[-1]
            inv_am1 = 1.0 / (alpha - 1.0)
            Xs = X * (alpha - 1.0)
            max_val = jnp.max(Xs, axis=-1, keepdims=True)
            tau_lo = max_val - 1.0
            tau_hi = max_val - (1.0 / d) ** (alpha - 1.0)
            f_lo = jnp.sum(jnp.maximum(Xs - tau_lo, 0.0) ** inv_am1, axis=-1, keepdims=True) - 1.0

            def body(i, carry):
                tau_lo, dm, _ = carry
                dm = dm * 0.5
                tau_m = tau_lo + dm
                f_m = jnp.sum(jnp.maximum(Xs - tau_m, 0.0) ** inv_am1, axis=-1, keepdims=True) - 1.0
                tau_lo = jnp.where(f_m * f_lo >= 0.0, tau_m, tau_lo)
                return (tau_lo, dm, tau_m)
            dm0 = tau_hi - tau_lo
            _, _, tau_m = jax.lax.fori_loop(0, n_iter, body, (tau_lo, dm0, tau_lo))
            p = jnp.maximum(Xs - tau_m, 0.0) ** inv_am1
            return p / jnp.sum(p, axis=-1, keepdims=True)
        B, S, D = x.shape
        xt = x.reshape(B * S, D)
        logits = (xt @ Wr + br) / TEMP
        gates = entmax_bisect(logits)
        gates = jnp.where(gates > THRESH, gates, 0.0)
        h = jax.nn.relu(jnp.einsum('td,edf->etf', xt, W1) + b1[:, None, :])
        y = jnp.einsum('etf,efd->etd', h, W2) + b2[:, None, :]
        out = jnp.einsum('etd,te->td', y, gates)
        return out.reshape(B, S, D)
    x = L0_attn_x
    x = _layernorm(x + _L0_attn_ref(x, L0_attn_Wkqv, L0_attn_Wm1, L0_attn_bm1, L0_attn_Wm2, L0_attn_bm2, L0_attn_gn_g, L0_attn_gn_b, L0_attn_Wf1, L0_attn_bf1, L0_attn_Wf2, L0_attn_bf2, L0_attn_ln_g, L0_attn_ln_b), axis=-1)
    x = _layernorm(x + _L0_ffn_ref(x, L0_ffn_Wr, L0_ffn_br, L0_ffn_W1, L0_ffn_b1, L0_ffn_W2, L0_ffn_b2), axis=-1)
    return x

_drawn_inputs = setup_inputs


def setup_inputs(seed=0):
    import zlib

    import numpy as np

    out = dict(_drawn_inputs(seed))
    spreads = {'L0_attn_bm1': (0.0, 0.686),
     'L0_attn_bm2': (0.0, 0.1),
     'L0_attn_gn_g': (1.0, 0.2),
     'L0_attn_gn_b': (0.0, 0.1),
     'L0_attn_bf1': (0.0, 0.501),
     'L0_attn_bf2': (0.0, 0.1),
     'L0_attn_ln_g': (1.0, 0.2),
     'L0_attn_ln_b': (0.0, 0.1),
     'L0_ffn_br': (0.0, 0.34),
     'L0_ffn_b1': (0.0, 0.378),
     'L0_ffn_b2': (0.0, 0.1)}
    factors = {'L0_attn_Wkqv': 4.662, 'L0_attn_Wm1': 6.088, 'L0_attn_Wm2': 4.449}
    for name, (base, spread) in spreads.items():
        noise = np.random.default_rng([zlib.crc32(name.encode()), seed]).standard_normal(out[name].shape)
        drawn = base * np.exp(spread * noise) if base else spread * noise
        out[name] = jnp.asarray(drawn.astype(out[name].dtype))
    for name, factor in factors.items():
        out[name] = (out[name] * factor).astype(out[name].dtype)
    return out
```

```python
from contextlib import ExitStack

import concourse.bass as bass
from concourse import mybir

F32 = mybir.dt.float32
F32R = mybir.dt.float32r
ALU = mybir.AluOpType
ACT = mybir.ActivationFunctionType
AX = mybir.AxisListType

P = 128
EPS = 1e-5
NITER = 25
THRESH = 1e-9
DMA = 16


def f32(ap):
    return ap.bitcast(F32)


def hold(eng, held):
    eng.sem_inc(held, 1)


def retention_layers(nc, x, Wkqv, Wm1, bm1, Wm2, bm2, gn_g, gn_b, Wf1, bf1, Wf2, bf2,
                     ln_g, ln_b, score_floor, h_store):
    B, S, D = x.shape
    L = Wkqv.shape[0]
    DC = D // P
    TB = S // P
    MC = Wm1.shape[2] // P
    FC = Wf1.shape[2] // P
    SLOTS = 2
    PAIRS = B // SLOTS
    STEPS = L * PAIRS
    U = 4
    LC = 2 * MC + 4 * DC
    assert (DC, TB, MC, FC, U) == (2, 4, 4, 4, 4)
    LO = [0, P, 2 * P, 2 * P]

    x_v = x.rearrange("(i s) (k p) d -> i s p k d", s=SLOTS, p=P)
    h_v = h_store.rearrange("i s (k p) d -> i s p k d", p=P)

    with ExitStack() as ctx:
        def sb(name, shape, dt=F32):
            return ctx.enter_context(nc.sbuf_tensor(name, shape, dt))

        def sem(name):
            return ctx.enter_context(nc.semaphore(name))

        def sems(name):
            return [sem(f"{name}{s}") for s in range(SLOTS)]

        ident = sb("ident", [P, P])
        ones_r = sb("ones_r", [P, P], F32R)
        mean_w = sb("mean_w", [P, P])
        neg_half = sb("neg_half", [P, TB])
        floor = sb("floor", [P, S])
        const_rows = sb("const_rows", [L * LC, P])
        const_cols = sb("const_cols", [P, L * LC])
        lc = sb("lc", [P, LC])
        lc_bm1, lc_bm2, lc_gg = lc[:, 0:4], lc[:, 4:6], lc[:, 6:8]
        lc_gb, lc_bf1, lc_bf2 = lc[:, 8:10], lc[:, 10:14], lc[:, 14:16]
        raw_kqv = sb("raw_kqv", [P, DC, 3 * D])
        raw_m1 = sb("raw_m1", [P, DC, MC * P])
        raw_m2 = sb("raw_m2", [P, DC * D])
        raw_f1 = sb("raw_f1", [P, DC * FC * P])
        raw_f2 = sb("raw_f2", [P, FC * D])
        raw_ln = sb("raw_ln", [P, 2 * D])
        w_t = sb("w_t", [P, 3, DC * D])
        lnv = sb("lnv", [P, 2 * D])
        wqk = [sb(f"wqk_{n}", [P, DC * D], F32R) for n in ("hi", "lo")]
        wvm = [sb(f"wvm_{n}", [P, DC, MC * P], F32R) for n in ("hi", "lo")]
        wm2 = [sb(f"wm2_{n}", [P, DC * D], F32R) for n in ("hi", "lo")]
        wf1 = [sb(f"wf1_{n}", [P, DC * FC * P], F32R) for n in ("hi", "lo")]
        wf2 = [sb(f"wf2_{n}", [P, FC * D], F32R) for n in ("hi", "lo")]

        def slot_tiles(name, shape, dt=F32):
            return [sb(f"{name}{s}", shape, dt) for s in range(SLOTS)]

        def split_tiles(name, shape):
            return [[sb(f"{name}_{n}{s}", shape, F32R) for n in ("hi", "lo")] for s in range(SLOTS)]

        h_in = slot_tiles("h_in", [P, TB, D])
        h_out = slot_tiles("h_out", [P, TB, D])
        h_sp = split_tiles("h", [P, TB, D])
        hT_sp = split_tiles("hT", [P, DC, S])
        tu_sp = split_tiles("tu", [P, DC, S])
        ry_sp = split_tiles("ry", [P, DC, S])
        pf_sp = split_tiles("pf", [P, FC, S])
        tmp = slot_tiles("tmp", [P, 4, S])
        y = slot_tiles("y", [P, DC, S])
        gstat = slot_tiles("gstat", [P, DC, 6])
        gmv = slot_tiles("gmv", [P, DC, 2])
        gin = slot_tiles("gin", [P, 2 * DC])
        gsm = slot_tiles("gsm", [P, 12])
        zstat = slot_tiles("zstat", [P, TB, 6])
        zmv = slot_tiles("zmv", [P, TB, 2])
        zr = slot_tiles("zr", [P, TB])

        ps = ctx.enter_context(nc.psum_tensor("ps", [P, 8, 512], F32))

        def bank(s, r):
            return ps[:, 4 * s + r, :]

        consts_loaded = sem("consts_loaded")
        ident_zero, ident_ready, pool_consts = sem("ident_zero"), sem("ident_ready"), sem("pool_consts")
        const_psum, const_ready = sem("const_psum"), sem("const_ready")
        raw_loaded = sem("raw_loaded")
        lc_ready = sem("lc_ready")
        wt_psum, wt_ready = sem("wt_psum"), sem("wt_ready")
        fold_psum, fold_hi, fold_lo = sem("fold_psum"), sem("fold_hi"), sem("fold_lo")
        w_hi, w_lo = sem("w_hi"), sem("w_lo")
        h_loaded, h_stored = sems("h_loaded"), sems("h_stored")
        h_hi, h_lo = sems("h_hi"), sems("h_lo")
        hT_psum, hT_hi, hT_lo = sems("hT_psum"), sems("hT_hi"), sems("hT_lo")
        t_psum, t_hi, t_lo = sems("t_psum"), sems("t_hi"), sems("t_lo")
        s_psum, p_hi, p_lo, p_masked = sems("s_psum"), sems("p_hi"), sems("p_lo"), sems("p_masked")
        rowsum_psum, r_psum, r_scaled = sems("rowsum_psum"), sems("r_psum"), sems("r_scaled")
        r_hi, r_lo = sems("r_hi"), sems("r_lo")
        m_psum, gate_ready, u_ready = sems("m_psum"), sems("gate_ready"), sems("u_ready")
        u_hi, u_lo = sems("u_hi"), sems("u_lo")
        m2_psum, gn_in, gn_psum = sems("m2_psum"), sems("gn_in"), sems("gn_psum")
        y_ready, y_hi, y_lo = sems("y_ready"), sems("y_hi"), sems("y_lo")
        f1_psum, f_ready, f_hi, f_lo = sems("f1_psum"), sems("f_ready"), sems("f_hi"), sems("f_lo")
        f2_psum, z_ready = sems("f2_psum"), sems("z_ready")
        zT_psum, zT_read, h_new = sems("zT_psum"), sems("zT_read"), sems("h_new")
        g_var, g_rstd, z_var, z_rstd = sems("g_var"), sems("g_rstd"), sems("z_var"), sems("z_rstd")
        dve_done, dve_held, pool_held = sem("dve_done"), sem("dve_held"), sem("pool_held")

        RAW_DMAS = 7
        block = ctx.enter_context(nc.Block())

        @block.sync
        def _(sp):
            def load_weights(l):
                for dst, src in (
                    (raw_kqv[:, :, :], Wkqv[l].rearrange("(c p) n -> p c n", p=P)),
                    (raw_m1[:, :, :], Wm1[l].rearrange("(c p) n -> p c n", p=P)),
                    (raw_m2[:, :].rearrange("p (c n) -> p c n", c=DC), Wm2[l].rearrange("(c p) n -> p c n", p=P)),
                    (raw_f1[:, :].rearrange("p (c n) -> p c n", c=DC), Wf1[l].rearrange("(c p) n -> p c n", p=P)),
                    (raw_f2[:, :].rearrange("p (c n) -> p c n", c=FC), Wf2[l].rearrange("(c p) n -> p c n", p=P)),
                    (raw_ln[:, 0:D], ln_g[l:l + 1, :].to_broadcast([P, D])),
                    (raw_ln[:, D:2 * D], ln_b[l:l + 1, :].to_broadcast([P, D])),
                ):
                    sp.dma_start(dst, src).then_inc(raw_loaded, DMA)

            def next_weights(l):
                sp.wait_ge(fold_lo, 3 * l)
                sp.wait_ge(w_lo, 3 * l)
                sp.wait_ge(lc_ready, l)
                load_weights(l)

            def load_h(it, src):
                for s in range(SLOTS):
                    sp.wait_ge(hT_psum[s], it * U)
                    sp.wait_ge(h_lo[s], it * U)
                    sp.dma_start(h_in[s][:, :, :], src[s]).then_inc(h_loaded[s], DMA)

            def load_stored(it):
                for s in range(SLOTS):
                    sp.wait_ge(h_stored[s], (it - PAIRS + 2) * DMA)
                load_h(it, [h_v[it, s] for s in range(SLOTS)])

            def store_h(it):
                for s in range(SLOTS):
                    sp.wait_ge(h_new[s], (it + 2) * U)
                    sp.dma_start(h_v[it + PAIRS, s], h_out[s][:, :, :]).then_inc(h_stored[s], DMA)

            for s in range(SLOTS):
                sp.sem_inc(h_stored[s], DMA)
            load_weights(0)
            load_h(0, [x_v[0, s] for s in range(SLOTS)])
            sp.dma_start(floor[:, :], score_floor).then_inc(consts_loaded, DMA)
            next_weights(1)
            with sp.Fori(0, PAIRS - 1) as it:
                load_h(it + 1, [x_v[it + 1, s] for s in range(SLOTS)])
                store_h(it)
            for l in range(1, L):
                with sp.Fori(l * PAIRS - 1, (l + 1) * PAIRS - 1) as i:
                    load_stored(i + 1)
                    store_h(i)
                if l + 1 < L:
                    next_weights(l + 1)
            store_h(STEPS - 1)
            for s in range(SLOTS):
                sp.wait_ge(h_stored[s], (STEPS + 1) * DMA)

        @block.gpsimd
        def _(pool):
            nc.gpsimd.memset(ident[:, :], 0.0).then_inc(ident_zero, 1)
            pool.wait_ge(ident_zero, 1)
            nc.gpsimd.affine_select(out=ident[:, :], in_=ident[:, :], compare_op=ALU.not_equal, fill=1.0,
                                    base=0, pattern=[[-1, P]], channel_multiplier=1).then_inc(ident_ready, 1)
            nc.gpsimd.memset(f32(ones_r[:, :]), 1.0).then_inc(pool_consts, 1)
            nc.gpsimd.memset(neg_half[:, :], -0.5).then_inc(pool_consts, 1)
            nc.gpsimd.memset(mean_w[:, :], 1.0 / (P * DC)).then_inc(pool_consts, 1)

            pool.wait_ge(pool_consts, 3)

            def low_half(lo, full, hi, done, n):
                nc.gpsimd.tensor_tensor(out=lo, in0=full, in1=f32(hi), op=ALU.subtract).then_inc(done, n)

            with pool.Fori(0, L) as l:
                for n, (w, raw) in enumerate(((wm2, raw_m2), (wf1, raw_f1), (wf2, raw_f2))):
                    pool.wait_ge(w_hi, 3 * l + n + 1)
                    low_half(w[1][:, :], raw[:, :], w[0][:, :], w_lo, 1)
                with pool.Fori(0, PAIRS) as p:
                    base = pool.snap((l * PAIRS + p) * U)

                    def split_h(s):
                        pool.wait_ge(h_hi[s], base + U)
                        low_half(h_sp[s][1][:, :, :], h_in[s][:, :, :], h_sp[s][0][:, :, :], h_lo[s], U)

                    def mask_scores(s):
                        for b in range(TB):
                            pool.wait_ge(p_lo[s], base + b + 1)
                            hold(pool, pool_held)
                            for half in range(2):
                                part = pf_sp[s][half][:, b, LO[b]:(b + 1) * P]
                                ins = nc.gpsimd.affine_select(
                                    out=part, in_=f32(part), compare_op=ALU.is_ge, fill=0.0, base=LO[b] - b * P,
                                    pattern=[[1, (b + 1) * P - LO[b]]], channel_multiplier=-1)
                            ins.then_inc(p_masked[s], 1)

                    def split_r(s):
                        for c in range(DC):
                            pool.wait_ge(r_hi[s], base + 2 * c + 2)
                            low_half(ry_sp[s][1][:, c, :], tmp[s][:, c, :], ry_sp[s][0][:, c, :], r_lo[s], 2)

                    def split_u(s):
                        for c in range(DC):
                            pool.wait_ge(u_hi[s], base + 2 * c + 2)
                            low_half(tu_sp[s][1][:, c, :], tmp[s][:, c, :], tu_sp[s][0][:, c, :], u_lo[s], 2)

                    def rstd_group(s):
                        pool.wait_ge(g_var[s], base + U)
                        nc.gpsimd.tensor_tensor(out=gsm[s][:, 5:6], in0=gsm[s][:, 5:6], in1=neg_half[:, 0:1], op=ALU.pow).then_inc(g_rstd[s], U)

                    def rstd_tokens(s):
                        pool.wait_ge(z_var[s], base + U)
                        nc.gpsimd.tensor_tensor(out=zr[s][:, :], in0=zr[s][:, :], in1=neg_half[:, :], op=ALU.pow).then_inc(z_rstd[s], U)

                    def split_y(s):
                        for c in range(DC):
                            pool.wait_ge(y_hi[s], base + 2 * c + 2)
                            low_half(ry_sp[s][1][:, c, :], y[s][:, c, :], ry_sp[s][0][:, c, :], y_lo[s], 2)

                    def split_f(s):
                        for c in range(FC):
                            pool.wait_ge(f_hi[s], base + c + 1)
                            low_half(pf_sp[s][1][:, c, :], tmp[s][:, c, :], pf_sp[s][0][:, c, :], f_lo[s], 1)

                    split_h(0)
                    split_h(1)
                    mask_scores(0)
                    split_r(0)
                    mask_scores(1)
                    split_u(0)
                    split_r(1)
                    rstd_group(0)
                    split_y(0)
                    split_u(1)
                    split_f(0)
                    rstd_group(1)
                    split_y(1)
                    rstd_tokens(0)
                    split_f(1)
                    rstd_tokens(1)

        @block.scalar
        def _(act):
            row = 0
            for l in range(L):
                for c in (bm1, bm2, gn_g, gn_b, bf1, bf2):
                    n = c.shape[1] // P
                    act.dma_start(const_rows[row:row + n, :], c[l].rearrange("(n p) -> n p", p=P)).then_inc(consts_loaded, DMA)
                    row += n
            act.wait_ge(const_psum, 1)
            nc.scalar.activation(const_cols[:, :], bank(0, 0)[:, 0:L * LC], ACT.Copy).then_inc(const_ready, 1)

            with act.Fori(0, L) as l:
                for i, r in enumerate((bank(0, 0), bank(0, 1), bank(1, 0))):
                    act.wait_ge(wt_psum, 3 * l + i + 1)
                    nc.scalar.activation(w_t[:, i, :], r, ACT.Copy).then_inc(wt_ready, 1)
                for n, (w, raw) in enumerate(((wm2, raw_m2), (wf1, raw_f1), (wf2, raw_f2))):
                    nc.scalar.activation(w[0][:, :], raw[:, :], ACT.Copy).then_inc(w_hi, 1)
                for i, (w, r) in enumerate(((wqk[0][:, :], bank(1, 1)), (wvm[0][:, 0, :], bank(0, 0)),
                                            (wvm[0][:, 1, :], bank(0, 1)))):
                    act.wait_ge(fold_psum, 3 * l + i + 1)
                    nc.scalar.activation(w, r, ACT.Copy).then_inc(fold_hi, 1)
                act.wait_ge(lc_ready, l + 1)
                with act.Fori(0, PAIRS) as p:
                    it = act.snap(l * PAIRS + p)
                    base = act.snap(it * U)

                    def high_hT(s):
                        for c in range(DC):
                            act.wait_ge(hT_psum[s], base + 2 * c + 2)
                            nc.scalar.activation(hT_sp[s][0][:, c, :], bank(s, c), ACT.Copy).then_inc(hT_hi[s], 2)

                    def high_h(s):
                        act.wait_ge(h_loaded[s], it * DMA + DMA)
                        nc.scalar.activation(h_sp[s][0][:, :, :], h_in[s][:, :, :], ACT.Copy).then_inc(h_hi[s], U)

                    def high_t(s):
                        for c in range(DC):
                            act.wait_ge(t_psum[s], base + 2 * c + 2)
                            nc.scalar.activation(tu_sp[s][0][:, c, :], bank(s, 2 + c), ACT.Copy).then_inc(t_hi[s], 2)

                    def high_p(s):
                        for b in range(TB):
                            act.wait_ge(s_psum[s], base + b + 1)
                            nc.scalar.activation(pf_sp[s][0][:, b, LO[b]:S], bank(s, b)[:, LO[b]:S], ACT.Copy).then_inc(p_hi[s], 1)

                    def high_r(s):
                        for c in range(DC):
                            act.wait_ge(r_scaled[s], base + 2 * c + 2)
                            nc.scalar.activation(ry_sp[s][0][:, c, :], tmp[s][:, c, :], ACT.Copy).then_inc(r_hi[s], 2)

                    def gates(s):
                        for c in range(DC):
                            act.wait_ge(m_psum[s], base + 2 * c + 1)
                            nc.scalar.activation(tmp[s][:, 2 + c, :], bank(s, 3 if c == 0 else 1), ACT.Silu,
                                                 bias=lc_bm1[:, DC + c:DC + c + 1]).then_inc(gate_ready[s], 2)

                    def high_u(s):
                        for c in range(DC):
                            act.wait_ge(u_ready[s], base + 2 * c + 2)
                            nc.scalar.activation(tu_sp[s][0][:, c, :], tmp[s][:, c, :], ACT.Copy).then_inc(u_hi[s], 2)

                    def high_y(s):
                        for c in range(DC):
                            act.wait_ge(y_ready[s], base + 2 * c + 2)
                            nc.scalar.activation(ry_sp[s][0][:, c, :], y[s][:, c, :], ACT.Copy).then_inc(y_hi[s], 2)

                    def hidden(s):
                        def gelu(c):
                            act.wait_ge(f1_psum[s], base + c + 1)
                            nc.scalar.activation(tmp[s][:, c, :], bank(s, c), ACT.Gelu,
                                                 bias=lc_bf1[:, c:c + 1]).then_inc(f_ready[s], 1)

                        def high_f(c):
                            act.wait_ge(f_ready[s], base + c + 1)
                            nc.scalar.activation(pf_sp[s][0][:, c, :], tmp[s][:, c, :], ACT.Copy).then_inc(f_hi[s], 1)

                        gelu(0)
                        for c in range(1, FC):
                            gelu(c)
                            high_f(c - 1)
                        high_f(FC - 1)

                    high_hT(0)
                    high_hT(1)
                    high_h(0)
                    high_h(1)
                    high_t(0)
                    high_p(0)
                    high_t(1)
                    high_r(0)
                    high_p(1)
                    gates(0)
                    high_u(0)
                    high_r(1)
                    gates(1)
                    high_y(0)
                    high_u(1)
                    hidden(0)
                    high_y(1)
                    hidden(1)

        CHAIN = 28

        @block.vector
        def _(dve):
            def sub_hi(lo, full, hi, done, n):
                nc.vector.tensor_tensor(out=lo, in0=full, in1=f32(hi), op=ALU.subtract).then_inc(done, n)

            for s in range(SLOTS):
                dve.sem_inc(zT_read[s], U)
                dve.sem_inc(h_new[s], U)
            dve.wait_ge(const_ready, 1)
            with dve.Fori(0, L) as l:
                nc.vector.tensor_copy(lc[:, :], const_cols[:, bass.ds(l * LC, LC)])
                dve.wait_ge(raw_loaded, (l + 1) * (RAW_DMAS * DMA))
                for s in range(SLOTS):
                    dve.wait_ge(h_new[s], l * (PAIRS * U) + U)
                nc.vector.tensor_copy(lnv[:, :], raw_ln[:, :]).then_inc(lc_ready, 1)
                dve.wait_ge(lc_ready, l + 1)
                for i, (w, h, r) in enumerate(((wqk[1][:, :], wqk[0][:, :], bank(1, 1)),
                                               (wvm[1][:, 0, :], wvm[0][:, 0, :], bank(0, 0)),
                                               (wvm[1][:, 1, :], wvm[0][:, 1, :], bank(0, 1)))):
                    dve.wait_ge(fold_hi, 3 * l + i + 1)
                    sub_hi(w, r, h, fold_lo, 1)
                with dve.Fori(0, PAIRS) as p:
                    it = dve.snap(l * PAIRS + p)
                    base = dve.snap(it * U)
                    chain_base = dve.snap(it * CHAIN)
                    chained = [0]

                    def landed(ins):
                        chained[0] += 1
                        ins.then_inc(dve_done, 1)
                        dve.wait_ge(dve_done, chain_base + chained[0])

                    def low_hT(s):
                        for c in range(DC):
                            dve.wait_ge(hT_hi[s], base + 2 * c + 2)
                            sub_hi(hT_sp[s][1][:, c, :], bank(s, c), hT_sp[s][0][:, c, :], hT_lo[s], 2)

                    def low_t(s):
                        for c in range(DC):
                            dve.wait_ge(t_hi[s], base + 2 * c + 2)
                            sub_hi(tu_sp[s][1][:, c, :], bank(s, 2 + c), tu_sp[s][0][:, c, :], t_lo[s], 2)

                    def low_p(s):
                        for b in range(TB):
                            dve.wait_ge(p_hi[s], base + b + 1)
                            sub_hi(pf_sp[s][1][:, b, LO[b]:S], bank(s, b)[:, LO[b]:S], pf_sp[s][0][:, b, LO[b]:S],
                                   p_lo[s], 1)

                    def scale_r(s):
                        dve.wait_ge(rowsum_psum[s], base + U)
                        landed(nc.vector.tensor_tensor(out=tmp[s][:, 3, :], in0=bank(s, 0), in1=floor[:, :], op=ALU.max))
                        landed(nc.vector.scalar_tensor_tensor(out=tmp[s][:, 2, :], in0=bank(s, 0), scalar=-1.0,
                                                              in1=tmp[s][:, 3, :], op0=ALU.mult, op1=ALU.max))
                        landed(nc.vector.reciprocal(tmp[s][:, 3, :], tmp[s][:, 2, :]))
                        for c in range(DC):
                            dve.wait_ge(r_psum[s], base + 2 * c + 2)
                            nc.vector.tensor_tensor(out=tmp[s][:, c, :], in0=bank(s, 1 + c), in1=tmp[s][:, 3, :],
                                                    op=ALU.mult).then_inc(r_scaled[s], 2)

                    def gated(s):
                        for c in range(DC):
                            dve.wait_ge(m_psum[s], base + 2 * c + 2)
                            dve.wait_ge(gate_ready[s], base + 2 * c + 2)
                            nc.vector.scalar_tensor_tensor(
                                out=tmp[s][:, c, :], in0=bank(s, 0 if c == 0 else 2), scalar=lc_bm1[:, c:c + 1],
                                in1=tmp[s][:, 2 + c, :], op0=ALU.add, op1=ALU.mult).then_inc(u_ready[s], 2)

                    def groupnorm(s):
                        m2 = [bank(s, 3), bank(s, 0)]
                        sq, mom, var, rstd = gsm[s][:, 0:2], gsm[s][:, 2:4], gsm[s][:, 4:5], gsm[s][:, 5:6]
                        gain, off0, off = gsm[s][:, 6:8], gsm[s][:, 8:10], gsm[s][:, 10:12]
                        for c in range(DC):
                            dve.wait_ge(m2_psum[s], base + 2 * c + 2)
                            ins = nc.vector.bn_stats(gstat[s][:, c, :], m2[c])
                        landed(ins)
                        hold(dve, dve_held)
                        for c in range(DC):
                            ins = nc.vector.bn_aggr(gmv[s][:, c, :], gstat[s][:, c, :])
                        landed(ins)
                        landed(nc.vector.tensor_tensor(out=gin[s][:, 0:2], in0=gmv[s][:, :, 0], in1=lc_bm2, op=ALU.add))
                        landed(nc.vector.tensor_tensor(out=sq, in0=gin[s][:, 0:2], in1=gin[s][:, 0:2], op=ALU.mult))
                        nc.vector.tensor_tensor(out=gin[s][:, 2:4], in0=sq, in1=gmv[s][:, :, 1], op=ALU.add).then_inc(gn_in[s], U)
                        dve.wait_ge(gn_psum[s], base + U)
                        landed(nc.vector.tensor_reduce(out=mom, in_=bank(s, 1)[:, 0:4].rearrange("p (q c) -> p q c", c=DC),
                                                       op=ALU.add, axis=AX.X))
                        landed(nc.vector.scalar_tensor_tensor(out=var, in0=mom[:, 0:1], scalar=mom[:, 0:1], in1=mom[:, 1:2],
                                                              op0=ALU.mult, op1=ALU.subtract, reverse1=True))
                        nc.vector.tensor_scalar(rstd, var, EPS, None, ALU.add).then_inc(g_var[s], U)
                        dve.wait_ge(g_rstd[s], base + U)
                        landed(nc.vector.tensor_scalar(gain, lc_gg, rstd, None, ALU.mult))
                        landed(nc.vector.scalar_tensor_tensor(out=off0, in0=lc_bm2, scalar=mom[:, 0:1], in1=gain,
                                                              op0=ALU.subtract, op1=ALU.mult))
                        nc.vector.tensor_tensor(out=off, in0=off0, in1=lc_gb, op=ALU.add)
                        for c in range(DC):
                            ins = nc.vector.scalar_tensor_tensor(
                                out=tmp[s][:, c, :], in0=m2[c], scalar=gain[:, c:c + 1], in1=f32(hT_sp[s][0][:, c, :]),
                                op0=ALU.mult, op1=ALU.add)
                        landed(ins)
                        for c in range(DC):
                            nc.vector.scalar_tensor_tensor(
                                out=y[s][:, c, :], in0=tmp[s][:, c, :], scalar=off[:, c:c + 1], in1=f32(hT_sp[s][1][:, c, :]),
                                op0=ALU.add, op1=ALU.add).then_inc(y_ready[s], 2)

                    def residual(s):
                        for c in range(DC):
                            dve.wait_ge(f2_psum[s], base + 2 * c + 2)
                            nc.vector.scalar_tensor_tensor(
                                out=y[s][:, c, :], in0=bank(s, c), scalar=lc_bf2[:, c:c + 1], in1=y[s][:, c, :],
                                op0=ALU.add, op1=ALU.add).then_inc(z_ready[s], 2)

                    def layernorm(s):
                        def z(k):
                            return bank(s, 2 + k // 2)[:, (k % 2) * D:(k % 2 + 1) * D]

                        def part(k):
                            return tmp[s][:, k // 2, (k % 2) * D:(k % 2 + 1) * D]

                        for k in range(TB):
                            dve.wait_ge(zT_psum[s], base + 2 * (k // 2) + 2)
                            ins = nc.vector.bn_stats(zstat[s][:, k, :], z(k))
                        landed(ins)
                        hold(dve, dve_held)
                        for k in range(TB):
                            ins = nc.vector.bn_aggr(zmv[s][:, k, :], zstat[s][:, k, :])
                        landed(ins)
                        nc.vector.tensor_scalar(zr[s][:, :], zmv[s][:, :, 1], EPS, None, ALU.add).then_inc(z_var[s], U)
                        for k in range(TB):
                            ins = nc.vector.scalar_tensor_tensor(out=part(k), in0=z(k), scalar=zmv[s][:, k, 0:1],
                                                                 in1=lnv[:, 0:D], op0=ALU.subtract, op1=ALU.mult)
                        ins.then_inc(zT_read[s], U)
                        dve.wait_ge(zT_read[s], base + 2 * U)
                        dve.wait_ge(h_stored[s], it * DMA + DMA)
                        dve.wait_ge(z_rstd[s], base + U)
                        for k in range(TB):
                            ins = nc.vector.scalar_tensor_tensor(out=h_out[s][:, k, :], in0=part(k), scalar=zr[s][:, k:k + 1],
                                                                 in1=lnv[:, D:2 * D], op0=ALU.mult, op1=ALU.add)
                        ins.then_inc(h_new[s], U)

                    low_hT(0)
                    low_hT(1)
                    low_t(0)
                    low_p(0)
                    low_t(1)
                    scale_r(0)
                    low_p(1)
                    gated(0)
                    scale_r(1)
                    groupnorm(0)
                    gated(1)
                    groupnorm(1)
                    residual(0)
                    layernorm(0)
                    residual(1)
                    layernorm(1)
                    assert chained[0] == CHAIN, chained

        @block.tensor
        def _(pe):
            def mm3(out, w, x, first, last):
                nc.tensor.matmul(out, w[0], x[0], start=first, stop=False, skip_group_check=True)
                nc.tensor.matmul(out, w[0], x[1], start=False, stop=False, skip_group_check=True)
                return nc.tensor.matmul(out, w[1], x[0], start=False, stop=last, skip_group_check=True)

            def both(pair, *index):
                return [t[index] for t in pair]

            ALL = slice(None)

            def cols(n):
                return slice(n * P, (n + 1) * P)

            pe.wait_ge(ident_ready, 1)
            pe.wait_ge(pool_consts, 3)
            pe.wait_ge(consts_loaded, (6 * L + 1) * DMA)
            nc.tensor.transpose(bank(0, 0)[:, 0:L * LC], const_rows[:, :], ident[0:L * LC, 0:L * LC]).then_inc(const_psum, 1)
            pe.wait_ge(const_ready, 1)

            with pe.Fori(0, L) as l:
                pe.wait_ge(raw_loaded, (l + 1) * (RAW_DMAS * DMA))
                for i, r in enumerate((bank(0, 0), bank(0, 1), bank(1, 0))):
                    for cc in range(DC):
                        for dh in range(DC):
                            ins = nc.tensor.transpose(r[:, cc * D + dh * P:cc * D + (dh + 1) * P],
                                                      raw_kqv[:, dh, i * D + cc * P:i * D + (cc + 1) * P], ident[:, :])
                    ins.then_inc(wt_psum, 1)
                wt = w_t[:, :, :].rearrange("p i (c d) -> p i c d", c=DC)
                pe.wait_ge(wt_ready, 3 * l + 2)
                for dh in range(DC):
                    for cc in range(DC):
                        ins = nc.tensor.matmul(bank(1, 1)[:, dh * D:(dh + 1) * D], wt[:, 1, cc, cols(dh)], wt[:, 0, cc, :],
                                               start=cc == 0, stop=cc == DC - 1)
                ins.then_inc(fold_psum, 1)
                pe.wait_ge(wt_ready, 3 * l + 3)
                for dh in range(DC):
                    for cc in range(DC):
                        ins = nc.tensor.matmul(bank(0, dh), wt[:, 2, cc, cols(dh)], raw_m1[:, cc, :],
                                               start=cc == 0, stop=cc == DC - 1)
                    ins.then_inc(fold_psum, 1)
                with pe.Fori(0, PAIRS) as p:
                    it = pe.snap(l * PAIRS + p)
                    base = pe.snap(it * U)

                    def transpose_h(s):
                        pe.wait_ge(h_loaded[s], it * DMA + DMA)
                        pe.wait_ge(fold_lo, 3 * l + 3)
                        for c in range(DC):
                            for k in range(TB):
                                ins = nc.tensor.transpose(bank(s, c)[:, cols(k)], h_in[s][:, k, cols(c)], ident[:, :])
                            ins.then_inc(hT_psum[s], 2)

                    def project_t(s):
                        pe.wait_ge(fold_lo, 3 * l + 3)
                        pe.wait_ge(w_lo, 3 * l + 3)
                        pe.wait_ge(zT_read[s], base + U)
                        w = [t[:, :].rearrange("p (c n) -> p c n", c=DC) for t in wqk]
                        for c in range(DC):
                            for k in range(DC):
                                pe.wait_ge(hT_lo[s], base + 2 * k + 2)
                                ins = mm3(bank(s, 2 + c), both(w, ALL, k, cols(c)), both(hT_sp[s], ALL, k), k == 0, k == DC - 1)
                            ins.then_inc(t_psum[s], 2)

                    def scores(s):
                        for b in range(TB):
                            q = slice(LO[b], S)
                            for k in range(DC):
                                pe.wait_ge(t_lo[s], base + 2 * k + 2)
                                ins = mm3(bank(s, b)[:, q], both(hT_sp[s], ALL, k, cols(b)), both(tu_sp[s], ALL, k, q),
                                          k == 0, k == DC - 1)
                            ins.then_inc(s_psum[s], 1)

                    def retain(s):
                        pe.wait_ge(h_lo[s], base + U)
                        for b in range(TB):
                            q = slice(LO[b], S)
                            pe.wait_ge(p_masked[s], base + b + 1)
                            for half in range(2):
                                ins = nc.tensor.matmul(bank(s, 0)[:, q], ones_r[:, :], pf_sp[s][half][:, b, q],
                                                       start=b == 0 and half == 0, stop=b == TB - 1 and half == 1,
                                                       skip_group_check=True)
                        ins.then_inc(rowsum_psum[s], U)
                        for c in range(DC):
                            for b in range(TB):
                                q = slice(LO[b], S)
                                ins = mm3(bank(s, 1 + c)[:, q], both(h_sp[s], ALL, b, cols(c)), both(pf_sp[s], ALL, b, q),
                                          b == 0, b == TB - 1)
                            ins.then_inc(r_psum[s], 2)

                    def gated_projection(s):
                        for r, n in ((3, DC), (0, 0), (1, DC + 1), (2, 1)):
                            for k in range(DC):
                                pe.wait_ge(r_lo[s], base + 2 * k + 2)
                                ins = mm3(bank(s, r), both(wvm, ALL, k, cols(n)), both(ry_sp[s], ALL, k), k == 0, k == DC - 1)
                            ins.then_inc(m_psum[s], 1)

                    def out_projection(s):
                        w = [t[:, :].rearrange("p (c n) -> p c n", c=DC) for t in wm2]
                        for c, r in ((0, 3), (1, 0)):
                            for k in range(DC):
                                pe.wait_ge(u_lo[s], base + 2 * k + 2)
                                ins = mm3(bank(s, r), both(w, ALL, k, cols(c)), both(tu_sp[s], ALL, k), k == 0, k == DC - 1)
                            ins.then_inc(m2_psum[s], 2)

                    def group_moments(s):
                        pe.wait_ge(gn_in[s], base + U)
                        nc.tensor.matmul(bank(s, 1)[:, 0:2 * DC], mean_w[:, :], gin[s][:, :], start=True,
                                         stop=True).then_inc(gn_psum[s], U)

                    def up_projection(s):
                        w = [t[:, :].rearrange("p (c n) -> p c n", c=DC) for t in wf1]
                        for n in range(FC):
                            for k in range(DC):
                                pe.wait_ge(y_lo[s], base + 2 * k + 2)
                                ins = mm3(bank(s, n), both(w, ALL, k, cols(n)), both(ry_sp[s], ALL, k), k == 0, k == DC - 1)
                            ins.then_inc(f1_psum[s], 1)

                    def down_projection(s):
                        w = [t[:, :].rearrange("p (c n) -> p c n", c=FC) for t in wf2]
                        for c in range(DC):
                            for k in range(FC):
                                pe.wait_ge(f_lo[s], base + k + 1)
                                ins = mm3(bank(s, c), both(w, ALL, k, cols(c)), both(pf_sp[s], ALL, k), k == 0, k == FC - 1)
                            ins.then_inc(f2_psum[s], 2)

                    def transpose_z(s):
                        pe.wait_ge(z_ready[s], base + U)
                        for k in range(TB):
                            for c in range(DC):
                                at = (k % 2) * D + c * P
                                ins = nc.tensor.transpose(bank(s, 2 + k // 2)[:, at:at + P], y[s][:, c, cols(k)], ident[:, :])
                            if k % 2:
                                ins.then_inc(zT_psum[s], 2)

                    transpose_h(0)
                    transpose_h(1)
                    project_t(0)
                    scores(0)
                    project_t(1)
                    retain(0)
                    scores(1)
                    gated_projection(0)
                    retain(1)
                    out_projection(0)
                    gated_projection(1)
                    group_moments(0)
                    up_projection(0)
                    out_projection(1)
                    down_projection(0)
                    group_moments(1)
                    up_projection(1)
                    transpose_z(0)
                    down_projection(1)
                    transpose_z(1)


def expert_mixture(nc, x, h_last, Wr, br, W1, b1, W2, b2, out):
    E, D, F = W1.shape
    B, S, _ = x.shape
    DC, FC, TB = D // P, F // P, S // P
    NB = B * TB
    CH = FC * B
    RING = 4
    AHEAD = 2

    x_v = x.rearrange("t (k p) d -> t p k d", p=P)
    h_v = h_last.rearrange("i s (k p) d -> (i s) p k d", p=P)
    out_v = out.rearrange("t (k p) d -> t p k d", p=P)
    w1_v = W1.rearrange("e (c p) f -> e p c f", p=P)
    w2_v = W2.rearrange("e (c p) d -> e p c d", p=P)

    with ExitStack() as ctx:
        def sb(name, shape, dt=F32):
            return ctx.enter_context(nc.sbuf_tensor(name, shape, dt))

        def sem(name):
            return ctx.enter_context(nc.semaphore(name))

        ident = sb("m_ident", [P, P])
        b1_rows = sb("b1_rows", [E * FC, P])
        b1_cols = sb("b1_cols", [P, E * FC])
        b2_rows = sb("b2_rows", [E, D])
        wr = sb("wr", [P, DC, E])
        br_bc = sb("br_bc", [P, E])
        x1T = [sb(f"x1T_{n}", [P, DC, B * S], F32R) for n in ("hi", "lo")]
        acc = sb("acc", [P, NB, D])
        raw1 = sb("raw1", [P, DC * F])
        raw2 = sb("raw2", [P, FC * D])
        w1 = [[sb(f"w1_{n}{e}", [P, DC * F], F32R) for n in ("hi", "lo")] for e in range(2)]
        w2 = [[sb(f"w2_{n}{e}", [P, FC * D], F32R) for n in ("hi", "lo")] for e in range(2)]
        hid = [sb(f"hid_{n}", [P, RING, S], F32R) for n in ("hi", "lo")]
        act32 = sb("act32", [P, RING, S])
        h_in = act32[:, 0:2, :].rearrange("p c (k d) -> p (c k) d", d=D)
        x1 = act32[:, 2:4, :].rearrange("p c (k d) -> p (c k) d", d=D)
        x1Tf = sb("x1Tf", [P, DC, S])
        stat = sb("m_stat", [P, TB, 6])
        mv = sb("m_mv", [P, TB, 2])
        rstd = sb("rstd", [P, TB])
        neg_half = sb("m_neg_half", [P, TB])
        gates = sb("gates", [P, NB, E])
        ent_w = x1Tf[:, 0, 0:NB * E].rearrange("p (n e) -> p n e", e=E)
        ent_s = x1Tf[:, 0, NB * E:NB * (E + 8)].rearrange("p (i n) -> p i n", n=NB)
        gate_t = x1Tf[:, 1, 0:TB * E].rearrange("p (k e) -> p k e", e=E)
        gateT = act32[0:E, 2, :]

        ps = ctx.enter_context(nc.psum_tensor("m_ps", [P, 8, 512], F32))

        def hid_bank(n):
            return ps[:, n % RING, :]

        def out_bank(parity, k):
            return ps[:, RING + 2 * parity + k // 2, (k % 2) * D:(k % 2 + 1) * D]

        xT_bank, logit_bank, gateT_bank, b2_bank = (lambda c: ps[:, c, :]), ps[:, 2, :], ps[:, 3, :], (lambda c: ps[:, 4 + c, :])

        consts_loaded, ident_zero, ident_ready = sem("m_consts"), sem("m_ident_zero"), sem("m_ident_ready")
        b1_psum, b1_ready = sem("b1_psum"), sem("b1_ready")
        x_loaded, h_loaded, x1_ready, x1_kept = sem("x_loaded"), sem("m_h_loaded"), sem("x1_ready"), sem("x1_kept")
        xT_psum, xT_full, xT_split, logits = sem("xT_psum"), sem("xT_full"), sem("xT_split"), sem("logits")
        gate_copied, gateT_psum, gateT_ready = sem("gate_copied"), sem("gateT_psum"), sem("gateT_ready")
        b2_psum, b2_added = sem("b2_psum"), sem("b2_added")
        raw_loaded = sem("m_raw_loaded")
        w1_split, w2_split = sem("w1_split"), sem("w2_split")
        pool_hi = sem("pool_hi")
        hid_psum, hid_relu, hid_split, hid_used = sem("hid_psum"), sem("hid_relu"), sem("hid_split"), sem("hid_used")
        hid_high = sem("hid_high")
        out_added = sem("out_added")
        y_ready, y_stored = sem("out_ready"), sem("out_stored")
        m_var, m_rstd = sem("m_var"), sem("m_rstd")
        dve_done, dve_held, pool_held = sem("m_dve_done"), sem("m_dve_held"), sem("m_pool_held")

        block = ctx.enter_context(nc.Block())

        @block.sync
        def _(sp):
            for dst, src in ((b1_rows[:, :], b1.rearrange("e (n p) -> (e n) p", p=P)), (b2_rows[:, :], b2),
                             (wr[:, :, :], Wr.rearrange("(c p) e -> p c e", p=P)),
                             (br_bc[:, :], br.rearrange("(a e) -> a e", a=1).to_broadcast([P, E]))):
                sp.dma_start(dst, src).then_inc(consts_loaded, DMA)

            def load_expert(e):
                sp.dma_start(raw1[:, :].rearrange("p (c f) -> p c f", c=DC), w1_v[e]).then_inc(raw_loaded, DMA)
                sp.dma_start(raw2[:, :].rearrange("p (c d) -> p c d", c=FC), w2_v[e]).then_inc(raw_loaded, DMA)

            with sp.Fori(0, B) as t:
                sp.dma_start(acc[:, bass.ds(t * TB, TB), :], x_v[t]).then_inc(x_loaded, DMA)
                sp.wait_ge(x1_ready, t + 1)
                sp.dma_start(h_in, h_v[t]).then_inc(h_loaded, DMA)
            load_expert(0)
            with sp.Fori(1, E) as e:
                sp.wait_ge(w1_split, e)
                sp.wait_ge(w2_split, e)
                load_expert(e)
            with sp.Fori(0, B) as t:
                sp.wait_ge(y_ready, t + 1)
                sp.dma_start(out_v[t], acc[:, bass.ds(t * TB, TB), :]).then_inc(y_stored, DMA)
            sp.wait_ge(y_stored, B * DMA)

        @block.gpsimd
        def _(pool):
            nc.gpsimd.memset(ident[:, :], 0.0).then_inc(ident_zero, 1)
            pool.wait_ge(ident_zero, 1)
            nc.gpsimd.affine_select(out=ident[:, :], in_=ident[:, :], compare_op=ALU.not_equal, fill=1.0,
                                    base=0, pattern=[[-1, P]], channel_multiplier=1).then_inc(ident_ready, 1)

            nc.gpsimd.memset(neg_half[:, :], -0.5).then_inc(ident_zero, 1)
            pool.wait_ge(ident_zero, 2)

            def split_expert(e, parity):
                pool.wait_ge(raw_loaded, (e + 1) * (2 * DMA))
                hold(pool, pool_held)
                nc.gpsimd.tensor_copy(w1[parity][0][:, :], raw1[:, :]).then_inc(pool_hi, 1)
                nc.gpsimd.tensor_copy(w2[parity][0][:, :], raw2[:, :]).then_inc(pool_hi, 1)
                pool.wait_ge(pool_hi, 2 * e + 2)
                nc.gpsimd.tensor_tensor(out=w1[parity][1][:, :], in0=raw1[:, :], in1=f32(w1[parity][0][:, :]),
                                        op=ALU.subtract).then_inc(w1_split, 1)
                nc.gpsimd.tensor_tensor(out=w2[parity][1][:, :], in0=raw2[:, :], in1=f32(w2[parity][0][:, :]),
                                        op=ALU.subtract).then_inc(w2_split, 1)

            def rstd_tokens(t):
                pool.wait_ge(m_var, t + 1)
                nc.gpsimd.tensor_tensor(out=rstd[:, :], in0=rstd[:, :], in1=neg_half[:, :], op=ALU.pow).then_inc(m_rstd, 1)

            with pool.Fori(0, B) as t:
                rstd_tokens(t)
            split_expert(0, 0)
            split_expert(1, 1)
            with pool.Fori(1, E // 2) as pair:
                for parity in range(2):
                    pool.wait_ge(hid_used, (pair * 2 + parity - 1) * CH + RING)
                    split_expert(pair * 2 + parity, parity)
            with pool.Fori(B, 2 * B) as t:
                rstd_tokens(t)

        @block.scalar
        def _(act):
            act.sem_inc(hid_relu, RING)
            act.sem_inc(x1_kept, 1)
            act.sem_inc(xT_full, DC)
            act.sem_inc(gateT_ready, 1)
            act.wait_ge(b1_psum, 1)
            nc.scalar.activation(b1_cols[:, :], xT_bank(0)[:, 0:E * FC], ACT.Copy).then_inc(b1_ready, 1)
            with act.Fori(0, B) as t:
                act.wait_ge(x1_ready, t + 2)
                nc.scalar.activation(acc[:, bass.ds(t * TB, TB), :], x1, ACT.Copy).then_inc(x1_kept, 1)
                act.wait_ge(logits, t + 1)
                act.wait_ge(xT_split, 2 * t + 2)
                for c in range(DC):
                    act.wait_ge(xT_psum, 2 * t + c + 3)
                    nc.scalar.activation(x1Tf[:, c, :], xT_bank(c), ACT.Copy).then_inc(xT_full, 1)
            with act.Fori(0, B) as t:
                act.wait_ge(gateT_psum, t + 2)
                nc.scalar.activation(gateT[:, :], gateT_bank[0:E, :], ACT.Copy).then_inc(gateT_ready, 1)
            with act.Fori(0, E) as e:
                with act.Fori(0, B) as t:
                    chunk = act.snap(e * CH + t * FC)
                    for j in range(FC):
                        act.wait_ge(hid_psum, chunk + j + 1)
                        act.wait_ge(hid_split, chunk + j + 1)
                        nc.scalar.activation(act32[:, j % RING, :], hid_bank(j), ACT.Relu,
                                             bias=b1_cols[:, bass.ds(e * FC + j, 1)]).then_inc(hid_relu, 1)

        @block.vector
        def _(dve):
            dve.sem_inc(hid_split, RING)
            dve.sem_inc(x1_ready, 1)
            dve.sem_inc(xT_split, DC)
            dve.sem_inc(b2_added, 1)
            dve.sem_inc(out_added, 1)
            count = [0]

            def landed(ins, base=0):
                count[0] += 1
                ins.then_inc(dve_done, 1)
                dve.wait_ge(dve_done, base + count[0])

            TILE_CHAIN = 4
            with dve.Fori(0, B) as t:
                base = dve.snap(t * TILE_CHAIN)
                count[0] = 0
                at = bass.ds(t * TB, TB)
                dve.wait_ge(x_loaded, (t + 1) * DMA)
                dve.wait_ge(h_loaded, (t + 1) * DMA)
                landed(nc.vector.tensor_tensor(out=h_in, in0=acc[:, at, :], in1=h_in, op=ALU.add), base)
                for k in range(TB):
                    ins = nc.vector.bn_stats(stat[:, k, :], h_in[:, k, :])
                landed(ins, base)
                hold(dve, dve_held)
                for k in range(TB):
                    ins = nc.vector.bn_aggr(mv[:, k, :], stat[:, k, :])
                landed(ins, base)
                nc.vector.tensor_scalar(rstd[:, :], mv[:, :, 1], EPS, None, ALU.add).then_inc(m_var, 1)
                dve.wait_ge(m_rstd, t + 1)
                dve.wait_ge(x1_kept, t + 1)
                dve.wait_ge(xT_psum, 2 * t + 2)
                for k in range(TB):
                    ins = nc.vector.tensor_scalar(x1[:, k, :], h_in[:, k, :], mv[:, k, 0:1],
                                                  rstd[:, k:k + 1], ALU.subtract, ALU.mult)
                ins.then_inc(x1_ready, 1)
                dve.wait_ge(xT_full, 2 * t + 4)
                hi, lo = (h[:, :, bass.ds(t * S, S)] for h in x1T)
                landed(nc.vector.tensor_copy(hi, x1Tf[:, :, :]), base)
                nc.vector.tensor_tensor(out=lo, in0=x1Tf[:, :, :], in1=f32(hi), op=ALU.subtract).then_inc(xT_split, 2)
                assert count[0] == TILE_CHAIN

            def each(v):
                return v.unsqueeze(2).to_broadcast([P, NB, E])

            fixed = B * TILE_CHAIN
            count[0] = 0
            mx, lo, mid, span, f_lo, f_mid, step, tot = (ent_s[:, i, :] for i in range(8))
            scores, work = gates[:, :, :], ent_w[:, :, :]

            def rowsum_of_squares(total, tau):
                landed(nc.vector.tensor_tensor(out=work, in0=scores, in1=each(tau), op=ALU.subtract), fixed)
                landed(nc.vector.scalar_tensor_tensor(out=work, in0=work, scalar=0.0, in1=work, op0=ALU.max, op1=ALU.mult), fixed)
                landed(nc.vector.tensor_reduce(out=total, in_=work, op=ALU.add, axis=AX.X), fixed)

            dve.wait_ge(logits, B + 1)
            landed(nc.vector.tensor_tensor(out=scores, in0=logit_bank[:, 0:NB * E].rearrange("p (n e) -> p n e", e=E),
                                           in1=br_bc[:, :].unsqueeze(1).to_broadcast([P, NB, E]), op=ALU.add), fixed)
            landed(nc.vector.tensor_scalar(scores, scores, 0.5, None, ALU.mult), fixed)
            landed(nc.vector.tensor_reduce(out=mx, in_=scores, op=ALU.max, axis=AX.X), fixed)
            nc.vector.tensor_scalar(lo, mx, -1.0, None, ALU.add)
            landed(nc.vector.tensor_scalar(mid, mx, -float(E) ** -0.5, None, ALU.add), fixed)
            landed(nc.vector.tensor_tensor(out=span, in0=mid, in1=lo, op=ALU.subtract), fixed)
            rowsum_of_squares(f_lo, lo)
            landed(nc.vector.tensor_scalar(f_lo, f_lo, -1.0, None, ALU.add), fixed)
            for n in range(1, NITER + 1):
                landed(nc.vector.scalar_tensor_tensor(out=mid, in0=span, scalar=0.5 ** n, in1=lo, op0=ALU.mult, op1=ALU.add), fixed)
                rowsum_of_squares(f_mid, mid)
                if n < NITER:
                    landed(nc.vector.scalar_tensor_tensor(out=f_mid, in0=f_mid, scalar=-1.0, in1=f_lo, op0=ALU.add, op1=ALU.mult), fixed)
                    landed(nc.vector.scalar_tensor_tensor(out=step, in0=f_mid, scalar=0.0, in1=span, op0=ALU.is_ge, op1=ALU.mult), fixed)
                    landed(nc.vector.scalar_tensor_tensor(out=lo, in0=step, scalar=0.5 ** n, in1=lo, op0=ALU.mult, op1=ALU.add), fixed)
            landed(nc.vector.reciprocal(tot, f_mid), fixed)
            landed(nc.vector.tensor_tensor(out=work, in0=work, in1=each(tot), op=ALU.mult), fixed)
            landed(nc.vector.scalar_tensor_tensor(out=scores, in0=work, scalar=THRESH, in1=work, op0=ALU.is_gt, op1=ALU.mult), fixed)

            with dve.Fori(0, B) as t:
                dve.wait_ge(gateT_psum, t + 1)
                nc.vector.tensor_copy(gate_t[:, :, :], gates[:, bass.ds(t * TB, TB), :]).then_inc(gate_copied, 1)
                dve.wait_ge(b2_psum, t + 1)
                dve.wait_ge(x1_kept, B + 1)
                at = acc[:, bass.ds(t * TB, TB), :].rearrange("p (c k) d -> p c (k d)", c=2)
                nc.vector.tensor_tensor(out=at, in0=at, in1=ps[:, 4:6, :], op=ALU.add).then_inc(b2_added, 1)


            def split_chunk(chunk, j):
                dve.wait_ge(hid_relu, chunk + j + 1 + RING)
                dve.wait_ge(hid_used, chunk + j + 1)
                r = j % RING
                nc.vector.tensor_copy(hid[0][:, r, :], act32[:, r, :]).then_inc(hid_high, 1)
                dve.wait_ge(hid_high, chunk + j + 1)
                nc.vector.tensor_tensor(out=hid[1][:, r, :], in0=act32[:, r, :], in1=f32(hid[0][:, r, :]),
                                        op=ALU.subtract).then_inc(hid_split, 1)

            def add_tile(e, t, tiles, parity):
                dve.wait_ge(hid_used, (tiles + 1) * FC + RING)
                for k in range(TB):
                    at = acc[:, bass.ds(t * TB + k, 1), :].rearrange("p o d -> p (o d)")
                    gate = gates[:, bass.ds(t * TB + k, 1), bass.ds(e, 1)].rearrange("p o d -> p (o d)")
                    ins = nc.vector.scalar_tensor_tensor(out=at, in0=out_bank(parity, k), scalar=gate,
                                                         in1=at, op0=ALU.mult, op1=ALU.add)
                ins.then_inc(out_added, 1)

            with dve.Fori(0, E) as e:
                first = dve.snap(e * B)

                def next_tile(t, parity):
                    chunk = dve.snap((first + t) * FC)
                    for j in range(FC):
                        split_chunk(chunk, j)
                        if j == AHEAD - 1:
                            add_tile(e, t - 1, dve.snap(first + t - 1), 1 - parity)

                for j in range(FC):
                    split_chunk(dve.snap(first * FC), j)
                with dve.Fori(0, B // 2 - 1) as pair:
                    next_tile(dve.snap(pair * 2 + 1), 1)
                    next_tile(dve.snap(pair * 2 + 2), 0)
                next_tile(B - 1, 1)
                add_tile(e, B - 1, dve.snap(first + B - 1), 1)

            fixed += count[0]
            with dve.Fori(0, B) as t:
                base = dve.snap(t * 2 + fixed)
                count[0] = 0
                dve.wait_ge(out_added, E * B + 1)
                for k in range(TB):
                    ins = nc.vector.bn_stats(stat[:, k, :], acc[:, bass.ds(t * TB + k, 1), :])
                landed(ins, base)
                hold(dve, dve_held)
                for k in range(TB):
                    ins = nc.vector.bn_aggr(mv[:, k, :], stat[:, k, :])
                landed(ins, base)
                nc.vector.tensor_scalar(rstd[:, :], mv[:, :, 1], EPS, None, ALU.add).then_inc(m_var, 1)
                dve.wait_ge(m_rstd, t + B + 1)
                for k in range(TB):
                    at = acc[:, bass.ds(t * TB + k, 1), :]
                    ins = nc.vector.tensor_scalar(at, at, mv[:, k, 0:1], rstd[:, k:k + 1], ALU.subtract, ALU.mult)
                ins.then_inc(y_ready, 1)

        @block.tensor
        def _(pe):
            def mm3(out, w, x, first, last):
                nc.tensor.matmul(out, w[0], x[0], start=first, stop=False, skip_group_check=True)
                nc.tensor.matmul(out, w[0], x[1], start=False, stop=False, skip_group_check=True)
                return nc.tensor.matmul(out, w[1], x[0], start=False, stop=last, skip_group_check=True)

            def cols(n):
                return slice(n * P, (n + 1) * P)

            pe.sem_inc(hid_used, RING)
            pe.sem_inc(logits, 1)
            pe.sem_inc(xT_psum, DC)
            pe.sem_inc(gateT_psum, 1)
            pe.wait_ge(ident_ready, 1)
            pe.wait_ge(consts_loaded, 4 * DMA)
            nc.tensor.transpose(xT_bank(0)[:, 0:E * FC], b1_rows[:, :], ident[0:E * FC, 0:E * FC]).then_inc(b1_psum, 1)
            pe.wait_ge(b1_ready, 1)
            with pe.Fori(0, B) as t:
                pe.wait_ge(x1_ready, t + 2)
                pe.wait_ge(xT_full, 2 * t + 2)
                for c in range(DC):
                    for k in range(TB):
                        ins = nc.tensor.transpose(xT_bank(c)[:, cols(k)], x1[:, k, cols(c)], ident[:, :])
                    ins.then_inc(xT_psum, 1)
                pe.wait_ge(xT_full, 2 * t + 4)
                for k in range(TB):
                    for c in range(DC):
                        ins = nc.tensor.matmul(logit_bank[:, bass.ds((t * TB + k) * E, E)], x1Tf[:, c, cols(k)], wr[:, c, :],
                                               start=c == 0, stop=c == DC - 1)
                ins.then_inc(logits, 1)
            with pe.Fori(0, B) as t:
                pe.wait_ge(gate_copied, t + 1)
                pe.wait_ge(gateT_ready, t + 1)
                for k in range(TB):
                    ins = nc.tensor.matmul(gateT_bank[0:E, cols(k)], gate_t[:, k, :], ident[:, :], start=True, stop=True)
                ins.then_inc(gateT_psum, 1)
                pe.wait_ge(gateT_ready, t + 2)
                pe.wait_ge(b2_added, t + 1)
                for k in range(TB):
                    ins = nc.tensor.matmul(b2_bank(k // 2)[:, (k % 2) * D:(k % 2 + 1) * D], gateT[:, cols(k)], b2_rows[:, :],
                                           start=True, stop=True)
                ins.then_inc(b2_psum, 1)
            pe.wait_ge(b2_added, B + 1)

            def up(w, t, chunk, j):
                pe.wait_ge(hid_relu, chunk + j + 1)
                for c in range(DC):
                    ins = mm3(hid_bank(j), [h[:, c * F + j * P:c * F + (j + 1) * P] for h in w],
                              [h[:, c, bass.ds(t * S, S)] for h in x1T], c == 0, c == DC - 1)
                ins.then_inc(hid_psum, 1)

            def down(w, chunk, j, parity):
                pe.wait_ge(hid_split, chunk + j + 1 + RING)
                r = j % RING
                for k in range(TB):
                    ins = mm3(out_bank(parity, k), [h[:, r, cols(k)] for h in hid],
                              [h[:, j * D:(j + 1) * D] for h in w], j == 0 and k % 2 == 0, j == FC - 1)
                ins.then_inc(hid_used, 1)
                return ins

            def tile(parity_e, t, tiles, parity_t, more):
                chunk = tiles * FC
                for j in range(FC):
                    if j + AHEAD < FC:
                        up(w1[parity_e], t, chunk, j + AHEAD)
                    elif more:
                        up(w1[parity_e], t + 1, chunk + FC, j + AHEAD - FC)
                    if j == 0:
                        pe.wait_ge(out_added, tiles + 1)
                    down(w2[parity_e], chunk, j, parity_t)

            with pe.Fori(0, E // 2) as pair_e:
                for parity_e in range(2):
                    e = pe.snap(pair_e * 2 + parity_e)
                    first = pe.snap(e * B)
                    pe.wait_ge(w1_split, e + 1)
                    pe.wait_ge(w2_split, e + 1)
                    for j in range(AHEAD):
                        up(w1[parity_e], 0, first * FC, j)
                    with pe.Fori(0, B // 2 - 1) as pair_t:
                        for parity_t in range(2):
                            t = pe.snap(pair_t * 2 + parity_t)
                            tile(parity_e, t, pe.snap(first + t), parity_t, True)
                    tile(parity_e, B - 2, pe.snap(first + B - 2), 0, True)
                    tile(parity_e, B - 1, pe.snap(first + B - 1), 1, False)


def build(nc, x, Wkqv, Wm1, bm1, Wm2, bm2, gn_g, gn_b, Wf1, bf1, Wf2, bf2, ln_g, ln_b,
          Wr, br, W1, b1, W2, b2, score_floor, out):
    B, S, D = x.shape
    L = Wkqv.shape[0]
    pairs = B // 2
    h_store = nc.dram_tensor("h_store", ((L + 1) * pairs, 2, S, D), F32, kind="Internal").ap()
    retention_layers(nc, x, Wkqv, Wm1, bm1, Wm2, bm2, gn_g, gn_b, Wf1, bf1, Wf2, bf2, ln_g, ln_b,
                     score_floor, h_store)
    expert_mixture(nc, x, h_store[L * pairs:, :, :, :], Wr, br, W1, b1, W2, b2, out)


_INS = ["L0_attn_x", "L0_attn_Wkqv", "L0_attn_Wm1", "L0_attn_bm1", "L0_attn_Wm2", "L0_attn_bm2",
        "L0_attn_gn_g", "L0_attn_gn_b", "L0_attn_Wf1", "L0_attn_bf1", "L0_attn_Wf2", "L0_attn_bf2",
        "L0_attn_ln_g", "L0_attn_ln_b", "L0_ffn_Wr", "L0_ffn_br", "L0_ffn_W1", "L0_ffn_b1", "L0_ffn_W2", "L0_ffn_b2"]


def kernel(**inputs):
    import numpy as np
    import concourse.bacc as bacc
    from concourse.bass_utils import run_bass_kernel_spmd

    arrays = {f"in_{name}": np.ascontiguousarray(inputs[name]) for name in _INS}
    B, S, D = arrays["in_L0_attn_x"].shape
    row = np.float32(np.sqrt(D)) * (1 + np.sqrt(np.arange(S, dtype=np.float32)))
    arrays["in_score_floor"] = np.ascontiguousarray(np.broadcast_to(row.astype(np.float32), (P, S)))
    nc = bacc.Bacc("TRN2", target_bir_lowering=False, num_devices=1)
    args = [nc.dram_tensor(n, a.shape, mybir.dt.from_np(a.dtype), kind="ExternalInput").ap() for n, a in arrays.items()]
    args.append(nc.dram_tensor("out", (B, S, D), F32, kind="ExternalOutput").ap())
    build(nc, *args)
    r = run_bass_kernel_spmd(nc, [arrays], core_ids=[0])
    return r.results[0]["out"]
```

```python
from contextlib import ExitStack

import concourse.bass as bass
from concourse import mybir

F32 = mybir.dt.float32
F32R = mybir.dt.float32r
ALU = mybir.AluOpType
ACT = mybir.ActivationFunctionType
AX = mybir.AxisListType

P = 128
EPS = 1e-5
NITER = 25
THRESH = 1e-9
DMA = 16


def f32(ap):
    return ap.bitcast(F32)


def hold(eng, held):
    eng.sem_inc(held, 1)


class Step:

    def __init__(self, it, base, layer):
        self.it, self.base, self.layer = it, base, layer


def retention_layers(nc, x, Wkqv, Wm1, bm1, Wm2, bm2, gn_g, gn_b, Wf1, bf1, Wf2, bf2,
                     ln_g, ln_b, score_floor, h_store, folded):
    B, S, D = x.shape
    L = Wkqv.shape[0]
    DC = D // P
    TB = S // P
    MC = Wm1.shape[2] // P
    FC = Wf1.shape[2] // P
    SLOTS = 2
    A_, B_ = 0, 1
    PAIRS = B // SLOTS
    STEPS = L * PAIRS
    U = 4
    LC = 2 * MC + 4 * DC
    assert (DC, TB, MC, FC, U) == (2, 4, 4, 4, 4)
    LO = [0, P, 2 * P, 2 * P]
    SPANS, end = {}, 0
    for name, width in (("qk", DC * D), ("vm", DC * MC * P), ("m2", DC * D), ("f1", DC * FC * P), ("f2", FC * D)):
        SPANS[name] = slice(end, end + width)
        end += width
    FOLD = SPANS["vm"].stop
    WEIGHTS = end

    x_v = x.rearrange("(i s) (k p) d -> i s p k d", s=SLOTS, p=P)
    h_v = h_store.rearrange("i s (k p) d -> i s p k d", p=P)

    with ExitStack() as ctx:
        def sb(name, shape, dt=F32):
            return ctx.enter_context(nc.sbuf_tensor(name, shape, dt))

        def sem(name):
            return ctx.enter_context(nc.semaphore(name))

        def sems(name):
            return [sem(f"{name}{s}") for s in range(SLOTS)]

        ident = sb("ident", [P, P])
        ones_r = sb("ones_r", [P, P], F32R)
        mean_w = sb("mean_w", [P, P])
        neg_half = sb("neg_half", [P, TB])
        floor = sb("floor", [P, S])
        const_rows = sb("const_rows", [L * LC, P])
        const_cols = sb("const_cols", [P, L * LC])
        raw = sb("raw", [P, WEIGHTS])
        w_full = [sb(f"w_{n}", [P, WEIGHTS], F32R) for n in ("hi", "lo")]

        def weight(name, chunks):
            return [w[:, SPANS[name]].rearrange("p (c n) -> p c n", c=chunks) for w in w_full]

        def slot_tiles(name, shape, dt=F32):
            return [sb(f"{name}{s}", shape, dt) for s in range(SLOTS)]

        def split_tiles(name, shape):
            return [[sb(f"{name}_{n}{s}", shape, F32R) for n in ("hi", "lo")] for s in range(SLOTS)]

        lc = slot_tiles("lc", [P, LC])
        lnv = slot_tiles("lnv", [P, 2 * D])
        lc_bm1, lc_bm2, lc_gg = ([c[:, a:b] for c in lc] for a, b in ((0, 4), (4, 6), (6, 8)))
        lc_gb, lc_bf1, lc_bf2 = ([c[:, a:b] for c in lc] for a, b in ((8, 10), (10, 14), (14, 16)))
        h_in = slot_tiles("h_in", [P, TB, D])
        h_out = slot_tiles("h_out", [P, TB, D])
        h_sp = split_tiles("h", [P, TB, D])
        hT_sp = split_tiles("hT", [P, DC, S])
        tu_sp = split_tiles("tu", [P, DC, S])
        ry_sp = split_tiles("ry", [P, DC, S])
        pf_sp = split_tiles("pf", [P, FC, S])
        tmp = slot_tiles("tmp", [P, 4, S])
        y = slot_tiles("y", [P, DC, S])
        z = slot_tiles("z", [P, TB, D])
        gstat = slot_tiles("gstat", [P, DC, 6])
        gmv = slot_tiles("gmv", [P, DC, 2])
        gin = slot_tiles("gin", [P, 2 * DC])
        gsm = slot_tiles("gsm", [P, 12])
        zstat = slot_tiles("zstat", [P, TB, 6])
        zmv = slot_tiles("zmv", [P, TB, 2])
        zr = slot_tiles("zr", [P, TB])

        raw_kqv = [y[B_][:, 0, :], y[B_][:, 1, :], z[B_][:, 0:DC, :].rearrange("p c d -> p (c d)")]
        raw_m1 = h_out[B_][:, :, :].rearrange("p k d -> p (k d)").rearrange("p (c n) -> p c n", c=DC)
        w_t = tmp[B_][:, 0:3, :]

        ps = ctx.enter_context(nc.psum_tensor("ps", [P, 8, 512], F32))

        def bank(s, r):
            return ps[:, 4 * s + r, :]

        GATE, VALUE = (1, 2), (0, 3)

        def score_bank(s, b):
            return bank(s, (2 + b) % 4)

        consts_loaded = sem("consts_loaded")
        ident_zero, ident_ready, pool_consts = sem("ident_zero"), sem("ident_ready"), sem("pool_consts")
        const_psum, const_ready = sem("const_psum"), sem("const_ready")
        qkv_loaded, raw_loaded = sem("qkv_loaded"), sem("raw_loaded")
        wt_psum, wt_ready = sem("wt_psum"), sem("wt_ready")
        fold_psum, fold_out, fold_stored = sem("fold_psum"), sem("fold_out"), sem("fold_stored")
        w_hi, w_lo = ({m: sem(f"{m}_{n}") for m in SPANS} for n in ("hi", "lo"))
        lc_ready, lnv_loaded = sems("lc_ready"), sems("lnv_loaded")
        h_loaded, h_stored = sems("h_loaded"), sems("h_stored")
        h_hi, h_lo = sems("h_hi"), sems("h_lo")
        hT_psum, hT_hi, hT_lo = sems("hT_psum"), sems("hT_hi"), sems("hT_lo")
        t_psum, t_hi, t_lo = sems("t_psum"), sems("t_hi"), sems("t_lo")
        s_psum, p_hi, p_lo, p_masked = sems("s_psum"), sems("p_hi"), sems("p_lo"), sems("p_masked")
        rowsum_psum, r_psum, r_scaled = sems("rowsum_psum"), sems("r_psum"), sems("r_scaled")
        r_hi, r_lo = sems("r_hi"), sems("r_lo")
        m_psum, gate_ready, u_ready = sems("m_psum"), sems("gate_ready"), sems("u_ready")
        u_hi, u_lo = sems("u_hi"), sems("u_lo")
        m2_psum, gn_in, gn_psum = sems("m2_psum"), sems("gn_in"), sems("gn_psum")
        y_ready, y_hi, y_lo = sems("y_ready"), sems("y_hi"), sems("y_lo")
        f1_psum, f_ready, f_hi, f_lo = sems("f1_psum"), sems("f_ready"), sems("f_hi"), sems("f_lo")
        f2_psum, z_ready = sems("f2_psum"), sems("z_ready")
        zT_psum, z_kept, h_new = sems("zT_psum"), sems("z_kept"), sems("h_new")
        g_var, g_rstd, z_var, z_rstd = sems("g_var"), sems("g_rstd"), sems("z_var"), sems("z_rstd")
        z_scaled = sems("z_scaled")
        scale_done, gn_done, ln_done = sems("scale_done"), sems("gn_done"), sems("ln_done")
        dve_held, pool_held = sem("dve_held"), sem("pool_held")

        block = ctx.enter_context(nc.Block())

        def run_steps(eng, first, body, tail):
            def at(it, layer):
                if isinstance(it, int):
                    return Step(it, it * U, layer)
                return Step(it, eng.snap(it * U), layer)

            def within(l):
                with eng.Fori(1, PAIRS) as p:
                    it = eng.snap(l * PAIRS + p)
                    body(at(it, l), at(eng.snap(it - 1), l), False)

            first(at(0, 0))
            within(0)
            with eng.Fori(1, L) as l:
                it = eng.snap(l * PAIRS)
                body(at(it, l), at(eng.snap(it - 1), eng.snap(l - 1)), True)
                within(l)
            tail(at(STEPS - 1, L - 1))

        @block.sync
        def _(sp):
            def chunks(w):
                return w.rearrange("(c p) n -> p c n", p=P)

            def load_fold_operands(l):
                if l:
                    sp.wait_ge(fold_psum, 3 * l)
                for i, dst in enumerate(raw_kqv):
                    sp.dma_start(dst.rearrange("p (c n) -> p c n", c=DC),
                                 chunks(Wkqv[l][:, i * D:(i + 1) * D])).then_inc(qkv_loaded, DMA)
                sp.dma_start(raw_m1, chunks(Wm1[l])).then_inc(qkv_loaded, DMA)

            def store_fold(l):
                sp.wait_ge(fold_out, 3 * l + 3)
                sp.dma_start(folded[l], raw[:, 0:FOLD]).then_inc(fold_stored, DMA)

            def load_plain_weights(l):
                for name, w in (("m2", Wm2), ("f1", Wf1), ("f2", Wf2)):
                    c = w.shape[1] // P
                    sp.dma_start(raw[:, SPANS[name]].rearrange("p (c n) -> p c n", c=c), chunks(w[l])).then_inc(raw_loaded, DMA)

            def next_weights(l):
                for name in SPANS:
                    sp.wait_ge(w_lo[name], l)
                sp.dma_start(raw[:, 0:FOLD], folded[l]).then_inc(raw_loaded, DMA)
                load_plain_weights(l)

            def load_lnv(s, l):
                sp.dma_start(lnv[s][:, 0:D], ln_g[bass.ds(l, 1), :].to_broadcast([P, D])).then_inc(lnv_loaded[s], DMA)
                sp.dma_start(lnv[s][:, D:2 * D], ln_b[bass.ds(l, 1), :].to_broadcast([P, D])).then_inc(lnv_loaded[s], DMA)

            def load_x(s, it):
                if not (isinstance(it, int) and it == 0):
                    sp.wait_ge(hT_psum[s], it * U)
                    sp.wait_ge(h_lo[s], it * U)
                sp.dma_start(h_in[s][:, :, :], x_v[it, s]).then_inc(h_loaded[s], DMA)

            def load_h(s, it):
                sp.wait_ge(hT_psum[s], it * U)
                sp.wait_ge(h_lo[s], it * U)
                sp.wait_ge(h_stored[s], (it - PAIRS + 2) * DMA)
                sp.dma_start(h_in[s][:, :, :], h_v[it, s]).then_inc(h_loaded[s], DMA)

            def store_h(s, it):
                sp.wait_ge(h_new[s], it * U + 2 * U)
                sp.dma_start(h_v[it + PAIRS, s], h_out[s][:, :, :]).then_inc(h_stored[s], DMA)

            def step(it, load, seam=None):
                for s in range(SLOTS):
                    if load:
                        load(s, it + 1)
                    store_h(s, it - 1)
                    if seam is not None:
                        load_lnv(s, seam)

            for s in range(SLOTS):
                sp.sem_inc(h_stored[s], DMA)
            load_fold_operands(0)
            load_x(A_, 0)
            load_plain_weights(0)
            sp.dma_start(floor[:, :], score_floor).then_inc(consts_loaded, DMA)
            load_x(B_, 0)
            for s in range(SLOTS):
                load_lnv(s, 0)
            for l in range(1, L):
                load_fold_operands(l)
                store_fold(l)
                if l == 1:
                    load_x(A_, 1)
            sp.wait_ge(fold_stored, (L - 1) * DMA)
            next_weights(1)
            load_x(B_, 1)
            with sp.Fori(1, PAIRS - 1) as it:
                step(it, load_x)
            step(PAIRS - 1, load_h)
            with sp.Fori(1, L - 1) as l:
                step(sp.snap(l * PAIRS), load_h, l)
                next_weights(sp.snap(l + 1))
                with sp.Fori(1, PAIRS) as p:
                    step(sp.snap(l * PAIRS + p), load_h)
            step((L - 1) * PAIRS, load_h, L - 1)
            with sp.Fori((L - 1) * PAIRS + 1, STEPS - 1) as it:
                step(it, load_h)
            step(STEPS - 1, None)
            for s in range(SLOTS):
                store_h(s, STEPS - 1)
            for s in range(SLOTS):
                sp.wait_ge(h_stored[s], (STEPS + 1) * DMA)

        @block.gpsimd
        def _(pool):
            nc.gpsimd.memset(ident[:, :], 0.0).then_inc(ident_zero, 1)
            pool.wait_ge(ident_zero, 1)
            nc.gpsimd.affine_select(out=ident[:, :], in_=ident[:, :], compare_op=ALU.not_equal, fill=1.0,
                                    base=0, pattern=[[-1, P]], channel_multiplier=1).then_inc(ident_ready, 1)
            nc.gpsimd.memset(f32(ones_r[:, :]), 1.0).then_inc(pool_consts, 1)
            nc.gpsimd.memset(neg_half[:, :], -0.5).then_inc(pool_consts, 1)
            nc.gpsimd.memset(mean_w[:, :], 1.0 / (P * DC)).then_inc(pool_consts, 1)
            pool.wait_ge(pool_consts, 3)

            def low_half(lo, full, hi, done, n):
                nc.gpsimd.tensor_tensor(out=lo, in0=full, in1=f32(hi), op=ALU.subtract).then_inc(done, n)

            def split_weight(name, l):
                pool.wait_ge(w_hi[name], l + 1)
                low_half(w_full[1][:, SPANS[name]], raw[:, SPANS[name]], w_full[0][:, SPANS[name]], w_lo[name], 1)

            def split_h(s, at):
                pool.wait_ge(h_hi[s], at.base + U)
                low_half(h_sp[s][1][:, :, :], h_in[s][:, :, :], h_sp[s][0][:, :, :], h_lo[s], U)

            def mask_scores(s, at, blocks):
                for b in blocks:
                    pool.wait_ge(p_lo[s], at.base + b + 1)
                    hold(pool, pool_held)
                    for half in range(2):
                        part = pf_sp[s][half][:, b, LO[b]:(b + 1) * P]
                        ins = nc.gpsimd.affine_select(
                            out=part, in_=f32(part), compare_op=ALU.is_ge, fill=0.0, base=LO[b] - b * P,
                            pattern=[[1, (b + 1) * P - LO[b]]], channel_multiplier=-1)
                    ins.then_inc(p_masked[s], 1)

            def rstd_group(s, at):
                pool.wait_ge(g_var[s], at.base + U)
                nc.gpsimd.tensor_tensor(out=gsm[s][:, 5:6], in0=gsm[s][:, 5:6], in1=neg_half[:, 0:1], op=ALU.pow).then_inc(g_rstd[s], U)

            def rstd_tokens(s, at):
                pool.wait_ge(z_var[s], at.base + U)
                nc.gpsimd.tensor_tensor(out=zr[s][:, :], in0=zr[s][:, :], in1=neg_half[:, :], op=ALU.pow).then_inc(z_rstd[s], U)

            def split_f(s, at):
                for c in range(FC):
                    pool.wait_ge(f_hi[s], at.base + c + 1)
                    low_half(pf_sp[s][1][:, c, :], tmp[s][:, c, :], pf_sp[s][0][:, c, :], f_lo[s], 1)

            def body(now, before, seam):
                if seam:
                    split_weight("qk", now.layer)
                split_h(A_, now)
                if seam:
                    split_weight("vm", now.layer)
                mask_scores(A_, now, (0,))
                if before:
                    rstd_group(B_, before)
                mask_scores(A_, now, (1, 2, 3))
                if before:
                    rstd_tokens(A_, before)
                if seam:
                    split_weight("m2", now.layer)
                if before:
                    split_f(B_, before)
                if seam:
                    split_weight("f1", now.layer)
                split_h(B_, now)
                if seam:
                    split_weight("f2", now.layer)
                rstd_group(A_, now)
                mask_scores(B_, now, range(TB))
                split_f(A_, now)
                if before:
                    rstd_tokens(B_, before)

            def first(now):
                for name in SPANS:
                    split_weight(name, 0)
                body(now, None, False)

            def tail(last):
                rstd_tokens(A_, last)
                rstd_group(B_, last)
                split_f(B_, last)
                rstd_tokens(B_, last)

            run_steps(pool, first, body, tail)

        @block.scalar
        def _(act):
            for s in range(SLOTS):
                act.sem_inc(z_kept[s], U)
            row = 0
            for l in range(L):
                for c in (bm1, bm2, gn_g, gn_b, bf1, bf2):
                    n = c.shape[1] // P
                    act.dma_start(const_rows[row:row + n, :], c[l].rearrange("(n p) -> n p", p=P)).then_inc(consts_loaded, DMA)
                    row += n
            act.wait_ge(const_psum, 1)
            nc.scalar.activation(const_cols[:, :], bank(A_, 0)[:, 0:L * LC], ACT.Copy).then_inc(const_ready, 1)

            def empty_fold(l):
                for i in range(3):
                    act.wait_ge(wt_psum, 3 * l + i + 1)
                    nc.scalar.activation(w_t[:, i, :], bank(B_, i), ACT.Copy).then_inc(wt_ready, 1)
                if l == 1:
                    act.wait_ge(w_lo["qk"], 1)
                    act.wait_ge(w_lo["vm"], 1)
                elif l > 1:
                    act.wait_ge(fold_stored, (l - 1) * DMA)
                for i, r in enumerate((3, 0, 1)):
                    act.wait_ge(fold_psum, 3 * l + i + 1)
                    nc.scalar.activation(raw[:, i * S:(i + 1) * S], bank(B_, r), ACT.Copy).then_inc(fold_out, 1)

            def high_weight(name, l):
                nc.scalar.activation(w_full[0][:, SPANS[name]], raw[:, SPANS[name]], ACT.Copy).then_inc(w_hi[name], 1)

            def next_high_weight(name, l, used, at):
                act.wait_ge(used, at.base + U)
                act.wait_ge(raw_loaded, l * (4 * DMA) + 3 * DMA)
                high_weight(name, l)

            def high_hT(s, at):
                for c in range(DC):
                    act.wait_ge(hT_psum[s], at.base + 2 * c + 2)
                    nc.scalar.activation(hT_sp[s][0][:, c, :], bank(s, 2 + c), ACT.Copy).then_inc(hT_hi[s], 2)

            def high_h(s, at):
                act.wait_ge(h_loaded[s], at.it * DMA + DMA)
                nc.scalar.activation(h_sp[s][0][:, :, :], h_in[s][:, :, :], ACT.Copy).then_inc(h_hi[s], U)

            def high_t(s, at):
                for c in range(DC):
                    act.wait_ge(t_psum[s], at.base + 2 * c + 2)
                    nc.scalar.activation(tu_sp[s][0][:, c, :], bank(s, 2 + c), ACT.Copy).then_inc(t_hi[s], 2)

            def high_p(s, at, blocks):
                for b in blocks:
                    act.wait_ge(s_psum[s], at.base + b + 1)
                    nc.scalar.activation(pf_sp[s][0][:, b, LO[b]:S], score_bank(s, b)[:, LO[b]:S], ACT.Copy).then_inc(p_hi[s], 1)

            def high_r(s, at):
                for c in range(DC):
                    act.wait_ge(r_scaled[s], at.base + 2 * c + 2)
                    nc.scalar.activation(ry_sp[s][0][:, c, :], tmp[s][:, c, :], ACT.Copy).then_inc(r_hi[s], 2)

            def gate(s, at, c):
                act.wait_ge(lc_ready[s], at.layer + 1)
                act.wait_ge(m_psum[s], at.base + 2 * c + 1)
                nc.scalar.activation(tmp[s][:, 2 + c, :], bank(s, GATE[c]), ACT.Silu,
                                     bias=lc_bm1[s][:, DC + c:DC + c + 1]).then_inc(gate_ready[s], 2)

            def high_u(s, at, c):
                act.wait_ge(u_ready[s], at.base + 2 * c + 2)
                nc.scalar.activation(tu_sp[s][0][:, c, :], tmp[s][:, c, :], ACT.Copy).then_inc(u_hi[s], 2)

            def high_y(s, at):
                for c in range(DC):
                    act.wait_ge(y_ready[s], at.base + 2 * c + 2)
                    nc.scalar.activation(ry_sp[s][0][:, c, :], y[s][:, c, :], ACT.Copy).then_inc(y_hi[s], 2)

            def gelu(s, at, c):
                act.wait_ge(f1_psum[s], at.base + c + 1)
                nc.scalar.activation(tmp[s][:, c, :], bank(s, c), ACT.Gelu, bias=lc_bf1[s][:, c:c + 1]).then_inc(f_ready[s], 1)

            def high_f(s, at, c):
                act.wait_ge(f_ready[s], at.base + c + 1)
                nc.scalar.activation(pf_sp[s][0][:, c, :], tmp[s][:, c, :], ACT.Copy).then_inc(f_hi[s], 1)

            def hidden(s, at):
                gelu(s, at, 0)
                for c in range(1, FC):
                    gelu(s, at, c)
                    high_f(s, at, c - 1)

            def keep_z(s, at):
                act.wait_ge(h_new[s], at.base + U)
                for i in range(2):
                    act.wait_ge(zT_psum[s], at.base + 2 * i + 2)
                    nc.scalar.activation(z[s][:, 2 * i:2 * i + 2, :].rearrange("p k d -> p (k d)"), bank(s, i),
                                         ACT.Copy).then_inc(z_kept[s], 2)

            def body(now, before, seam):
                if seam:
                    next_high_weight("qk", now.layer, t_psum[B_], before)
                high_hT(A_, now)
                if before:
                    gate(B_, before, 0)
                    high_h(A_, now)
                    high_u(B_, before, 0)
                    gate(B_, before, 1)
                    high_u(B_, before, 1)
                else:
                    high_h(A_, now)
                    empty_fold(1)
                high_t(A_, now)
                if seam:
                    next_high_weight("vm", now.layer, m_psum[B_], before)
                if before:
                    keep_z(A_, before)
                else:
                    empty_fold(2)
                high_p(A_, now, range(TB))
                if seam:
                    next_high_weight("m2", now.layer, m2_psum[B_], before)
                if before:
                    high_y(B_, before)
                    hidden(B_, before)
                else:
                    empty_fold(3)
                high_r(A_, now)
                if before:
                    high_f(B_, before, FC - 1)
                for c in range(DC):
                    gate(A_, now, c)
                    high_u(A_, now, c)
                if seam:
                    next_high_weight("f1", now.layer, f1_psum[B_], before)
                high_hT(B_, now)
                high_h(B_, now)
                if seam:
                    next_high_weight("f2", now.layer, f2_psum[B_], before)
                high_t(B_, now)
                if before:
                    keep_z(B_, before)
                high_p(B_, now, range(TB - 1))
                high_y(A_, now)
                high_p(B_, now, (TB - 1,))
                hidden(A_, now)
                high_f(A_, now, FC - 1)
                high_r(B_, now)

            def first(now):
                empty_fold(0)
                act.wait_ge(fold_out, 3)
                for name in SPANS:
                    if name == "m2":
                        act.wait_ge(raw_loaded, 3 * DMA)
                    high_weight(name, 0)
                body(now, None, False)

            def tail(last):
                for c in range(DC):
                    gate(B_, last, c)
                    high_u(B_, last, c)
                keep_z(A_, last)
                high_y(B_, last)
                hidden(B_, last)
                high_f(B_, last, FC - 1)
                keep_z(B_, last)

            assert L == 4
            run_steps(act, first, body, tail)

        SCALE_CHAIN, GN_CHAIN, LN_CHAIN = 3, 9, 2

        @block.vector
        def _(dve):
            for s in range(SLOTS):
                dve.sem_inc(h_new[s], U)
            dve.wait_ge(const_ready, 1)

            def landed(ins, done, value):
                ins.then_inc(done, 1)
                dve.wait_ge(done, value)

            def sub_hi(lo, full, hi, done, n):
                nc.vector.tensor_tensor(out=lo, in0=full, in1=f32(hi), op=ALU.subtract).then_inc(done, n)

            def next_constants(s, l):
                nc.vector.tensor_copy(lc[s][:, :], const_cols[:, bass.ds(l * LC, LC)]).then_inc(lc_ready[s], 1)

            def low_hT(s, at):
                for c in range(DC):
                    dve.wait_ge(hT_hi[s], at.base + 2 * c + 2)
                    sub_hi(hT_sp[s][1][:, c, :], bank(s, 2 + c), hT_sp[s][0][:, c, :], hT_lo[s], 2)

            def low_t(s, at):
                for c in range(DC):
                    dve.wait_ge(t_hi[s], at.base + 2 * c + 2)
                    sub_hi(tu_sp[s][1][:, c, :], bank(s, 2 + c), tu_sp[s][0][:, c, :], t_lo[s], 2)

            def low_p(s, at, blocks):
                for b in blocks:
                    dve.wait_ge(p_hi[s], at.base + b + 1)
                    sub_hi(pf_sp[s][1][:, b, LO[b]:S], score_bank(s, b)[:, LO[b]:S], pf_sp[s][0][:, b, LO[b]:S], p_lo[s], 1)

            def low_r(s, at):
                for c in range(DC):
                    dve.wait_ge(r_hi[s], at.base + 2 * c + 2)
                    sub_hi(ry_sp[s][1][:, c, :], tmp[s][:, c, :], ry_sp[s][0][:, c, :], r_lo[s], 2)

            def low_u(s, at, c):
                dve.wait_ge(u_hi[s], at.base + 2 * c + 2)
                sub_hi(tu_sp[s][1][:, c, :], tmp[s][:, c, :], tu_sp[s][0][:, c, :], u_lo[s], 2)

            def low_y(s, at):
                for c in range(DC):
                    dve.wait_ge(y_hi[s], at.base + 2 * c + 2)
                    sub_hi(ry_sp[s][1][:, c, :], y[s][:, c, :], ry_sp[s][0][:, c, :], y_lo[s], 2)

            def scale_r(s, at):
                base = at.it * SCALE_CHAIN
                dve.wait_ge(rowsum_psum[s], at.base + U)
                landed(nc.vector.tensor_tensor(out=tmp[s][:, 3, :], in0=bank(s, 0), in1=floor[:, :], op=ALU.max), scale_done[s], base + 1)
                landed(nc.vector.scalar_tensor_tensor(out=tmp[s][:, 2, :], in0=bank(s, 0), scalar=-1.0, in1=tmp[s][:, 3, :],
                                                      op0=ALU.mult, op1=ALU.max), scale_done[s], base + 2)
                landed(nc.vector.reciprocal(tmp[s][:, 3, :], tmp[s][:, 2, :]), scale_done[s], base + 3)
                for c in range(DC):
                    dve.wait_ge(r_psum[s], at.base + 2 * c + 2)
                    nc.vector.tensor_tensor(out=tmp[s][:, c, :], in0=bank(s, 2 + c), in1=tmp[s][:, 3, :],
                                            op=ALU.mult).then_inc(r_scaled[s], 2)

            def gated(s, at, c):
                dve.wait_ge(m_psum[s], at.base + 2 * c + 2)
                dve.wait_ge(gate_ready[s], at.base + 2 * c + 2)
                nc.vector.scalar_tensor_tensor(
                    out=tmp[s][:, c, :], in0=bank(s, VALUE[c]), scalar=lc_bm1[s][:, c:c + 1],
                    in1=tmp[s][:, 2 + c, :], op0=ALU.add, op1=ALU.mult).then_inc(u_ready[s], 2)

            def group_parts(s):
                sq, mom, rstd = gsm[s][:, 0:2], gsm[s][:, 2:4], gsm[s][:, 5:6]
                return sq, mom, rstd, gsm[s][:, 6:8], gsm[s][:, 8:10], gsm[s][:, 10:12]

            def groupnorm_in(s, at):
                sq, mom, rstd, gain, off0, off = group_parts(s)
                base = at.it * GN_CHAIN
                for c in range(DC):
                    dve.wait_ge(m2_psum[s], at.base + 2 * c + 2)
                    ins = nc.vector.bn_stats(gstat[s][:, c, :], bank(s, c))
                landed(ins, gn_done[s], base + 1)
                hold(dve, dve_held)
                for c in range(DC):
                    ins = nc.vector.bn_aggr(gmv[s][:, c, :], gstat[s][:, c, :])
                landed(ins, gn_done[s], base + 2)
                landed(nc.vector.tensor_tensor(out=gin[s][:, 0:2], in0=gmv[s][:, :, 0], in1=lc_bm2[s], op=ALU.add), gn_done[s], base + 3)
                landed(nc.vector.tensor_tensor(out=sq, in0=gin[s][:, 0:2], in1=gin[s][:, 0:2], op=ALU.mult), gn_done[s], base + 4)
                nc.vector.scalar_tensor_tensor(out=gin[s][:, 2:4], in0=sq, scalar=EPS, in1=gmv[s][:, :, 1],
                                               op0=ALU.add, op1=ALU.add).then_inc(gn_in[s], U)

            def groupnorm_var(s, at):
                sq, mom, rstd, gain, off0, off = group_parts(s)
                base = at.it * GN_CHAIN
                dve.wait_ge(gn_psum[s], at.base + U)
                landed(nc.vector.tensor_reduce(out=mom, in_=bank(s, 2)[:, 0:4].rearrange("p (q c) -> p q c", c=DC),
                                               op=ALU.add, axis=AX.X), gn_done[s], base + 5)
                nc.vector.scalar_tensor_tensor(out=rstd, in0=mom[:, 0:1], scalar=mom[:, 0:1], in1=mom[:, 1:2],
                                               op0=ALU.mult, op1=ALU.subtract, reverse1=True).then_inc(g_var[s], U)

            def groupnorm_out(s, at):
                sq, mom, rstd, gain, off0, off = group_parts(s)
                base = at.it * GN_CHAIN
                dve.wait_ge(g_rstd[s], at.base + U)
                landed(nc.vector.tensor_scalar(gain, lc_gg[s], rstd, None, ALU.mult), gn_done[s], base + 6)
                landed(nc.vector.scalar_tensor_tensor(out=off0, in0=lc_bm2[s], scalar=mom[:, 0:1], in1=gain,
                                                      op0=ALU.subtract, op1=ALU.mult), gn_done[s], base + 7)
                nc.vector.tensor_tensor(out=off, in0=off0, in1=lc_gb[s], op=ALU.add).then_inc(gn_done[s], 1)
                for c in range(DC):
                    ins = nc.vector.scalar_tensor_tensor(
                        out=tmp[s][:, c, :], in0=bank(s, c), scalar=gain[:, c:c + 1], in1=f32(hT_sp[s][0][:, c, :]),
                        op0=ALU.mult, op1=ALU.add)
                landed(ins, gn_done[s], base + 9)
                for c in range(DC):
                    nc.vector.scalar_tensor_tensor(
                        out=y[s][:, c, :], in0=tmp[s][:, c, :], scalar=off[:, c:c + 1], in1=f32(hT_sp[s][1][:, c, :]),
                        op0=ALU.add, op1=ALU.add).then_inc(y_ready[s], 2)

            def residual(s, at, c):
                dve.wait_ge(f2_psum[s], at.base + 2 * c + 2)
                nc.vector.scalar_tensor_tensor(
                    out=y[s][:, c, :], in0=bank(s, c), scalar=lc_bf2[s][:, c:c + 1], in1=y[s][:, c, :],
                    op0=ALU.add, op1=ALU.add).then_inc(z_ready[s], 2)

            def layernorm_var(s, at):
                base = at.it * LN_CHAIN
                dve.wait_ge(z_kept[s], at.base + 2 * U)
                for k in range(TB):
                    ins = nc.vector.bn_stats(zstat[s][:, k, :], z[s][:, k, :])
                landed(ins, ln_done[s], base + 1)
                hold(dve, dve_held)
                for k in range(TB):
                    ins = nc.vector.bn_aggr(zmv[s][:, k, :], zstat[s][:, k, :])
                landed(ins, ln_done[s], base + 2)
                nc.vector.tensor_scalar(zr[s][:, :], zmv[s][:, :, 1], EPS, None, ALU.add).then_inc(z_var[s], U)

            def layernorm_out(s, at):
                dve.wait_ge(lnv_loaded[s], at.layer * (2 * DMA) + 2 * DMA)
                for k in range(TB):
                    ins = nc.vector.scalar_tensor_tensor(out=z[s][:, k, :], in0=z[s][:, k, :], scalar=zmv[s][:, k, 0:1],
                                                         in1=lnv[s][:, 0:D], op0=ALU.subtract, op1=ALU.mult)
                ins.then_inc(z_scaled[s], U)
                dve.wait_ge(z_scaled[s], at.base + U)
                dve.wait_ge(h_stored[s], at.it * DMA + DMA)
                dve.wait_ge(z_rstd[s], at.base + U)
                for k in range(TB):
                    ins = nc.vector.scalar_tensor_tensor(out=h_out[s][:, k, :], in0=z[s][:, k, :], scalar=zr[s][:, k:k + 1],
                                                         in1=lnv[s][:, D:2 * D], op0=ALU.mult, op1=ALU.add)
                ins.then_inc(h_new[s], U)

            def body(now, before, seam):
                if before:
                    for c in range(DC):
                        residual(A_, before, c)
                if seam:
                    dve.wait_ge(z_ready[A_], before.base + U)
                    hold(dve, dve_held)
                    next_constants(A_, now.layer)
                low_hT(A_, now)
                if before:
                    for c in range(DC):
                        gated(B_, before, c)
                        low_u(B_, before, c)
                low_t(A_, now)
                if before:
                    layernorm_var(A_, before)
                    groupnorm_in(B_, before)
                low_p(A_, now, (0,))
                if before:
                    groupnorm_var(B_, before)
                low_p(A_, now, (1, 2, 3))
                if before:
                    groupnorm_out(B_, before)
                    low_y(B_, before)
                scale_r(A_, now)
                low_r(A_, now)
                if before:
                    layernorm_out(A_, before)
                if seam:
                    dve.wait_ge(lc_ready[A_], now.layer + 1)
                for c in range(DC):
                    gated(A_, now, c)
                    low_u(A_, now, c)
                if before:
                    residual(B_, before, 0)
                low_hT(B_, now)
                if before:
                    residual(B_, before, 1)
                if seam:
                    dve.wait_ge(z_ready[B_], before.base + U)
                    hold(dve, dve_held)
                    next_constants(B_, now.layer)
                groupnorm_in(A_, now)
                low_t(B_, now)
                groupnorm_var(A_, now)
                groupnorm_out(A_, now)
                low_y(A_, now)
                low_p(B_, now, range(TB))
                if before:
                    layernorm_var(B_, before)
                scale_r(B_, now)
                low_r(B_, now)
                if before:
                    layernorm_out(B_, before)

            def first(now):
                for s in range(SLOTS):
                    next_constants(s, 0)
                    dve.wait_ge(lc_ready[s], 1)
                body(now, None, False)

            def tail(last):
                for c in range(DC):
                    residual(A_, last, c)
                for c in range(DC):
                    gated(B_, last, c)
                    low_u(B_, last, c)
                layernorm_var(A_, last)
                groupnorm_in(B_, last)
                layernorm_out(A_, last)
                groupnorm_var(B_, last)
                groupnorm_out(B_, last)
                low_y(B_, last)
                for c in range(DC):
                    residual(B_, last, c)
                layernorm_var(B_, last)
                layernorm_out(B_, last)

            run_steps(dve, first, body, tail)

        @block.tensor
        def _(pe):
            def mm3(out, w, x, first, last):
                nc.tensor.matmul(out, w[0], x[0], start=first, stop=False, skip_group_check=True)
                nc.tensor.matmul(out, w[0], x[1], start=False, stop=False, skip_group_check=True)
                return nc.tensor.matmul(out, w[1], x[0], start=False, stop=last, skip_group_check=True)

            def both(pair, *index):
                return [t[index] for t in pair]

            ALL = slice(None)

            def cols(n):
                return slice(n * P, (n + 1) * P)

            pe.wait_ge(ident_ready, 1)
            pe.wait_ge(pool_consts, 3)
            pe.wait_ge(consts_loaded, (6 * L + 1) * DMA)
            nc.tensor.transpose(bank(A_, 0)[:, 0:L * LC], const_rows[:, :], ident[0:L * LC, 0:L * LC]).then_inc(const_psum, 1)

            def fold(l):
                pe.wait_ge(qkv_loaded, 4 * DMA * (l + 1))
                if l:
                    pe.wait_ge(fold_out, 3 * l)
                for i in range(3):
                    for cc in range(DC):
                        for dh in range(DC):
                            ins = nc.tensor.transpose(bank(B_, i)[:, cc * D + dh * P:cc * D + (dh + 1) * P],
                                                      raw_kqv[i][:, dh * D + cc * P:dh * D + (cc + 1) * P], ident[:, :])
                    ins.then_inc(wt_psum, 1)
                wt = w_t.rearrange("p i (c d) -> p i c d", c=DC)
                pe.wait_ge(wt_ready, 3 * l + 2)
                for dh in range(DC):
                    for cc in range(DC):
                        ins = nc.tensor.matmul(bank(B_, 3)[:, dh * D:(dh + 1) * D], wt[:, 1, cc, cols(dh)], wt[:, 0, cc, :],
                                               start=cc == 0, stop=cc == DC - 1)
                ins.then_inc(fold_psum, 1)
                pe.wait_ge(wt_ready, 3 * l + 3)
                for dh in range(DC):
                    for cc in range(DC):
                        ins = nc.tensor.matmul(bank(B_, dh), wt[:, 2, cc, cols(dh)], raw_m1[:, cc, :],
                                               start=cc == 0, stop=cc == DC - 1)
                    ins.then_inc(fold_psum, 1)

            def transpose_h(s, at):
                pe.wait_ge(h_loaded[s], at.it * DMA + DMA)
                for c in range(DC):
                    for k in range(TB):
                        ins = nc.tensor.transpose(bank(s, 2 + c)[:, cols(k)], h_in[s][:, k, cols(c)], ident[:, :])
                    ins.then_inc(hT_psum[s], 2)

            def project_t(s, at):
                w = weight("qk", DC)
                pe.wait_ge(w_lo["qk"], at.layer + 1)
                for c in range(DC):
                    for k in range(DC):
                        pe.wait_ge(hT_lo[s], at.base + 2 * k + 2)
                        ins = mm3(bank(s, 2 + c), both(w, ALL, k, cols(c)), both(hT_sp[s], ALL, k), k == 0, k == DC - 1)
                    ins.then_inc(t_psum[s], 2)

            def scores(s, at, blocks):
                for b in blocks:
                    q = slice(LO[b], S)
                    if b == 2:
                        pe.wait_ge(z_kept[s], at.base + U)
                    for k in range(DC):
                        pe.wait_ge(t_lo[s], at.base + 2 * k + 2)
                        ins = mm3(score_bank(s, b)[:, q], both(hT_sp[s], ALL, k, cols(b)), both(tu_sp[s], ALL, k, q),
                                  k == 0, k == DC - 1)
                    ins.then_inc(s_psum[s], 1)

            def retain(s, at):
                def weighted_h(b):
                    q = slice(LO[b], S)
                    for c in range(DC):
                        pe.wait_ge(p_masked[s], at.base + max(b, c) + 1)
                        ins = mm3(bank(s, 2 + c)[:, q], both(h_sp[s], ALL, b, cols(c)), both(pf_sp[s], ALL, b, q),
                                  b == 0, b == TB - 1)
                        if b == TB - 1:
                            ins.then_inc(r_psum[s], 2)

                pe.wait_ge(h_lo[s], at.base + U)
                weighted_h(0)
                weighted_h(1)
                for b in range(TB):
                    q = slice(LO[b], S)
                    pe.wait_ge(p_masked[s], at.base + max(b, 2) + 1)
                    for half in range(2):
                        ins = nc.tensor.matmul(bank(s, 0)[:, q], ones_r[:, :], pf_sp[s][half][:, b, q],
                                               start=b == 0 and half == 0, stop=b == TB - 1 and half == 1,
                                               skip_group_check=True)
                ins.then_inc(rowsum_psum[s], U)
                weighted_h(2)
                weighted_h(3)

            def gated_projection(s, at):
                w = weight("vm", DC)
                pe.wait_ge(w_lo["vm"], at.layer + 1)
                for r, n in ((GATE[0], DC), (VALUE[0], 0), (GATE[1], DC + 1), (VALUE[1], 1)):
                    for k in range(DC):
                        pe.wait_ge(r_lo[s], at.base + 2 * k + 2)
                        ins = mm3(bank(s, r), both(w, ALL, k, cols(n)), both(ry_sp[s], ALL, k), k == 0, k == DC - 1)
                    ins.then_inc(m_psum[s], 1)

            def out_projection(s, at):
                w = weight("m2", DC)
                pe.wait_ge(w_lo["m2"], at.layer + 1)
                for c in range(DC):
                    for k in range(DC):
                        pe.wait_ge(u_lo[s], at.base + 2 * k + 2)
                        ins = mm3(bank(s, c), both(w, ALL, k, cols(c)), both(tu_sp[s], ALL, k), k == 0, k == DC - 1)
                    ins.then_inc(m2_psum[s], 2)

            def group_moments(s, at):
                pe.wait_ge(gn_in[s], at.base + U)
                nc.tensor.matmul(bank(s, 2)[:, 0:2 * DC], mean_w[:, :], gin[s][:, :], start=True,
                                 stop=True).then_inc(gn_psum[s], U)

            def up_projection(s, at):
                w = weight("f1", DC)
                pe.wait_ge(w_lo["f1"], at.layer + 1)
                for n in range(FC):
                    for k in range(DC):
                        pe.wait_ge(y_lo[s], at.base + 2 * k + 2)
                        ins = mm3(bank(s, n), both(w, ALL, k, cols(n)), both(ry_sp[s], ALL, k), k == 0, k == DC - 1)
                    ins.then_inc(f1_psum[s], 1)

            def down_projection(s, at, c):
                w = weight("f2", FC)
                pe.wait_ge(w_lo["f2"], at.layer + 1)
                for k in range(FC):
                    pe.wait_ge(f_lo[s], at.base + k + 1)
                    ins = mm3(bank(s, c), both(w, ALL, k, cols(c)), both(pf_sp[s], ALL, k), k == 0, k == FC - 1)
                ins.then_inc(f2_psum[s], 2)

            def transpose_z(s, at):
                pe.wait_ge(z_ready[s], at.base + U)
                for k in range(TB):
                    for c in range(DC):
                        to = (k % 2) * D + c * P
                        ins = nc.tensor.transpose(bank(s, k // 2)[:, to:to + P], y[s][:, c, cols(k)], ident[:, :])
                    if k % 2:
                        ins.then_inc(zT_psum[s], 2)

            def body(now, before, seam):
                transpose_h(A_, now)
                if before:
                    gated_projection(B_, before)
                else:
                    fold(1)
                project_t(A_, now)
                if before:
                    transpose_z(A_, before)
                    out_projection(B_, before)
                else:
                    fold(2)
                scores(A_, now, (0, 1))
                if before:
                    group_moments(B_, before)
                scores(A_, now, (2, 3))
                retain(A_, now)
                if before:
                    up_projection(B_, before)
                else:
                    fold(3)
                gated_projection(A_, now)
                if before:
                    down_projection(B_, before, 0)
                transpose_h(B_, now)
                if before:
                    down_projection(B_, before, 1)
                out_projection(A_, now)
                project_t(B_, now)
                if before:
                    transpose_z(B_, before)
                group_moments(A_, now)
                scores(B_, now, range(TB))
                up_projection(A_, now)
                retain(B_, now)
                for c in range(DC):
                    down_projection(A_, now, c)

            def first(now):
                fold(0)
                body(now, None, False)

            def tail(last):
                gated_projection(B_, last)
                transpose_z(A_, last)
                out_projection(B_, last)
                group_moments(B_, last)
                up_projection(B_, last)
                for c in range(DC):
                    down_projection(B_, last, c)
                transpose_z(B_, last)

            run_steps(pe, first, body, tail)


def expert_mixture(nc, x, h_last, Wr, br, W1, b1, W2, b2, out):
    E, D, F = W1.shape
    B, S, _ = x.shape
    DC, FC, TB = D // P, F // P, S // P
    NB = B * TB
    RING = 4
    FULL = 2
    AHEAD = 2
    OUTS = 2
    POW_AT = 5

    x_v = x.rearrange("t (k p) d -> t p k d", p=P)
    h_v = h_last.rearrange("i s (k p) d -> (i s) p k d", p=P)
    out_v = out.rearrange("t (k p) d -> t p k d", p=P)
    w1_v = W1.rearrange("e (c p) f -> e p c f", p=P)
    w2_v = W2.rearrange("e (c p) d -> e p c d", p=P)

    with ExitStack() as ctx:
        def sb(name, shape, dt=F32):
            return ctx.enter_context(nc.sbuf_tensor(name, shape, dt))

        def sem(name):
            return ctx.enter_context(nc.semaphore(name))

        ident = sb("m_ident", [P, P])
        b1_rows = sb("b1_rows", [E * FC, P])
        b1_cols = sb("b1_cols", [P, E * FC])
        b1_e = sb("b1_e", [P, FC])
        b2_bc = sb("b2_bc", [P, 2, D])
        wr = sb("wr", [P, DC, E])
        br_bc = sb("br_bc", [P, E])
        x1T = [sb(f"x1T_{n}", [P, DC, B * S], F32R) for n in ("hi", "lo")]
        acc = sb("acc", [P, NB, D])
        raw1 = sb("raw1", [P, DC * F])
        raw2 = sb("raw2", [P, FC * D])
        w_even = sb("w_even", [P, 4, DC * F], F32R)
        with ExitStack() as early:
            def before(name, shape):
                return early.enter_context(nc.sbuf_tensor(name, shape, F32))

            xh = before("xh", [P, NB, D])
            x1 = [before(f"x1_{n}", [P, TB, D]) for n in range(2)]
            x1Tf = [before(f"x1Tf{n}", [P, DC, S]) for n in range(2)]
        w_odd = sb("w_odd", [P, 4, DC * F], F32R)
        hid = [sb(f"hid_{n}", [P, RING, S], F32R) for n in ("hi", "lo")]
        w1 = [[w[:, 0, :], w[:, 1, :]] for w in (w_even, w_odd)]
        w2 = [[w[:, 2, :], w[:, 3, :]] for w in (w_even, w_odd)]
        act32 = sb("act32", [P, FULL, S])
        tile_out = sb("tile_out", [P, TB, D])
        stat = [sb(f"m_stat{n}", [P, TB, 6]) for n in range(2)]
        mv = [sb(f"m_mv{n}", [P, TB, 2]) for n in range(2)]
        rstd = [sb(f"rstd{n}", [P, TB]) for n in range(2)]
        neg_half = sb("m_neg_half", [P, TB])
        gates = sb("gates", [P, NB, E])
        ent_w = tile_out[:, 0, 0:NB * E].rearrange("p (n e) -> p n e", e=E)
        ent_s = tile_out[:, 1, 0:NB * 8].rearrange("p (i n) -> p i n", n=NB)

        ps = ctx.enter_context(nc.psum_tensor("m_ps", [P, 8, 512], F32))

        def hid_bank(n):
            return ps[:, n % RING, :]

        def out_half(parity, half):
            return ps[:, RING + 2 * parity + half, :]

        def out_bank(parity, k):
            return out_half(parity, k // 2)[:, (k % 2) * D:(k % 2 + 1) * D]

        def xT_bank(parity, c):
            return ps[:, 2 * parity + c, :]

        logit_bank, b1_bank = ps[:, 4, :], ps[:, 5, :]

        consts_loaded, ident_zero, ident_ready = sem("m_consts"), sem("m_ident_zero"), sem("m_ident_ready")
        b1_psum, b1_ready = sem("b1_psum"), sem("b1_ready")
        xh_loaded = [sem("xh_loaded_even"), sem("xh_loaded_odd")]
        x1_ready, x1_kept = sem("x1_ready"), sem("x1_kept")
        xT_psum, xT_full, xT_split, logits = sem("xT_psum"), sem("xT_full"), sem("xT_split"), sem("logits")
        raw_loaded, b2_loaded = sem("m_raw_loaded"), [sem("b2_loaded_even"), sem("b2_loaded_odd")]
        w_high, w1_split, w2_split = sem("w_high"), sem("w1_split"), sem("w2_split")
        hid_psum, hid_relu, hid_split, hid_used = sem("hid_psum"), sem("hid_relu"), sem("hid_split"), sem("hid_used")
        b2_added, out_added = sem("b2_added"), sem("out_added")
        y_ready, y_stored = sem("out_ready"), sem("out_stored")
        m_var, m_rstd = sem("m_var"), sem("m_rstd")
        dve_done, dve_held = sem("m_dve_done"), sem("m_dve_held")
        act_held, pool_held = sem("m_act_held"), sem("m_pool_held")

        block = ctx.enter_context(nc.Block())

        @block.sync
        def _(sp):
            def load_tile(t, parity):
                sp.dma_start(acc[:, bass.ds(t * TB, TB), :], x_v[t]).then_inc(xh_loaded[parity], DMA)
                sp.dma_start(xh[:, bass.ds(t * TB, TB), :], h_v[t]).then_inc(xh_loaded[parity], DMA)

            def load_weights(e):
                sp.dma_start(raw1[:, :].rearrange("p (c f) -> p c f", c=DC), w1_v[e]).then_inc(raw_loaded, DMA)
                sp.dma_start(raw2[:, :].rearrange("p (c d) -> p c d", c=FC), w2_v[e]).then_inc(raw_loaded, DMA)

            def load_bias(e, parity):
                sp.dma_start(b2_bc[:, parity, :], b2[bass.ds(e, 1), :].to_broadcast([P, D])).then_inc(b2_loaded[parity], DMA)

            def next_expert(e, parity):
                sp.wait_ge(w1_split, e)
                sp.wait_ge(w2_split, e)
                load_weights(e)
                sp.wait_ge(b2_added, 2 * B * (e - 1) + 2 * OUTS)
                load_bias(e, parity)

            for t in range(2):
                load_tile(t, t)
            for dst, src in ((b1_rows[:, :], b1.rearrange("e (n p) -> (e n) p", p=P)),
                             (wr[:, :, :], Wr.rearrange("(c p) e -> p c e", p=P)),
                             (br_bc[:, :], br.rearrange("(a e) -> a e", a=1).to_broadcast([P, E]))):
                sp.dma_start(dst, src).then_inc(consts_loaded, DMA)
            load_weights(0)
            with sp.Fori(1, B // 2) as pair:
                for parity in range(2):
                    sp.wait_ge(m_var, pair * 2 + parity - 1)
                    load_tile(sp.snap(pair * 2 + parity), parity)
            for e in range(2):
                load_bias(e, e)
            sp.wait_ge(w1_split, 1)
            sp.wait_ge(w2_split, 1)
            load_weights(1)
            with sp.Fori(1, E // 2) as pair:
                for parity in range(2):
                    next_expert(sp.snap(pair * 2 + parity), parity)
            with sp.Fori(0, B) as t:
                sp.wait_ge(y_ready, t + 1)
                sp.dma_start(out_v[t], acc[:, bass.ds(t * TB, TB), :]).then_inc(y_stored, DMA)
            sp.wait_ge(y_stored, B * DMA)

        @block.gpsimd
        def _(pool):
            pool.sem_inc(hid_split, FULL)
            pool.sem_inc(xT_split, 2)
            nc.gpsimd.memset(ident[:, :], 0.0).then_inc(ident_zero, 1)
            pool.wait_ge(ident_zero, 1)
            nc.gpsimd.affine_select(out=ident[:, :], in_=ident[:, :], compare_op=ALU.not_equal, fill=1.0,
                                    base=0, pattern=[[-1, P]], channel_multiplier=1).then_inc(ident_ready, 1)
            nc.gpsimd.memset(neg_half[:, :], -0.5).then_inc(ident_zero, 1)
            pool.wait_ge(ident_zero, 2)

            def rstd_tokens(n, parity):
                pool.wait_ge(m_var, n + 1)
                nc.gpsimd.tensor_tensor(out=rstd[parity][:, :], in0=rstd[parity][:, :], in1=neg_half[:, :],
                                        op=ALU.pow).then_inc(m_rstd, 1)

            def split_x1(t, parity):
                pool.wait_ge(xT_full, 2 * t + 6)
                hold(pool, pool_held)
                hi, lo = (h[:, :, bass.ds(t * S, S)] for h in x1T)
                nc.gpsimd.tensor_tensor(out=lo, in0=x1Tf[parity][:, :, :], in1=f32(hi), op=ALU.subtract).then_inc(xT_split, 1)

            rstd_tokens(0, 0)
            with pool.Fori(0, B // 2 - 1) as pair:
                for parity in range(2):
                    t = pool.snap(pair * 2 + parity)
                    rstd_tokens(t + 1, 1 - parity)
                    split_x1(t, parity)
            rstd_tokens(B - 1, (B - 1) % 2)
            for t in (B - 2, B - 1):
                split_x1(t, t % 2)

            def split_chunk(chunk, j):
                pool.wait_ge(hid_relu, chunk + j + 1 + RING)
                nc.gpsimd.tensor_tensor(out=hid[1][:, j % RING, :], in0=act32[:, j % FULL, :], in1=f32(hid[0][:, j % RING, :]),
                                        op=ALU.subtract).then_inc(hid_split, 1)

            with pool.Fori(0, (E - 1) * B + 1) as tile:
                chunk = pool.snap(tile * FC)
                for j in range(FC):
                    split_chunk(chunk, j)

            def last_tile(t, parity):
                chunk = t * FC + (E - 1) * B * FC
                for j in range(FC):
                    if j == POW_AT:
                        rstd_tokens(t + B - 1, 1 - parity)
                    split_chunk(chunk, j)

            with pool.Fori(0, B // 2 - 1) as pair:
                for parity in (1, 0):
                    last_tile(pool.snap(pair * 2 + 2 - parity), parity)
            last_tile(B - 1, 1)
            rstd_tokens(2 * B - 1, 1)

        @block.scalar
        def _(act):
            act.sem_inc(hid_relu, RING)
            act.sem_inc(xT_full, 2 * DC)
            act.sem_inc(x1_kept, 2)
            act.wait_ge(b1_psum, 1)
            nc.scalar.activation(b1_cols[:, :], b1_bank[:, 0:E * FC], ACT.Copy).then_inc(b1_ready, 1)
            act.wait_ge(raw_loaded, 2 * DMA)
            for w, raw in ((w1[0], raw1), (w2[0], raw2)):
                nc.scalar.activation(w[0], raw[:, :], ACT.Copy).then_inc(w_high, 1)
            with act.Fori(0, B // 2) as pair:
                for parity in range(2):
                    t = act.snap(pair * 2 + parity)
                    act.wait_ge(x1_ready, t + 1)
                    hold(act, act_held)
                    nc.scalar.activation(acc[:, bass.ds(t * TB, TB), :], x1[parity][:, :, :], ACT.Copy).then_inc(x1_kept, 1)
                    act.wait_ge(logits, t + 1)
                    act.wait_ge(xT_split, t + 1)
                    act.wait_ge(xT_psum, t + 3)
                    hold(act, act_held)
                    for c in range(DC):
                        nc.scalar.activation(x1Tf[parity][:, c, :], xT_bank(parity, c), ACT.Copy)
                        nc.scalar.activation(x1T[0][:, c, bass.ds(t * S, S)], xT_bank(parity, c), ACT.Copy).then_inc(xT_full, 1)
            act.wait_ge(logits, B + 2)
            act.wait_ge(xT_split, B + 2)
            hold(act, act_held)
            with act.Fori(0, E) as e:
                act.wait_ge(hid_relu, e * (B * FC) + RING)
                hold(act, act_held)
                nc.scalar.activation(b1_e[:, :], b1_cols[:, bass.ds(e * FC, FC)], ACT.Copy).then_inc(b1_ready, 1)
                act.wait_ge(b1_ready, e + 2)
                hold(act, act_held)
                with act.Fori(0, B) as t:
                    chunk = act.snap((e * B + t) * FC)
                    for j in range(FC):
                        bias = b1_e[:, j:j + 1]
                        act.wait_ge(hid_psum, chunk + j + 1)
                        act.wait_ge(hid_used, chunk + j + 1)
                        nc.scalar.activation(hid[0][:, j % RING, :], hid_bank(j), ACT.Relu, bias=bias)
                        act.wait_ge(hid_split, chunk + j + 1)
                        nc.scalar.activation(act32[:, j % FULL, :], hid_bank(j), ACT.Relu, bias=bias).then_inc(hid_relu, 1)

        @block.vector
        def _(dve):
            dve.sem_inc(b2_added, 2 * OUTS)
            dve.sem_inc(out_added, 1)
            count = [0]

            def landed(ins, base=0):
                count[0] += 1
                ins.then_inc(dve_done, 1)
                dve.wait_ge(dve_done, base + count[0])

            def moments(src, t, parity, base):
                for k in range(TB):
                    ins = nc.vector.bn_stats(stat[parity][:, k, :], src[:, bass.ds(t * TB + k, 1), :])
                landed(ins, base)
                hold(dve, dve_held)
                for k in range(TB):
                    ins = nc.vector.bn_aggr(mv[parity][:, k, :], stat[parity][:, k, :])
                landed(ins, base)
                nc.vector.tensor_scalar(rstd[parity][:, :], mv[parity][:, :, 1], EPS, None, ALU.add).then_inc(m_var, 1)

            def normalise(dst, src, t, parity, n, done):
                dve.wait_ge(m_rstd, n + 1)
                for k in range(TB):
                    ins = nc.vector.tensor_scalar(dst(k), src[:, bass.ds(t * TB + k, 1), :], mv[parity][:, k, 0:1],
                                                  rstd[parity][:, k:k + 1], ALU.subtract, ALU.mult)
                ins.then_inc(done, 1)

            TILE_CHAIN = 3

            def sum_moments(t, parity, loads):
                base = t * TILE_CHAIN
                count[0] = 0
                dve.wait_ge(xh_loaded[parity], loads * (2 * DMA))
                at = bass.ds(t * TB, TB)
                landed(nc.vector.tensor_tensor(out=xh[:, at, :], in0=acc[:, at, :], in1=xh[:, at, :], op=ALU.add), base)
                hold(dve, dve_held)
                moments(xh, t, parity, base)
                assert count[0] == TILE_CHAIN

            def normalise_x1(t, parity):
                dve.wait_ge(x1_kept, t + 1)
                dve.wait_ge(xT_psum, t + 1)
                normalise(lambda k: x1[parity][:, k:k + 1, :], xh, t, parity, t, x1_ready)

            sum_moments(0, 0, 1)
            with dve.Fori(0, B // 2 - 1) as pair:
                for parity in range(2):
                    t = dve.snap(pair * 2 + parity)
                    sum_moments(dve.snap(t + 1), 1 - parity, pair + 1 + parity)
                    normalise_x1(t, parity)
            sum_moments(B - 1, 1, B // 2)
            for t in (B - 2, B - 1):
                normalise_x1(t, t % 2)

            def split_weights(parity, n):
                dve.wait_ge(w_high, 2 * n + 2)
                for w, raw, done in ((w1, raw1, w1_split), (w2, raw2, w2_split)):
                    nc.vector.tensor_tensor(out=w[parity][1], in0=raw[:, :], in1=f32(w[parity][0]),
                                            op=ALU.subtract).then_inc(done, 1)

            split_weights(0, 0)

            def each(v):
                return v.unsqueeze(2).to_broadcast([P, NB, E])

            fixed = B * TILE_CHAIN
            count[0] = 0
            mx, lo, total, above, sign, step, tot = (ent_s[:, i, :] for i in range(7))
            scores, work = gates[:, :, :], ent_w
            SPAN = 1.0 - float(E) ** -0.5

            def rowsum_of_squares(ahead):
                landed(nc.vector.scalar_tensor_tensor(out=work, in0=scores, scalar=ahead, in1=each(lo), op0=ALU.subtract, op1=ALU.subtract), fixed)
                landed(nc.vector.scalar_tensor_tensor(out=work, in0=work, scalar=0.0, in1=work, op0=ALU.max, op1=ALU.mult), fixed)
                landed(nc.vector.tensor_reduce(out=total, in_=work, op=ALU.add, axis=AX.X), fixed)

            dve.wait_ge(logits, B + 2)
            landed(nc.vector.tensor_tensor(out=scores, in0=logit_bank[:, 0:NB * E].rearrange("p (n e) -> p n e", e=E),
                                           in1=br_bc[:, :].unsqueeze(1).to_broadcast([P, NB, E]), op=ALU.add), fixed)
            landed(nc.vector.tensor_scalar(scores, scores, 0.5, None, ALU.mult), fixed)
            landed(nc.vector.tensor_reduce(out=mx, in_=scores, op=ALU.max, axis=AX.X), fixed)
            landed(nc.vector.tensor_scalar(lo, mx, -1.0, None, ALU.add), fixed)
            rowsum_of_squares(0.0)
            nc.vector.tensor_scalar(above, total, 1.0, None, ALU.is_gt)
            landed(nc.vector.tensor_scalar(step, total, 1.0, None, ALU.is_lt), fixed)
            landed(nc.vector.tensor_tensor(out=sign, in0=above, in1=step, op=ALU.subtract), fixed)
            for n in range(1, NITER + 1):
                half = SPAN * 0.5 ** n
                rowsum_of_squares(half)
                if n < NITER:
                    landed(nc.vector.tensor_tensor(out=total, in0=total, in1=sign, op=ALU.mult), fixed)
                    landed(nc.vector.tensor_tensor(out=step, in0=total, in1=sign, op=ALU.is_ge), fixed)
                    landed(nc.vector.scalar_tensor_tensor(out=lo, in0=step, scalar=half, in1=lo, op0=ALU.mult, op1=ALU.add), fixed)
            landed(nc.vector.reciprocal(tot, total), fixed)
            landed(nc.vector.tensor_tensor(out=work, in0=work, in1=each(tot), op=ALU.mult), fixed)
            landed(nc.vector.scalar_tensor_tensor(out=scores, in0=work, scalar=THRESH, in1=work, op0=ALU.is_gt, op1=ALU.mult), fixed)
            dve.wait_ge(x1_kept, B + 2)

            def add_tile(e, t, tiles, pair_e, parity_e, parity_t):
                dve.wait_ge(hid_used, (tiles + 1) * FC + RING)
                dve.wait_ge(b2_loaded[parity_e], (pair_e + 1) * DMA)
                dve.wait_ge(out_added, tiles + 1)
                for half in range(2):
                    nc.vector.tensor_tensor(out=tile_out[:, 2 * half:2 * half + 2, :],
                                            in0=out_half(parity_t, half).rearrange("p (k d) -> p k d", d=D),
                                            in1=b2_bc[:, parity_e, :].unsqueeze(1).to_broadcast([P, 2, D]),
                                            op=ALU.add).then_inc(b2_added, 1)
                dve.wait_ge(b2_added, 2 * (tiles + 1) + 2 * OUTS)
                for k in range(TB):
                    at = acc[:, bass.ds(t * TB + k, 1), :].rearrange("p o d -> p (o d)")
                    gate = gates[:, bass.ds(t * TB + k, 1), bass.ds(e, 1)].rearrange("p o d -> p (o d)")
                    ins = nc.vector.scalar_tensor_tensor(out=at, in0=tile_out[:, k, :], scalar=gate,
                                                         in1=at, op0=ALU.mult, op1=ALU.add)
                ins.then_inc(out_added, 1)

            def next_weights(e, parity):
                dve.wait_ge(raw_loaded, (e + 1) * (2 * DMA))
                for w, raw in ((w1, raw1), (w2, raw2)):
                    nc.vector.tensor_copy(w[parity][0], raw[:, :]).then_inc(w_high, 1)
                split_weights(parity, e)

            def expert(pair_e, parity_e, e, last):
                if not last:
                    next_weights(e + 1, 1 - parity_e)
                with dve.Fori(0, B // 2) as pair:
                    for parity_t in range(2):
                        t = dve.snap(pair * 2 + parity_t)
                        tiles = dve.snap(e * B + t)
                        add_tile(e, t, tiles, pair_e, parity_e, parity_t)
                        if last:
                            dve.wait_ge(out_added, tiles + 2)
                            hold(dve, dve_held)
                            count[0] = 0
                            moments(acc, t, parity_t, t * 2 + done)
                            normalise(lambda k: acc[:, bass.ds(t * TB + k, 1), :], acc, t, parity_t, t + B, y_ready)

            done = fixed + count[0]
            with dve.Fori(0, E // 2 - 1) as pair_e:
                for parity_e in range(2):
                    expert(pair_e, parity_e, dve.snap(pair_e * 2 + parity_e), False)
            expert(E // 2 - 1, 0, E - 2, False)
            expert(E // 2 - 1, 1, E - 1, True)

        @block.tensor
        def _(pe):
            def mm3(out, w, x, first, last):
                nc.tensor.matmul(out, w[0], x[0], start=first, stop=False, skip_group_check=True)
                nc.tensor.matmul(out, w[0], x[1], start=False, stop=False, skip_group_check=True)
                return nc.tensor.matmul(out, w[1], x[0], start=False, stop=last, skip_group_check=True)

            def cols(n):
                return slice(n * P, (n + 1) * P)

            pe.sem_inc(hid_used, RING)
            pe.sem_inc(logits, 2)
            pe.sem_inc(xT_psum, 2)
            pe.wait_ge(ident_ready, 1)
            pe.wait_ge(consts_loaded, 3 * DMA)
            nc.tensor.transpose(b1_bank[:, 0:E * FC], b1_rows[:, :], ident[0:E * FC, 0:E * FC]).then_inc(b1_psum, 1)

            def transpose_x1(t, parity):
                pe.wait_ge(x1_ready, t + 1)
                pe.wait_ge(xT_full, 2 * t + 2)
                for c in range(DC):
                    for k in range(TB):
                        ins = nc.tensor.transpose(xT_bank(parity, c)[:, cols(k)], x1[parity][:, k, cols(c)], ident[:, :])
                ins.then_inc(xT_psum, 1)

            def route(t, parity):
                pe.wait_ge(xT_full, 2 * t + 6)
                for k in range(TB):
                    for c in range(DC):
                        ins = nc.tensor.matmul(logit_bank[:, bass.ds((t * TB + k) * E, E)], x1Tf[parity][:, c, cols(k)], wr[:, c, :],
                                               start=c == 0, stop=c == DC - 1)
                ins.then_inc(logits, 1)

            transpose_x1(0, 0)
            with pe.Fori(0, B // 2 - 1) as pair:
                for parity in range(2):
                    t = pe.snap(pair * 2 + parity)
                    transpose_x1(t + 1, 1 - parity)
                    route(t, parity)
            transpose_x1(B - 1, 1)
            route(B - 2, 0)
            route(B - 1, 1)
            pe.wait_ge(xT_split, B + 2)
            pe.wait_ge(b1_ready, 1)
            pe.wait_ge(w1_split, 1)
            pe.wait_ge(w2_split, 1)
            pe.wait_ge(dve_done, B * 3 + 1)

            def up(w, t, chunk, j):
                pe.wait_ge(hid_relu, chunk + j + 1)
                for c in range(DC):
                    ins = mm3(hid_bank(j), [h[:, c * F + j * P:c * F + (j + 1) * P] for h in w],
                              [h[:, c, bass.ds(t * S, S)] for h in x1T], c == 0, c == DC - 1)
                ins.then_inc(hid_psum, 1)

            def down(w, chunk, j, parity):
                pe.wait_ge(hid_split, chunk + j + 1 + FULL)
                r = j % RING
                for k in range(TB):
                    ins = mm3(out_bank(parity, k), [h[:, r, cols(k)] for h in hid],
                              [h[:, j * D:(j + 1) * D] for h in w], j == 0 and k % 2 == 0, j == FC - 1)
                ins.then_inc(hid_used, 1)

            def tile(e, parity_e, t, tiles, parity_t, following):
                chunk = pe.snap(tiles * FC)
                for j in range(FC):
                    if j + AHEAD < FC:
                        up(w1[parity_e], t, chunk, j + AHEAD)
                    elif following:
                        w, t_next = following
                        if w is not w1[parity_e]:
                            pe.wait_ge(w1_split, e + 2)
                            pe.wait_ge(w2_split, e + 2)
                        up(w, t_next, pe.snap(chunk + FC), j + AHEAD - FC)
                    if j == 0:
                        pe.wait_ge(b2_added, 2 * tiles + 2)
                    down(w2[parity_e], chunk, j, parity_t)

            def expert(e, parity_e, last):
                with pe.Fori(0, B // 2 - 1) as pair_t:
                    for parity_t in range(2):
                        t = pe.snap(pair_t * 2 + parity_t)
                        tile(e, parity_e, t, pe.snap(e * B + t), parity_t, (w1[parity_e], t + 1))
                tile(e, parity_e, B - 2, pe.snap(e * B + B - 2), 0, (w1[parity_e], B - 1))
                tile(e, parity_e, B - 1, pe.snap(e * B + B - 1), 1, None if last else (w1[1 - parity_e], 0))

            for j in range(AHEAD):
                up(w1[0], 0, 0, j)
            with pe.Fori(0, E // 2 - 1) as pair_e:
                for parity_e in range(2):
                    expert(pe.snap(pair_e * 2 + parity_e), parity_e, False)
            expert(E - 2, 0, False)
            expert(E - 1, 1, True)


def build(nc, x, Wkqv, Wm1, bm1, Wm2, bm2, gn_g, gn_b, Wf1, bf1, Wf2, bf2, ln_g, ln_b,
          Wr, br, W1, b1, W2, b2, score_floor, out):
    B, S, D = x.shape
    L = Wkqv.shape[0]
    pairs = B // 2
    h_store = nc.dram_tensor("h_store", ((L + 1) * pairs, 2, S, D), F32, kind="Internal").ap()
    folded = nc.dram_tensor("folded", (L, P, 6 * D), F32, kind="Internal").ap()
    retention_layers(nc, x, Wkqv, Wm1, bm1, Wm2, bm2, gn_g, gn_b, Wf1, bf1, Wf2, bf2, ln_g, ln_b,
                     score_floor, h_store, folded)
    expert_mixture(nc, x, h_store[L * pairs:, :, :, :], Wr, br, W1, b1, W2, b2, out)


_INS = ["L0_attn_x", "L0_attn_Wkqv", "L0_attn_Wm1", "L0_attn_bm1", "L0_attn_Wm2", "L0_attn_bm2",
        "L0_attn_gn_g", "L0_attn_gn_b", "L0_attn_Wf1", "L0_attn_bf1", "L0_attn_Wf2", "L0_attn_bf2",
        "L0_attn_ln_g", "L0_attn_ln_b", "L0_ffn_Wr", "L0_ffn_br", "L0_ffn_W1", "L0_ffn_b1", "L0_ffn_W2", "L0_ffn_b2"]


def kernel(**inputs):
    import numpy as np
    import concourse.bacc as bacc
    from concourse.bass_utils import run_bass_kernel_spmd

    arrays = {f"in_{name}": np.ascontiguousarray(inputs[name]) for name in _INS}
    B, S, D = arrays["in_L0_attn_x"].shape
    row = np.float32(np.sqrt(D)) * (1 + np.sqrt(np.arange(S, dtype=np.float32)))
    arrays["in_score_floor"] = np.ascontiguousarray(np.broadcast_to(row.astype(np.float32), (P, S)))
    nc = bacc.Bacc("TRN2", target_bir_lowering=False, num_devices=1)
    args = [nc.dram_tensor(n, a.shape, mybir.dt.from_np(a.dtype), kind="ExternalInput").ap() for n, a in arrays.items()]
    args.append(nc.dram_tensor("out", (B, S, D), F32, kind="ExternalOutput").ap())
    build(nc, *args)
    r = run_bass_kernel_spmd(nc, [arrays], core_ids=[0])
    return r.results[0]["out"]
```

```python
from contextlib import ExitStack

import concourse.bass as bass
from concourse import mybir

F32 = mybir.dt.float32
F32R = mybir.dt.float32r
ALU = mybir.AluOpType
ACT = mybir.ActivationFunctionType
AX = mybir.AxisListType

P = 128
EPS = 1e-5
NITER = 25
THRESH = 1e-9
DMA = 16


def f32(ap):
    return ap.bitcast(F32)


def hold(eng, held):
    eng.sem_inc(held, 1)


class Step:

    def __init__(self, it, base, layer):
        self.it, self.base, self.layer = it, base, layer


def retention_layers(nc, x, Wkqv, Wm1, bm1, Wm2, bm2, gn_g, gn_b, Wf1, bf1, Wf2, bf2,
                     ln_g, ln_b, score_floor, h_store, folded, h_stored, dve_held, pool_held):
    B, S, D = x.shape
    L = Wkqv.shape[0]
    DC = D // P
    TB = S // P
    MC = Wm1.shape[2] // P
    FC = Wf1.shape[2] // P
    SLOTS = 2
    A_, B_ = 0, 1
    PAIRS = B // SLOTS
    STEPS = L * PAIRS
    U = 4
    LC = 2 * MC + 4 * DC
    assert (DC, TB, MC, FC, U) == (2, 4, 4, 4, 4)
    LO = [0, P, 2 * P, 2 * P]
    SPANS, end = {}, 0
    for name, width in (("qk", DC * D), ("vm", DC * MC * P), ("m2", DC * D), ("f1", DC * FC * P), ("f2", FC * D)):
        SPANS[name] = slice(end, end + width)
        end += width
    FOLD = SPANS["vm"].stop
    WEIGHTS = end

    x_v = x.rearrange("(i s) (k p) d -> i s p k d", s=SLOTS, p=P)
    h_v = h_store.rearrange("i s (k p) d -> i s p k d", p=P)

    with ExitStack() as ctx:
        def sb(name, shape, dt=F32):
            return ctx.enter_context(nc.sbuf_tensor(name, shape, dt))

        def sem(name):
            return ctx.enter_context(nc.semaphore(name))

        def sems(name):
            return [sem(f"{name}{s}") for s in range(SLOTS)]

        ident = sb("ident", [P, P])
        ones_r = sb("ones_r", [P, P], F32R)
        mean_w = sb("mean_w", [P, P])
        neg_half = sb("neg_half", [P, TB])
        floor = sb("floor", [P, S])
        const_rows = sb("const_rows", [L * LC, P])
        const_cols = sb("const_cols", [P, L * LC])
        raw = sb("raw", [P, WEIGHTS])
        w_full = [sb(f"w_{n}", [P, WEIGHTS], F32R) for n in ("hi", "lo")]

        def weight(name, chunks):
            return [w[:, SPANS[name]].rearrange("p (c n) -> p c n", c=chunks) for w in w_full]

        def slot_tiles(name, shape, dt=F32):
            return [sb(f"{name}{s}", shape, dt) for s in range(SLOTS)]

        def split_tiles(name, shape):
            return [[sb(f"{name}_{n}{s}", shape, F32R) for n in ("hi", "lo")] for s in range(SLOTS)]

        lc = slot_tiles("lc", [P, LC])
        lnv = slot_tiles("lnv", [P, 2 * D])
        lc_bm1, lc_bm2, lc_gg = ([c[:, a:b] for c in lc] for a, b in ((0, 4), (4, 6), (6, 8)))
        lc_gb, lc_bf1, lc_bf2 = ([c[:, a:b] for c in lc] for a, b in ((8, 10), (10, 14), (14, 16)))
        h_in = slot_tiles("h_in", [P, TB, D])
        h_out = slot_tiles("h_out", [P, TB, D])
        h_sp = split_tiles("h", [P, TB, D])
        hT_sp = split_tiles("hT", [P, DC, S])
        tu_sp = split_tiles("tu", [P, DC, S])
        ry_sp = split_tiles("ry", [P, DC, S])
        pf_sp = split_tiles("pf", [P, FC, S])
        tmp = slot_tiles("tmp", [P, 4, S])
        y = slot_tiles("y", [P, DC, S])
        z = slot_tiles("z", [P, TB, D])
        inv = [t[:, 0, :] for t in y]
        warm = sb("warm", [P, 1])
        gstat = slot_tiles("gstat", [P, DC, 6])
        gmv = slot_tiles("gmv", [P, DC, 2])
        gin = slot_tiles("gin", [P, 2 * DC])
        gsm = slot_tiles("gsm", [P, 12])
        zstat = slot_tiles("zstat", [P, TB, 6])
        zmv = slot_tiles("zmv", [P, TB, 2])
        zr = slot_tiles("zr", [P, 2, TB])

        raw_kqv = [y[B_][:, 0, :], y[B_][:, 1, :], z[B_][:, 0:DC, :].rearrange("p c d -> p (c d)")]
        raw_m1 = h_out[B_][:, :, :].rearrange("p k d -> p (k d)").rearrange("p (c n) -> p c n", c=DC)
        w_t = tmp[B_][:, 0:3, :]

        ps = ctx.enter_context(nc.psum_tensor("ps", [P, 8, 512], F32))

        def bank(s, r):
            return ps[:, 4 * s + r, :]

        GATE, VALUE, OUT, MOMENTS = (1, 3), (2, 0), (1, 2), 3

        def score_bank(s, b):
            return bank(s, (2 + b) % 4)

        consts_loaded = sem("consts_loaded")
        ident_ready, pool_consts = sem("ident_ready"), sem("pool_consts")
        const_psum, const_ready = sem("const_psum"), sem("const_ready")
        qkv_loaded, raw_loaded = sem("qkv_loaded"), sem("raw_loaded")
        wt_psum, wt_ready = sem("wt_psum"), sem("wt_ready")
        fold_psum, fold_out, fold_stored = sem("fold_psum"), sem("fold_out"), sem("fold_stored")
        w_hi, w_lo = ({m: sem(f"{m}_{n}") for m in SPANS} for n in ("hi", "lo"))
        lc_ready, lnv_loaded = sems("lc_ready"), sems("lnv_loaded")
        h_loaded = sems("h_loaded")
        h_hi, h_lo = sems("h_hi"), sems("h_lo")
        hT_psum, hT_hi, hT_lo = sems("hT_psum"), sems("hT_hi"), sems("hT_lo")
        t_psum, t_hi, t_lo = sems("t_psum"), sems("t_hi"), sems("t_lo")
        s_psum, p_hi, p_lo, p_masked = sems("s_psum"), sems("p_hi"), sems("p_lo"), sems("p_masked")
        rowsum_psum, r_psum = sems("rowsum_psum"), sems("r_psum")
        r_hi, r_lo = sems("r_hi"), sems("r_lo")
        m_psum, gate_scaled, value_scaled = sems("m_psum"), sems("gate_scaled"), sems("value_scaled")
        gate_ready, u_ready = sems("gate_ready"), sems("u_ready")
        u_hi, u_lo = sems("u_hi"), sems("u_lo")
        m2_psum, gn_in, gn_psum = sems("m2_psum"), sems("gn_in"), sems("gn_psum")
        y_ready, y_hi, y_lo = sems("y_ready"), sems("y_hi"), sems("y_lo")
        f1_psum, f_ready, f_hi, f_lo = sems("f1_psum"), sems("f_ready"), sems("f_hi"), sems("f_lo")
        f2_psum, z_ready = sems("f2_psum"), sems("z_ready")
        zT_psum, z_kept, h_new = sems("zT_psum"), sems("z_kept"), sems("h_new")
        g_var, g_rstd, z_var, z_rstd = sems("g_var"), sems("g_rstd"), sems("z_var"), sems("z_rstd")
        z_normed, z_gained = sems("z_normed"), sems("z_gained")
        scale_done, gn_done, ln_done = sems("scale_done"), sems("gn_done"), sems("ln_done")

        block = ctx.enter_context(nc.Block())

        def run_steps(eng, first, body, tail):
            def at(it, layer):
                if isinstance(it, int):
                    return Step(it, it * U, layer)
                return Step(it, eng.snap(it * U), layer)

            def within(l):
                with eng.Fori(1, PAIRS) as p:
                    it = eng.snap(l * PAIRS + p)
                    body(at(it, l), at(eng.snap(it - 1), l), False)

            first(at(0, 0))
            within(0)
            with eng.Fori(1, L) as l:
                it = eng.snap(l * PAIRS)
                body(at(it, l), at(eng.snap(it - 1), eng.snap(l - 1)), True)
                within(l)
            tail(at(STEPS - 1, L - 1))

        def layernorm_out(eng, ops, s, at):
            gain, bias = (lnv[s][:, n * D:(n + 1) * D].unsqueeze(1).to_broadcast([P, TB, D]) for n in range(2))
            eng.wait_ge(lnv_loaded[s], at.layer * (2 * DMA) + 2 * DMA)
            eng.wait_ge(z_normed[s], at.base + U)
            ops.tensor_tensor(out=z[s][:, :, :], in0=z[s][:, :, :], in1=gain, op=ALU.mult).then_inc(z_gained[s], U)
            eng.wait_ge(z_gained[s], at.base + U)
            eng.wait_ge(h_stored[s], at.it * DMA + DMA)
            ops.tensor_tensor(out=h_out[s][:, :, :], in0=z[s][:, :, :], in1=bias, op=ALU.add).then_inc(h_new[s], U)

        @block.sync
        def _(sp):
            def chunks(w):
                return w.rearrange("(c p) n -> p c n", p=P)

            def load_fold_operands(l):
                if l:
                    sp.wait_ge(fold_psum, 3 * l)
                for i, dst in enumerate(raw_kqv):
                    sp.dma_start(dst.rearrange("p (c n) -> p c n", c=DC),
                                 chunks(Wkqv[l][:, i * D:(i + 1) * D])).then_inc(qkv_loaded, DMA)
                sp.dma_start(raw_m1, chunks(Wm1[l])).then_inc(qkv_loaded, DMA)

            def store_fold(l):
                sp.wait_ge(fold_out, 3 * l + 3)
                sp.dma_start(folded[l], raw[:, 0:FOLD]).then_inc(fold_stored, DMA)

            def load_plain_weights(l):
                for name, w in (("m2", Wm2), ("f1", Wf1), ("f2", Wf2)):
                    c = w.shape[1] // P
                    sp.dma_start(raw[:, SPANS[name]].rearrange("p (c n) -> p c n", c=c), chunks(w[l])).then_inc(raw_loaded, DMA)

            def next_weights(l):
                for name in SPANS:
                    sp.wait_ge(w_lo[name], l)
                sp.dma_start(raw[:, 0:FOLD], folded[l]).then_inc(raw_loaded, DMA)
                load_plain_weights(l)

            def load_lnv(s, l):
                sp.dma_start(lnv[s][:, 0:D], ln_g[bass.ds(l, 1), :].to_broadcast([P, D])).then_inc(lnv_loaded[s], DMA)
                sp.dma_start(lnv[s][:, D:2 * D], ln_b[bass.ds(l, 1), :].to_broadcast([P, D])).then_inc(lnv_loaded[s], DMA)

            def load_x(s, it):
                if not (isinstance(it, int) and it == 0):
                    sp.wait_ge(hT_psum[s], it * U)
                    sp.wait_ge(h_lo[s], it * U)
                sp.dma_start(h_in[s][:, :, :], x_v[it, s]).then_inc(h_loaded[s], DMA)

            def load_h(s, it):
                sp.wait_ge(hT_psum[s], it * U)
                sp.wait_ge(h_lo[s], it * U)
                sp.wait_ge(h_stored[s], (it - PAIRS + 2) * DMA)
                sp.dma_start(h_in[s][:, :, :], h_v[it, s]).then_inc(h_loaded[s], DMA)

            def store_h(s, it):
                sp.wait_ge(h_new[s], it * U + 2 * U)
                sp.dma_start(h_v[it + PAIRS, s], h_out[s][:, :, :]).then_inc(h_stored[s], DMA)

            def step(it, load, seam=None):
                for s in range(SLOTS):
                    if load:
                        load(s, it + 1)
                    store_h(s, it - 1)
                    if seam is not None:
                        load_lnv(s, seam)

            for s in range(SLOTS):
                sp.sem_inc(h_stored[s], DMA)
            load_fold_operands(0)
            load_x(A_, 0)
            load_plain_weights(0)
            sp.dma_start(floor[:, :], score_floor).then_inc(consts_loaded, DMA)
            load_x(B_, 0)
            for s in range(SLOTS):
                load_lnv(s, 0)
            for l in range(1, L):
                load_fold_operands(l)
                store_fold(l)
                if l == 1:
                    load_x(A_, 1)
            sp.wait_ge(fold_stored, (L - 1) * DMA)
            next_weights(1)
            load_x(B_, 1)
            with sp.Fori(1, PAIRS - 1) as it:
                step(it, load_x)
            step(PAIRS - 1, load_h)
            with sp.Fori(1, L - 1) as l:
                step(sp.snap(l * PAIRS), load_h, l)
                next_weights(sp.snap(l + 1))
                with sp.Fori(1, PAIRS) as p:
                    step(sp.snap(l * PAIRS + p), load_h)
            step((L - 1) * PAIRS, load_h, L - 1)
            with sp.Fori((L - 1) * PAIRS + 1, STEPS - 1) as it:
                step(it, load_h)
            step(STEPS - 1, None)
            for s in range(SLOTS):
                store_h(s, STEPS - 1)

        @block.gpsimd
        def _(pool):
            for s in range(SLOTS):
                pool.sem_inc(h_new[s], U)
            nc.gpsimd.memset(ident[:, :], 0.0).then_inc(pool_consts, 1)
            pool.wait_ge(pool_consts, 1)
            nc.gpsimd.affine_select(out=ident[:, :], in_=ident[:, :], compare_op=ALU.not_equal, fill=1.0,
                                    base=0, pattern=[[-1, P]], channel_multiplier=1).then_inc(ident_ready, 1)
            nc.gpsimd.memset(f32(ones_r[:, :]), 1.0).then_inc(pool_consts, 1)
            nc.gpsimd.memset(neg_half[:, :], -0.5).then_inc(pool_consts, 1)
            nc.gpsimd.memset(mean_w[:, :], 1.0 / (P * DC)).then_inc(pool_consts, 1)
            pool.wait_ge(pool_consts, 4)

            def low_half(lo, full, hi, done, n):
                nc.gpsimd.tensor_tensor(out=lo, in0=full, in1=f32(hi), op=ALU.subtract).then_inc(done, n)

            def split_weight(name, l):
                pool.wait_ge(w_hi[name], l + 1)
                low_half(w_full[1][:, SPANS[name]], raw[:, SPANS[name]], w_full[0][:, SPANS[name]], w_lo[name], 1)

            def split_h(s, at):
                pool.wait_ge(h_hi[s], at.base + U)
                low_half(h_sp[s][1][:, :, :], h_in[s][:, :, :], h_sp[s][0][:, :, :], h_lo[s], U)

            def mask_scores(s, at, blocks):
                for b in blocks:
                    pool.wait_ge(p_lo[s], at.base + b + 1)
                    hold(pool, pool_held)
                    for half in range(2):
                        part = pf_sp[s][half][:, b, LO[b]:(b + 1) * P]
                        ins = nc.gpsimd.affine_select(
                            out=part, in_=f32(part), compare_op=ALU.is_ge, fill=0.0, base=LO[b] - b * P,
                            pattern=[[1, (b + 1) * P - LO[b]]], channel_multiplier=-1)
                    ins.then_inc(p_masked[s], 1)

            def rstd_group(s, at):
                pool.wait_ge(g_var[s], at.base + U)
                nc.gpsimd.tensor_tensor(out=gsm[s][:, 5:6], in0=gsm[s][:, 5:6], in1=neg_half[:, 0:1], op=ALU.pow).then_inc(g_rstd[s], U)

            def layernorm_rstd(s, at):
                pool.wait_ge(z_var[s], at.base + U)
                nc.gpsimd.tensor_tensor(out=zr[s][:, 0, :], in0=zr[s][:, 0, :], in1=neg_half[:, :], op=ALU.pow).then_inc(z_rstd[s], 2)
                pool.wait_ge(z_rstd[s], at.base + 2)
                nc.gpsimd.tensor_tensor(out=zr[s][:, 1, :], in0=zr[s][:, 0, :], in1=zr[s][:, 1, :], op=ALU.mult).then_inc(z_rstd[s], 2)

            def split_f(s, at):
                for c in range(FC):
                    pool.wait_ge(f_hi[s], at.base + c + 1)
                    low_half(pf_sp[s][1][:, c, :], tmp[s][:, c, :], pf_sp[s][0][:, c, :], f_lo[s], 1)

            def body(now, before, seam):
                if seam:
                    split_weight("qk", now.layer)
                split_h(A_, now)
                if seam or not before:
                    split_weight("vm", now.layer)
                if not before:
                    split_weight("m2", 0)
                mask_scores(A_, now, (0,))
                if before:
                    rstd_group(B_, before)
                mask_scores(A_, now, (1, 2, 3))
                if seam:
                    split_weight("m2", now.layer)
                if before:
                    split_f(B_, before)
                    layernorm_rstd(A_, before)
                else:
                    split_weight("f1", 0)
                    split_weight("f2", 0)
                split_h(B_, now)
                if seam:
                    split_weight("f1", now.layer)
                rstd_group(A_, now)
                if seam:
                    split_weight("f2", now.layer)
                mask_scores(B_, now, range(TB))
                split_f(A_, now)
                if before:
                    layernorm_rstd(B_, before)
                    layernorm_out(pool, nc.gpsimd, A_, before)
                    layernorm_out(pool, nc.gpsimd, B_, before)

            def first(now):
                split_weight("qk", 0)
                body(now, None, False)

            def tail(last):
                rstd_group(B_, last)
                split_f(B_, last)
                layernorm_rstd(A_, last)
                layernorm_out(pool, nc.gpsimd, A_, last)
                layernorm_rstd(B_, last)

            run_steps(pool, first, body, tail)

        @block.scalar
        def _(act):
            for s in range(SLOTS):
                act.sem_inc(z_kept[s], U)
            row = 0
            for c in (bm1, bm2, gn_g, gn_b, bf1, bf2):
                n = L * c.shape[1] // P
                act.dma_start(const_rows[row:row + n, :], c.rearrange("l (n p) -> (l n) p", p=P)).then_inc(consts_loaded, DMA)
                row += n
            act.wait_ge(pool_consts, 4)

            def order_constants():
                act.wait_ge(const_psum, 1)
                row = at = 0
                for c in (bm1, bm2, gn_g, gn_b, bf1, bf2):
                    n = c.shape[1] // P
                    ins = nc.scalar.activation(const_cols[:, :].rearrange("p (l c) -> p l c", l=L)[:, :, at:at + n],
                                               bank(A_, 0)[:, row:row + L * n].rearrange("p (l c) -> p l c", l=L), ACT.Copy)
                    row += L * n
                    at += n
                ins.then_inc(const_ready, 1)

            def empty_fold(l):
                for i in range(3):
                    act.wait_ge(wt_psum, 3 * l + i + 1)
                    nc.scalar.activation(w_t[:, i, :], bank(B_, i), ACT.Copy).then_inc(wt_ready, 1)
                if l == 1:
                    act.wait_ge(w_lo["qk"], 1)
                    act.wait_ge(w_lo["vm"], 1)
                elif l > 1:
                    act.wait_ge(fold_stored, (l - 1) * DMA)
                for i, r in enumerate((3, 0, 1)):
                    act.wait_ge(fold_psum, 3 * l + i + 1)
                    nc.scalar.activation(raw[:, i * S:(i + 1) * S], bank(B_, r), ACT.Copy).then_inc(fold_out, 1)

            def high_weight(name, l):
                nc.scalar.activation(w_full[0][:, SPANS[name]], raw[:, SPANS[name]], ACT.Copy).then_inc(w_hi[name], 1)

            def next_high_weight(name, l, used, at):
                act.wait_ge(used, at.base + U)
                act.wait_ge(raw_loaded, l * (4 * DMA) + 3 * DMA)
                high_weight(name, l)

            def load_table(func):
                nc.scalar.activation(warm[:, :], neg_half[:, 0:1], func)

            def high_hT(s, at):
                for c in range(DC):
                    act.wait_ge(hT_psum[s], at.base + 2 * c + 2)
                    nc.scalar.activation(hT_sp[s][0][:, c, :], bank(s, 2 + c), ACT.Copy).then_inc(hT_hi[s], 2)

            def high_h(s, at):
                act.wait_ge(h_loaded[s], at.it * DMA + DMA)
                nc.scalar.activation(h_sp[s][0][:, :, :], h_in[s][:, :, :], ACT.Copy).then_inc(h_hi[s], U)

            def high_t(s, at):
                for c in range(DC):
                    act.wait_ge(t_psum[s], at.base + 2 * c + 2)
                    nc.scalar.activation(tu_sp[s][0][:, c, :], bank(s, 2 + c), ACT.Copy).then_inc(t_hi[s], 2)

            def high_p(s, at, blocks):
                for b in blocks:
                    act.wait_ge(s_psum[s], at.base + b + 1)
                    nc.scalar.activation(pf_sp[s][0][:, b, LO[b]:S], score_bank(s, b)[:, LO[b]:S], ACT.Copy).then_inc(p_hi[s], 1)

            def high_r(s, at):
                for c in range(DC):
                    act.wait_ge(r_psum[s], at.base + 2 * c + 2)
                    nc.scalar.activation(ry_sp[s][0][:, c, :], bank(s, 2 + c), ACT.Copy).then_inc(r_hi[s], 2)

            def gate(s, at, c):
                act.wait_ge(lc_ready[s], at.layer + 1)
                act.wait_ge(gate_scaled[s], at.base + 2 * c + 2)
                nc.scalar.activation(tmp[s][:, 2 + c, :], tmp[s][:, 2 + c, :], ACT.Silu,
                                     bias=lc_bm1[s][:, DC + c:DC + c + 1]).then_inc(gate_ready[s], 2)

            def high_u(s, at, c):
                act.wait_ge(u_ready[s], at.base + 2 * c + 2)
                nc.scalar.activation(tu_sp[s][0][:, c, :], tmp[s][:, c, :], ACT.Copy).then_inc(u_hi[s], 2)

            def high_y(s, at, c):
                act.wait_ge(y_ready[s], at.base + 2 * c + 2)
                nc.scalar.activation(ry_sp[s][0][:, c, :], y[s][:, c, :], ACT.Copy).then_inc(y_hi[s], 2)

            def gelu(s, at, c):
                act.wait_ge(f1_psum[s], at.base + c + 1)
                nc.scalar.activation(tmp[s][:, c, :], bank(s, c), ACT.Gelu, bias=lc_bf1[s][:, c:c + 1]).then_inc(f_ready[s], 1)

            def high_f(s, at, c):
                act.wait_ge(f_ready[s], at.base + c + 1)
                nc.scalar.activation(pf_sp[s][0][:, c, :], tmp[s][:, c, :], ACT.Copy).then_inc(f_hi[s], 1)

            def hidden(s, at):
                gelu(s, at, 0)
                for c in range(1, FC):
                    gelu(s, at, c)
                    high_f(s, at, c - 1)

            def keep_z(s, at):
                act.wait_ge(h_new[s], at.base + U)
                for i in range(2):
                    act.wait_ge(zT_psum[s], at.base + 2 * i + 2)
                    nc.scalar.activation(z[s][:, 2 * i:2 * i + 2, :].rearrange("p k d -> p (k d)"), bank(s, i),
                                         ACT.Copy).then_inc(z_kept[s], 2)

            def normalise_z(s, at):
                act.wait_ge(z_rstd[s], at.base + U)
                for k in range(TB):
                    ins = nc.scalar.activation(z[s][:, k, :], z[s][:, k, :], ACT.Identity, bias=zr[s][:, 1, k:k + 1],
                                               scale=zr[s][:, 0, k:k + 1])
                ins.then_inc(z_normed[s], U)

            def body(now, before, seam):
                if seam:
                    next_high_weight("qk", now.layer, t_psum[B_], before)
                high_hT(A_, now)
                if before:
                    gate(B_, before, 0)
                    high_h(A_, now)
                    high_u(B_, before, 0)
                    gate(B_, before, 1)
                    high_u(B_, before, 1)
                    load_table(ACT.Gelu)
                else:
                    high_h(A_, now)
                    high_weight("vm", 0)
                high_t(A_, now)
                if seam:
                    next_high_weight("vm", now.layer, m_psum[B_], before)
                if before:
                    keep_z(A_, before)
                else:
                    empty_fold(1)
                high_p(A_, now, range(TB))
                if not before:
                    for name in ("m2", "f1", "f2"):
                        high_weight(name, 0)
                if seam:
                    next_high_weight("m2", now.layer, m2_psum[B_], before)
                if before:
                    for c in range(DC):
                        high_y(B_, before, c)
                    high_r(A_, now)
                    hidden(B_, before)
                    high_f(B_, before, FC - 1)
                else:
                    high_r(A_, now)
                    empty_fold(2)
                load_table(ACT.Silu)
                for c in range(DC):
                    gate(A_, now, c)
                    high_u(A_, now, c)
                if not before:
                    empty_fold(3)
                high_hT(B_, now)
                load_table(ACT.Gelu)
                high_h(B_, now)
                if seam:
                    next_high_weight("f1", now.layer, f1_psum[B_], before)
                if seam:
                    next_high_weight("f2", now.layer, f2_psum[B_], before)
                high_t(B_, now)
                if before:
                    keep_z(B_, before)
                high_p(B_, now, (0,))
                high_y(A_, now, 0)
                high_p(B_, now, (1,))
                high_y(A_, now, 1)
                high_p(B_, now, (2, 3))
                if before:
                    normalise_z(A_, before)
                hidden(A_, now)
                high_f(A_, now, FC - 1)
                load_table(ACT.Silu)
                high_r(B_, now)
                if before:
                    normalise_z(B_, before)

            def first(now):
                empty_fold(0)
                order_constants()
                act.wait_ge(fold_out, 3)
                act.wait_ge(raw_loaded, 3 * DMA)
                high_weight("qk", 0)
                body(now, None, False)

            def tail(last):
                for c in range(DC):
                    gate(B_, last, c)
                    high_u(B_, last, c)
                load_table(ACT.Gelu)
                keep_z(A_, last)
                for c in range(DC):
                    high_y(B_, last, c)
                hidden(B_, last)
                high_f(B_, last, FC - 1)
                normalise_z(A_, last)
                keep_z(B_, last)
                normalise_z(B_, last)

            assert L == 4
            run_steps(act, first, body, tail)

        SCALE_CHAIN, GN_CHAIN, LN_CHAIN = 3, 10, 3

        @block.vector
        def _(dve):

            def landed(ins, done, value):
                ins.then_inc(done, 1)
                dve.wait_ge(done, value)

            def sub_hi(lo, full, hi, done, n):
                nc.vector.tensor_tensor(out=lo, in0=full, in1=f32(hi), op=ALU.subtract).then_inc(done, n)

            def next_constants(s, l):
                nc.vector.tensor_copy(lc[s][:, :], const_cols[:, bass.ds(l * LC, LC)]).then_inc(lc_ready[s], 1)

            def low_hT(s, at):
                for c in range(DC):
                    dve.wait_ge(hT_hi[s], at.base + 2 * c + 2)
                    sub_hi(hT_sp[s][1][:, c, :], bank(s, 2 + c), hT_sp[s][0][:, c, :], hT_lo[s], 2)

            def low_t(s, at, c):
                dve.wait_ge(t_hi[s], at.base + 2 * c + 2)
                sub_hi(tu_sp[s][1][:, c, :], bank(s, 2 + c), tu_sp[s][0][:, c, :], t_lo[s], 2)

            def low_p(s, at, blocks):
                for b in blocks:
                    dve.wait_ge(p_hi[s], at.base + b + 1)
                    sub_hi(pf_sp[s][1][:, b, LO[b]:S], score_bank(s, b)[:, LO[b]:S], pf_sp[s][0][:, b, LO[b]:S], p_lo[s], 1)

            def low_r(s, at):
                for c in range(DC):
                    dve.wait_ge(r_hi[s], at.base + 2 * c + 2)
                    sub_hi(ry_sp[s][1][:, c, :], bank(s, 2 + c), ry_sp[s][0][:, c, :], r_lo[s], 2)

            def low_u(s, at, c):
                dve.wait_ge(u_hi[s], at.base + 2 * c + 2)
                sub_hi(tu_sp[s][1][:, c, :], tmp[s][:, c, :], tu_sp[s][0][:, c, :], u_lo[s], 2)

            def low_y(s, at, c):
                dve.wait_ge(y_hi[s], at.base + 2 * c + 2)
                sub_hi(ry_sp[s][1][:, c, :], y[s][:, c, :], ry_sp[s][0][:, c, :], y_lo[s], 2)

            def divisor(s, at):
                base = at.it * SCALE_CHAIN
                dve.wait_ge(rowsum_psum[s], at.base + U)
                landed(nc.vector.tensor_tensor(out=y[s][:, 1, :], in0=bank(s, 0), in1=floor[:, :], op=ALU.max), scale_done[s], base + 1)
                nc.vector.scalar_tensor_tensor(out=y[s][:, 1, :], in0=bank(s, 0), scalar=-1.0, in1=y[s][:, 1, :],
                                               op0=ALU.mult, op1=ALU.max).then_inc(scale_done[s], 1)

            def invert(s, at):
                base = at.it * SCALE_CHAIN
                dve.wait_ge(scale_done[s], base + 2)
                nc.vector.reciprocal(inv[s], y[s][:, 1, :]).then_inc(scale_done[s], 1)

            def scaled(s, at, c, banks, out, which, done):
                dve.wait_ge(m_psum[s], at.base + 2 * c + which)
                dve.wait_ge(scale_done[s], at.it * SCALE_CHAIN + SCALE_CHAIN)
                nc.vector.tensor_tensor(out=tmp[s][:, out + c, :], in0=bank(s, banks[c]), in1=inv[s], op=ALU.mult).then_inc(done[s], 2)

            def gated(s, at, c):
                dve.wait_ge(value_scaled[s], at.base + 2 * c + 2)
                dve.wait_ge(gate_ready[s], at.base + 2 * c + 2)
                nc.vector.scalar_tensor_tensor(
                    out=tmp[s][:, c, :], in0=tmp[s][:, c, :], scalar=lc_bm1[s][:, c:c + 1],
                    in1=tmp[s][:, 2 + c, :], op0=ALU.add, op1=ALU.mult).then_inc(u_ready[s], 2)

            def gated_products(s, at, meanwhile=lambda part: None):
                scaled(s, at, 0, GATE, 2, 1, gate_scaled)
                scaled(s, at, 0, VALUE, 0, 2, value_scaled)
                meanwhile(0)
                gated(s, at, 0)
                scaled(s, at, 1, GATE, 2, 1, gate_scaled)
                low_u(s, at, 0)
                scaled(s, at, 1, VALUE, 0, 2, value_scaled)
                gated(s, at, 1)
                meanwhile(1)
                low_u(s, at, 1)

            def group_parts(s):
                sq, mom, rstd = gsm[s][:, 0:2], gsm[s][:, 2:4], gsm[s][:, 5:6]
                return sq, mom, rstd, gsm[s][:, 6:8], gsm[s][:, 8:10], gsm[s][:, 10:12]

            def groupnorm_in(s, at):
                sq, mom, rstd, gain, off0, off = group_parts(s)
                base = at.it * GN_CHAIN
                for c in range(DC):
                    dve.wait_ge(m2_psum[s], at.base + 2 * c + 2)
                    ins = nc.vector.bn_stats(gstat[s][:, c, :], bank(s, OUT[c]))
                landed(ins, gn_done[s], base + 1)
                hold(dve, dve_held)
                for c in range(DC):
                    ins = nc.vector.bn_aggr(gmv[s][:, c, :], gstat[s][:, c, :])
                landed(ins, gn_done[s], base + 2)
                landed(nc.vector.tensor_tensor(out=gin[s][:, 0:2], in0=gmv[s][:, :, 0], in1=lc_bm2[s], op=ALU.add), gn_done[s], base + 3)
                landed(nc.vector.tensor_tensor(out=sq, in0=gin[s][:, 0:2], in1=gin[s][:, 0:2], op=ALU.mult), gn_done[s], base + 4)
                nc.vector.scalar_tensor_tensor(out=gin[s][:, 2:4], in0=sq, scalar=EPS, in1=gmv[s][:, :, 1],
                                               op0=ALU.add, op1=ALU.add).then_inc(gn_in[s], U)

            def groupnorm_var(s, at):
                sq, mom, rstd, gain, off0, off = group_parts(s)
                base = at.it * GN_CHAIN
                dve.wait_ge(gn_psum[s], at.base + U)
                landed(nc.vector.tensor_reduce(out=mom, in_=bank(s, MOMENTS)[:, 0:4].rearrange("p (q c) -> p q c", c=DC),
                                               op=ALU.add, axis=AX.X), gn_done[s], base + 5)
                nc.vector.scalar_tensor_tensor(out=rstd, in0=mom[:, 0:1], scalar=mom[:, 0:1], in1=mom[:, 1:2],
                                               op0=ALU.mult, op1=ALU.subtract, reverse1=True).then_inc(g_var[s], U)

            def groupnorm_out(s, at):
                sq, mom, rstd, gain, off0, off = group_parts(s)
                base = at.it * GN_CHAIN
                dve.wait_ge(g_rstd[s], at.base + U)
                landed(nc.vector.tensor_scalar(gain, lc_gg[s], rstd, None, ALU.mult), gn_done[s], base + 6)

                def gained(c):
                    nc.vector.scalar_tensor_tensor(
                        out=tmp[s][:, c, :], in0=bank(s, OUT[c]), scalar=gain[:, c:c + 1], in1=f32(hT_sp[s][0][:, c, :]),
                        op0=ALU.mult, op1=ALU.add).then_inc(gn_done[s], 1)

                nc.vector.scalar_tensor_tensor(out=off0, in0=lc_bm2[s], scalar=mom[:, 0:1], in1=gain,
                                               op0=ALU.subtract, op1=ALU.mult).then_inc(gn_done[s], 1)
                def summed(c):
                    nc.vector.scalar_tensor_tensor(
                        out=y[s][:, c, :], in0=tmp[s][:, c, :], scalar=off[:, c:c + 1], in1=f32(hT_sp[s][1][:, c, :]),
                        op0=ALU.add, op1=ALU.add).then_inc(y_ready[s], 2)

                gained(0)
                dve.wait_ge(gn_done[s], base + 7)
                nc.vector.tensor_tensor(out=off, in0=off0, in1=lc_gb[s], op=ALU.add).then_inc(gn_done[s], 1)
                dve.wait_ge(gn_done[s], base + 9)
                summed(0)
                gained(1)
                low_y(s, at, 0)
                dve.wait_ge(gn_done[s], base + 10)
                summed(1)
                low_y(s, at, 1)

            def residual(s, at, c):
                dve.wait_ge(f2_psum[s], at.base + 2 * c + 2)
                nc.vector.scalar_tensor_tensor(
                    out=y[s][:, c, :], in0=bank(s, c), scalar=lc_bf2[s][:, c:c + 1], in1=y[s][:, c, :],
                    op0=ALU.add, op1=ALU.add).then_inc(z_ready[s], 2)

            def layernorm_stats(s, at, blocks):
                dve.wait_ge(z_kept[s], at.base + 2 * U)
                for k in blocks:
                    ins = nc.vector.bn_stats(zstat[s][:, k, :], z[s][:, k, :])
                ins.then_inc(ln_done[s], 1)

            def layernorm_var(s, at):
                base = at.it * LN_CHAIN
                dve.wait_ge(ln_done[s], base + 2)
                hold(dve, dve_held)
                for k in range(TB):
                    ins = nc.vector.bn_aggr(zmv[s][:, k, :], zstat[s][:, k, :])
                landed(ins, ln_done[s], base + 3)
                nc.vector.tensor_scalar(zr[s][:, 1, :], zmv[s][:, :, 0], -1.0, None, ALU.mult)
                nc.vector.tensor_scalar(zr[s][:, 0, :], zmv[s][:, :, 1], EPS, None, ALU.add).then_inc(z_var[s], U)

            HALVES = ((0, 1), (2, 3))

            def body(now, before, seam):
                if before:
                    for c in range(DC):
                        residual(A_, before, c)
                if seam:
                    dve.wait_ge(z_ready[A_], before.base + U)
                    hold(dve, dve_held)
                    next_constants(A_, now.layer)
                low_hT(A_, now)
                if before:
                    gated_products(B_, before)
                low_t(A_, now, 0)
                low_t(A_, now, 1)
                if before:
                    groupnorm_in(B_, before)
                low_p(A_, now, (0,))
                if before:
                    groupnorm_var(B_, before)
                low_p(A_, now, (1, 2, 3))
                if before:
                    groupnorm_out(B_, before)
                divisor(A_, now)
                low_r(A_, now)
                invert(A_, now)
                if seam:
                    dve.wait_ge(lc_ready[A_], now.layer + 1)
                if before:
                    gated_products(A_, now, lambda part: layernorm_stats(A_, before, HALVES[part]))
                    layernorm_var(A_, before)
                    residual(B_, before, 0)
                else:
                    gated_products(A_, now)
                low_hT(B_, now)
                groupnorm_in(A_, now)
                if before:
                    residual(B_, before, 1)
                if seam:
                    dve.wait_ge(z_ready[B_], before.base + U)
                    hold(dve, dve_held)
                    next_constants(B_, now.layer)
                low_t(B_, now, 0)
                groupnorm_var(A_, now)
                low_t(B_, now, 1)
                groupnorm_out(A_, now)
                low_p(B_, now, range(TB))
                if before:
                    for blocks in HALVES:
                        layernorm_stats(B_, before, blocks)
                    layernorm_var(B_, before)
                divisor(B_, now)
                low_r(B_, now)
                invert(B_, now)

            def first(now):
                dve.wait_ge(const_ready, 1)
                for s in range(SLOTS):
                    next_constants(s, 0)
                    dve.wait_ge(lc_ready[s], 1)
                body(now, None, False)

            def tail(last):
                for c in range(DC):
                    residual(A_, last, c)
                gated_products(B_, last)
                groupnorm_in(B_, last)
                groupnorm_var(B_, last)
                groupnorm_out(B_, last)
                for blocks in HALVES:
                    layernorm_stats(A_, last, blocks)
                layernorm_var(A_, last)
                for c in range(DC):
                    residual(B_, last, c)
                for blocks in HALVES:
                    layernorm_stats(B_, last, blocks)
                layernorm_var(B_, last)
                layernorm_out(dve, nc.vector, B_, last)

            run_steps(dve, first, body, tail)

        @block.tensor
        def _(pe):
            def mm3(out, w, x, first, last):
                nc.tensor.matmul(out, w[0], x[0], start=first, stop=False, skip_group_check=True)
                nc.tensor.matmul(out, w[0], x[1], start=False, stop=False, skip_group_check=True)
                return nc.tensor.matmul(out, w[1], x[0], start=False, stop=last, skip_group_check=True)

            def both(pair, *index):
                return [t[index] for t in pair]

            ALL = slice(None)

            def cols(n):
                return slice(n * P, (n + 1) * P)

            pe.wait_ge(ident_ready, 1)
            pe.wait_ge(pool_consts, 4)
            def fold(l):
                pe.wait_ge(qkv_loaded, 4 * DMA * (l + 1))
                if l:
                    pe.wait_ge(fold_out, 3 * l)
                for i in range(3):
                    for cc in range(DC):
                        for dh in range(DC):
                            ins = nc.tensor.transpose(bank(B_, i)[:, cc * D + dh * P:cc * D + (dh + 1) * P],
                                                      raw_kqv[i][:, dh * D + cc * P:dh * D + (cc + 1) * P], ident[:, :])
                    ins.then_inc(wt_psum, 1)
                wt = w_t.rearrange("p i (c d) -> p i c d", c=DC)
                pe.wait_ge(wt_ready, 3 * l + 2)
                for dh in range(DC):
                    for cc in range(DC):
                        ins = nc.tensor.matmul(bank(B_, 3)[:, dh * D:(dh + 1) * D], wt[:, 1, cc, cols(dh)], wt[:, 0, cc, :],
                                               start=cc == 0, stop=cc == DC - 1)
                ins.then_inc(fold_psum, 1)
                pe.wait_ge(wt_ready, 3 * l + 3)
                for dh in range(DC):
                    for cc in range(DC):
                        ins = nc.tensor.matmul(bank(B_, dh), wt[:, 2, cc, cols(dh)], raw_m1[:, cc, :],
                                               start=cc == 0, stop=cc == DC - 1)
                    ins.then_inc(fold_psum, 1)

            def transpose_h(s, at):
                pe.wait_ge(h_loaded[s], at.it * DMA + DMA)
                for c in range(DC):
                    for k in range(TB):
                        ins = nc.tensor.transpose(bank(s, 2 + c)[:, cols(k)], h_in[s][:, k, cols(c)], ident[:, :])
                    ins.then_inc(hT_psum[s], 2)

            def project_t(s, at, c):
                w = weight("qk", DC)
                pe.wait_ge(w_lo["qk"], at.layer + 1)
                for k in range(DC):
                    pe.wait_ge(hT_lo[s], at.base + 2 * k + 2)
                    ins = mm3(bank(s, 2 + c), both(w, ALL, k, cols(c)), both(hT_sp[s], ALL, k), k == 0, k == DC - 1)
                ins.then_inc(t_psum[s], 2)

            def scores(s, at, blocks):
                for b in blocks:
                    q = slice(LO[b], S)
                    if b == 2:
                        pe.wait_ge(z_kept[s], at.base + U)
                    for k in range(DC):
                        pe.wait_ge(t_lo[s], at.base + 2 * k + 2)
                        ins = mm3(score_bank(s, b)[:, q], both(hT_sp[s], ALL, k, cols(b)), both(tu_sp[s], ALL, k, q),
                                  k == 0, k == DC - 1)
                    ins.then_inc(s_psum[s], 1)

            def retain(s, at):
                def weighted_h(b):
                    q = slice(LO[b], S)
                    for c in range(DC):
                        pe.wait_ge(p_masked[s], at.base + max(b, c) + 1)
                        ins = mm3(bank(s, 2 + c)[:, q], both(h_sp[s], ALL, b, cols(c)), both(pf_sp[s], ALL, b, q),
                                  b == 0, b == TB - 1)
                        if b == TB - 1:
                            ins.then_inc(r_psum[s], 2)

                pe.wait_ge(h_lo[s], at.base + U)
                weighted_h(0)
                weighted_h(1)
                for b in range(TB):
                    q = slice(LO[b], S)
                    pe.wait_ge(p_masked[s], at.base + max(b, 2) + 1)
                    for half in range(2):
                        ins = nc.tensor.matmul(bank(s, 0)[:, q], ones_r[:, :], pf_sp[s][half][:, b, q],
                                               start=b == 0 and half == 0, stop=b == TB - 1 and half == 1,
                                               skip_group_check=True)
                ins.then_inc(rowsum_psum[s], U)
                weighted_h(2)
                weighted_h(3)

            def gated_projection(s, at):
                w = weight("vm", DC)
                pe.wait_ge(w_lo["vm"], at.layer + 1)
                for r, n in ((GATE[0], DC), (VALUE[0], 0), (GATE[1], DC + 1), (VALUE[1], 1)):
                    if r == 0:
                        pe.wait_ge(scale_done[s], at.it * SCALE_CHAIN + 2)
                    for k in range(DC):
                        pe.wait_ge(r_lo[s], at.base + 2 * k + 2)
                        ins = mm3(bank(s, r), both(w, ALL, k, cols(n)), both(ry_sp[s], ALL, k), k == 0, k == DC - 1)
                    ins.then_inc(m_psum[s], 1)

            def out_projection(s, at):
                w = weight("m2", DC)
                pe.wait_ge(w_lo["m2"], at.layer + 1)
                for c in range(DC):
                    for k in range(DC):
                        pe.wait_ge(u_lo[s], at.base + 2 * k + 2)
                        ins = mm3(bank(s, OUT[c]), both(w, ALL, k, cols(c)), both(tu_sp[s], ALL, k), k == 0, k == DC - 1)
                    ins.then_inc(m2_psum[s], 2)

            def group_moments(s, at):
                pe.wait_ge(gn_in[s], at.base + U)
                nc.tensor.matmul(bank(s, MOMENTS)[:, 0:2 * DC], mean_w[:, :], gin[s][:, :], start=True,
                                 stop=True).then_inc(gn_psum[s], U)

            def up_projection(s, at):
                w = weight("f1", DC)
                pe.wait_ge(w_lo["f1"], at.layer + 1)
                for k in range(DC):
                    pe.wait_ge(y_lo[s], at.base + 2 * k + 2)
                    for n in range(FC):
                        ins = mm3(bank(s, n), both(w, ALL, k, cols(n)), both(ry_sp[s], ALL, k), k == 0, k == DC - 1)
                        if k == DC - 1:
                            ins.then_inc(f1_psum[s], 1)

            def down_projection(s, at, c, hidden=range(FC)):
                w = weight("f2", FC)
                pe.wait_ge(w_lo["f2"], at.layer + 1)
                for k in hidden:
                    pe.wait_ge(f_lo[s], at.base + k + 1)
                    ins = mm3(bank(s, c), both(w, ALL, k, cols(c)), both(pf_sp[s], ALL, k), k == 0, k == FC - 1)
                if k == FC - 1:
                    ins.then_inc(f2_psum[s], 2)

            def transpose_z(s, at):
                pe.wait_ge(z_ready[s], at.base + U)
                for k in range(TB):
                    for c in range(DC):
                        to = (k % 2) * D + c * P
                        ins = nc.tensor.transpose(bank(s, k // 2)[:, to:to + P], y[s][:, c, cols(k)], ident[:, :])
                    if k % 2:
                        ins.then_inc(zT_psum[s], 2)

            def body(now, before, seam):
                transpose_h(A_, now)
                if before:
                    gated_projection(B_, before)
                for c in range(DC):
                    project_t(A_, now, c)
                if before:
                    transpose_z(A_, before)
                    out_projection(B_, before)
                else:
                    fold(1)
                scores(A_, now, (0, 1, 2))
                if before:
                    group_moments(B_, before)
                scores(A_, now, (3,))
                retain(A_, now)
                if before:
                    up_projection(B_, before)
                else:
                    fold(2)
                gated_projection(A_, now)
                if before:
                    down_projection(B_, before, 0)
                else:
                    fold(3)
                    pe.wait_ge(fold_out, 3 * L)
                transpose_h(B_, now)
                if before:
                    down_projection(B_, before, 1, (0, 1))
                out_projection(A_, now)
                if before:
                    down_projection(B_, before, 1, (2, 3))
                for c in range(DC):
                    project_t(B_, now, c)
                group_moments(A_, now)
                if before:
                    transpose_z(B_, before)
                scores(B_, now, range(TB))
                up_projection(A_, now)
                retain(B_, now)
                for c in range(DC):
                    down_projection(A_, now, c)

            def first(now):
                fold(0)
                pe.wait_ge(consts_loaded, 7 * DMA)
                nc.tensor.transpose(bank(A_, 0)[:, 0:L * LC], const_rows[:, :], ident[0:L * LC, 0:L * LC]).then_inc(const_psum, 1)
                body(now, None, False)

            def tail(last):
                gated_projection(B_, last)
                transpose_z(A_, last)
                out_projection(B_, last)
                group_moments(B_, last)
                up_projection(B_, last)
                for c in range(DC):
                    down_projection(B_, last, c)
                transpose_z(B_, last)

            run_steps(pe, first, body, tail)


def expert_mixture(nc, x, h_last, Wr, br, W1, b1, W2, b2, out, h_stored, stores, dve_held, pool_held):
    E, D, F = W1.shape
    B, S, _ = x.shape
    DC, FC, TB = D // P, F // P, S // P
    NB = B * TB
    RING = 4
    FULL = 2
    AHEAD = 2
    HID = 2
    OUTS = 2
    SPARE = OUTS
    POW_AT = 5

    x_v = x.rearrange("t (k p) d -> t p k d", p=P)
    h_v = h_last.rearrange("i s (k p) d -> (i s) p k d", p=P)
    out_v = out.rearrange("t (k p) d -> t p k d", p=P)
    w1_v = W1.rearrange("e (c p) f -> e p c f", p=P)
    w2_v = W2.rearrange("e (c p) d -> e p c d", p=P)

    with ExitStack() as ctx:
        def sb(name, shape, dt=F32):
            return ctx.enter_context(nc.sbuf_tensor(name, shape, dt))

        def sem(name):
            return ctx.enter_context(nc.semaphore(name))

        ident = sb("m_ident", [P, P])
        b1_rows = sb("b1_rows", [E * FC, P])
        b1_cols = sb("b1_cols", [P, E * FC])
        b1_e = sb("b1_e", [P, FC])
        b2_bc = sb("b2_bc", [P, 2, D])
        wr = sb("wr", [P, DC, E])
        br_bc = sb("br_bc", [P, E])
        x1T = [sb(f"x1T_{n}", [P, DC, B * S], F32R) for n in ("hi", "lo")]
        acc = sb("acc", [P, NB, D])
        raw1 = sb("raw1", [P, DC * F])
        raw2 = sb("raw2", [P, FC * D])
        w_even = sb("w_even", [P, 4, DC * F], F32R)
        with ExitStack() as early:
            def before(name, shape):
                return early.enter_context(nc.sbuf_tensor(name, shape, F32))

            xh = before("xh", [P, NB, D])
            x1 = [before(f"x1_{n}", [P, TB, D]) for n in range(2)]
            x1Tf = [before(f"x1Tf{n}", [P, DC, S]) for n in range(2)]
        w_odd = sb("w_odd", [P, 4, DC * F], F32R)
        hid = [sb(f"hid_{n}", [P, RING, S], F32R) for n in ("hi", "lo")]
        w1 = [[w[:, 0, :], w[:, 1, :]] for w in (w_even, w_odd)]
        w2 = [[w[:, 2, :], w[:, 3, :]] for w in (w_even, w_odd)]
        act32 = sb("act32", [P, FULL, S])
        tile_out = sb("tile_out", [P, TB, D])
        stat = [sb(f"m_stat{n}", [P, TB, 6]) for n in range(2)]
        mv = [sb(f"m_mv{n}", [P, TB, 2]) for n in range(2)]
        rstd = [sb(f"rstd{n}", [P, TB]) for n in range(2)]
        neg_half = sb("m_neg_half", [P, TB])
        gates = sb("gates", [P, NB, E])
        ent_w = tile_out[:, 0, 0:NB * E].rearrange("p (n e) -> p n e", e=E)
        ent_s = tile_out[:, 1, 0:NB * 8].rearrange("p (i n) -> p i n", n=NB)

        ps = ctx.enter_context(nc.psum_tensor("m_ps", [P, 8, 512], F32))

        def hid_bank(n):
            return ps[:, n % HID, :]

        def out_half(parity, half):
            return ps[:, HID + 2 * parity + half, :]

        def out_bank(parity, k):
            return out_half(parity, k // 2)[:, (k % 2) * D:(k % 2 + 1) * D]

        def xT_bank(parity, c):
            return ps[:, 2 * parity + c, :]

        logit_bank, b1_bank = ps[:, 4, :], ps[:, 5, :]

        consts_loaded, ident_zero, ident_ready = sem("m_consts"), sem("m_ident_zero"), sem("m_ident_ready")
        b1_psum, b1_ready = sem("b1_psum"), sem("b1_ready")
        xh_loaded = [sem("xh_loaded_even"), sem("xh_loaded_odd")]
        x1_ready, x1_kept = sem("x1_ready"), sem("x1_kept")
        xT_psum, xT_full, xT_split, logits = sem("xT_psum"), sem("xT_full"), sem("xT_split"), sem("logits")
        raw_loaded, b2_loaded = sem("m_raw_loaded"), [sem("b2_loaded_even"), sem("b2_loaded_odd")]
        w_high, w1_split, w2_split = sem("w_high"), sem("w1_split"), sem("w2_split")
        hid_psum, hid_relu, hid_split, hid_used = sem("hid_psum"), sem("hid_relu"), sem("hid_split"), sem("hid_used")
        b2_added, out_added = sem("b2_added"), sem("out_added")
        y_ready, y_stored = sem("out_ready"), sem("out_stored")
        m_var, m_rstd = sem("m_var"), sem("m_rstd")
        dve_done, act_held = sem("m_dve_done"), sem("m_act_held")

        block = ctx.enter_context(nc.Block())

        @block.sync
        def _(sp):
            def load_tile(t, parity):
                if not isinstance(t, int):
                    t = sp.snap(t)
                sp.dma_start(acc[:, bass.ds(t * TB, TB), :], x_v[t]).then_inc(xh_loaded[parity], DMA)
                sp.dma_start(xh[:, bass.ds(t * TB, TB), :], h_v[t]).then_inc(xh_loaded[parity], DMA)

            def load_weights(e):
                sp.dma_start(raw1[:, :].rearrange("p (c f) -> p c f", c=DC), w1_v[e]).then_inc(raw_loaded, DMA)
                sp.dma_start(raw2[:, :].rearrange("p (c d) -> p c d", c=FC), w2_v[e]).then_inc(raw_loaded, DMA)

            def load_bias(e, parity):
                sp.dma_start(b2_bc[:, parity, :], b2[bass.ds(e, 1), :].to_broadcast([P, D])).then_inc(b2_loaded[parity], DMA)

            def next_expert(e, parity):
                sp.wait_ge(w1_split, e)
                sp.wait_ge(w2_split, e)
                load_weights(e)
                sp.wait_ge(b2_added, 2 * B * (e - 1) + 2 * OUTS)
                load_bias(e, parity)

            for t in range(2):
                load_tile(t, t)
            for dst, src in ((b1_rows[:, :], b1.rearrange("e (n p) -> (e n) p", p=P)),
                             (wr[:, :, :], Wr.rearrange("(c p) e -> p c e", p=P)),
                             (br_bc[:, :], br.rearrange("(a e) -> a e", a=1).to_broadcast([P, E]))):
                sp.dma_start(dst, src).then_inc(consts_loaded, DMA)
            for stored in h_stored:
                sp.wait_ge(stored, stores * DMA)

            def load_pair(pair):
                for parity in range(2):
                    sp.wait_ge(m_var, pair * 2 + parity - 1)
                    load_tile(pair * 2 + parity, parity)

            load_pair(1)
            load_weights(0)
            with sp.Fori(2, B // 2) as pair:
                load_pair(pair)
            for e in range(2):
                load_bias(e, e)
            sp.wait_ge(w1_split, 1)
            sp.wait_ge(w2_split, 1)
            load_weights(1)
            with sp.Fori(1, E // 2) as pair:
                for parity in range(2):
                    next_expert(sp.snap(pair * 2 + parity), parity)
            with sp.Fori(0, B) as t:
                sp.wait_ge(y_ready, t + 1)
                sp.dma_start(out_v[t], acc[:, bass.ds(t * TB, TB), :]).then_inc(y_stored, DMA)
            sp.wait_ge(y_stored, B * DMA)

        @block.gpsimd
        def _(pool):
            pool.sem_inc(hid_split, FULL)
            pool.sem_inc(xT_split, 2)
            nc.gpsimd.memset(ident[:, :], 0.0).then_inc(ident_zero, 1)
            pool.wait_ge(ident_zero, 1)
            nc.gpsimd.affine_select(out=ident[:, :], in_=ident[:, :], compare_op=ALU.not_equal, fill=1.0,
                                    base=0, pattern=[[-1, P]], channel_multiplier=1).then_inc(ident_ready, 1)
            nc.gpsimd.memset(neg_half[:, :], -0.5).then_inc(ident_zero, 1)
            pool.wait_ge(ident_zero, 2)

            def rstd_tokens(n, parity):
                pool.wait_ge(m_var, n + 1)
                nc.gpsimd.tensor_tensor(out=rstd[parity][:, :], in0=rstd[parity][:, :], in1=neg_half[:, :],
                                        op=ALU.pow).then_inc(m_rstd, 1)

            def split_x1(t, parity):
                pool.wait_ge(xT_full, 2 * t + 6)
                hold(pool, pool_held)
                hi, lo = (h[:, :, bass.ds(t * S, S)] for h in x1T)
                nc.gpsimd.tensor_tensor(out=lo, in0=x1Tf[parity][:, :, :], in1=f32(hi), op=ALU.subtract).then_inc(xT_split, 1)

            rstd_tokens(0, 0)
            with pool.Fori(0, B // 2 - 1) as pair:
                for parity in range(2):
                    t = pool.snap(pair * 2 + parity)
                    rstd_tokens(t + 1, 1 - parity)
                    split_x1(t, parity)
            rstd_tokens(B - 1, (B - 1) % 2)
            for t in (B - 2, B - 1):
                split_x1(t, t % 2)

            def split_chunk(chunk, j):
                pool.wait_ge(hid_relu, chunk + j + 1 + HID)
                nc.gpsimd.tensor_tensor(out=hid[1][:, j % RING, :], in0=act32[:, j % FULL, :], in1=f32(hid[0][:, j % RING, :]),
                                        op=ALU.subtract).then_inc(hid_split, 1)

            with pool.Fori(0, (E - 1) * B + 1) as tile:
                chunk = pool.snap(tile * FC)
                for j in range(FC):
                    split_chunk(chunk, j)

            def last_tile(t, parity):
                chunk = t * FC + (E - 1) * B * FC
                for j in range(FC):
                    if j == POW_AT:
                        rstd_tokens(t + B - 1, 1 - parity)
                    split_chunk(chunk, j)

            with pool.Fori(0, B // 2 - 1) as pair:
                for parity in (1, 0):
                    last_tile(pool.snap(pair * 2 + 2 - parity), parity)
            last_tile(B - 1, 1)
            rstd_tokens(2 * B - 1, 1)

        @block.scalar
        def _(act):
            act.sem_inc(hid_relu, HID)
            act.sem_inc(xT_full, 2 * DC)
            act.sem_inc(x1_kept, 2)
            act.wait_ge(b1_psum, 1)
            nc.scalar.activation(b1_cols[:, :], b1_bank[:, 0:E * FC], ACT.Copy).then_inc(b1_ready, 1)

            def keep_tiles(pair):
                for parity in range(2):
                    t = pair * 2 + parity
                    if not isinstance(t, int):
                        t = act.snap(t)
                    act.wait_ge(x1_ready, t + 1)
                    hold(act, act_held)
                    nc.scalar.activation(acc[:, bass.ds(t * TB, TB), :], x1[parity][:, :, :], ACT.Copy).then_inc(x1_kept, 1)
                    act.wait_ge(logits, t + 1)
                    act.wait_ge(xT_split, t + 1)
                    act.wait_ge(xT_psum, t + 3)
                    hold(act, act_held)
                    for c in range(DC):
                        nc.scalar.activation(x1Tf[parity][:, c, :], xT_bank(parity, c), ACT.Copy)
                        nc.scalar.activation(x1T[0][:, c, bass.ds(t * S, S)], xT_bank(parity, c), ACT.Copy).then_inc(xT_full, 1)

            for pair in range(2):
                keep_tiles(pair)
            act.wait_ge(raw_loaded, 2 * DMA)
            for w, raw in ((w1[0], raw1), (w2[0], raw2)):
                nc.scalar.activation(w[0], raw[:, :], ACT.Copy).then_inc(w_high, 1)
            with act.Fori(2, B // 2) as pair:
                keep_tiles(pair)
            act.wait_ge(logits, B + 2)
            act.wait_ge(xT_split, B + 2)
            hold(act, act_held)
            with act.Fori(0, E) as e:
                act.wait_ge(hid_relu, e * (B * FC) + HID)
                hold(act, act_held)
                nc.scalar.activation(b1_e[:, :], b1_cols[:, bass.ds(e * FC, FC)], ACT.Copy).then_inc(b1_ready, 1)
                act.wait_ge(b1_ready, e + 2)
                hold(act, act_held)
                with act.Fori(0, B) as t:
                    chunk = act.snap((e * B + t) * FC)
                    for j in range(FC):
                        bias = b1_e[:, j:j + 1]
                        act.wait_ge(hid_psum, chunk + j + 1)
                        act.wait_ge(hid_used, chunk + j + 1)
                        nc.scalar.activation(hid[0][:, j % RING, :], hid_bank(j), ACT.Relu, bias=bias)
                        act.wait_ge(hid_split, chunk + j + 1)
                        nc.scalar.activation(act32[:, j % FULL, :], hid_bank(j), ACT.Relu, bias=bias).then_inc(hid_relu, 1)

        @block.vector
        def _(dve):
            dve.sem_inc(b2_added, 2 * OUTS)
            dve.sem_inc(out_added, 1)
            count = [0]

            def landed(ins, base=0):
                count[0] += 1
                ins.then_inc(dve_done, 1)
                dve.wait_ge(dve_done, base + count[0])

            def moments(src, t, parity, base):
                for k in range(TB):
                    ins = nc.vector.bn_stats(stat[parity][:, k, :], src[:, bass.ds(t * TB + k, 1), :])
                landed(ins, base)
                hold(dve, dve_held)
                for k in range(TB):
                    ins = nc.vector.bn_aggr(mv[parity][:, k, :], stat[parity][:, k, :])
                landed(ins, base)
                nc.vector.tensor_scalar(rstd[parity][:, :], mv[parity][:, :, 1], EPS, None, ALU.add).then_inc(m_var, 1)

            def normalise(dst, src, t, parity, n, done):
                dve.wait_ge(m_rstd, n + 1)
                for k in range(TB):
                    ins = nc.vector.tensor_scalar(dst(k), src[:, bass.ds(t * TB + k, 1), :], mv[parity][:, k, 0:1],
                                                  rstd[parity][:, k:k + 1], ALU.subtract, ALU.mult)
                ins.then_inc(done, 1)

            TILE_CHAIN = 3

            def sum_moments(t, parity, loads):
                base = t * TILE_CHAIN
                count[0] = 0
                dve.wait_ge(xh_loaded[parity], loads * (2 * DMA))
                at = bass.ds(t * TB, TB)
                landed(nc.vector.tensor_tensor(out=xh[:, at, :], in0=acc[:, at, :], in1=xh[:, at, :], op=ALU.add), base)
                hold(dve, dve_held)
                moments(xh, t, parity, base)
                assert count[0] == TILE_CHAIN

            def normalise_x1(t, parity):
                dve.wait_ge(x1_kept, t + 1)
                dve.wait_ge(xT_psum, t + 1)
                normalise(lambda k: x1[parity][:, k:k + 1, :], xh, t, parity, t, x1_ready)

            sum_moments(0, 0, 1)
            with dve.Fori(0, B // 2 - 1) as pair:
                for parity in range(2):
                    t = dve.snap(pair * 2 + parity)
                    sum_moments(dve.snap(t + 1), 1 - parity, pair + 1 + parity)
                    normalise_x1(t, parity)
            sum_moments(B - 1, 1, B // 2)
            for t in (B - 2, B - 1):
                normalise_x1(t, t % 2)

            def split_weights(parity, n):
                dve.wait_ge(w_high, 2 * n + 2)
                for w, raw, done in ((w1, raw1, w1_split), (w2, raw2, w2_split)):
                    nc.vector.tensor_tensor(out=w[parity][1], in0=raw[:, :], in1=f32(w[parity][0]),
                                            op=ALU.subtract).then_inc(done, 1)

            split_weights(0, 0)

            def each(v):
                return v.unsqueeze(2).to_broadcast([P, NB, E])

            fixed = B * TILE_CHAIN
            count[0] = 0
            mx, lo, total, above, sign, step, tot = (ent_s[:, i, :] for i in range(7))
            scores, work = gates[:, :, :], ent_w
            SPAN = 1.0 - float(E) ** -0.5

            def rowsum_of_squares(ahead):
                landed(nc.vector.scalar_tensor_tensor(out=work, in0=scores, scalar=ahead, in1=each(lo), op0=ALU.subtract, op1=ALU.subtract), fixed)
                landed(nc.vector.scalar_tensor_tensor(out=work, in0=work, scalar=0.0, in1=work, op0=ALU.max, op1=ALU.mult), fixed)
                landed(nc.vector.tensor_reduce(out=total, in_=work, op=ALU.add, axis=AX.X), fixed)

            dve.wait_ge(logits, B + 2)
            landed(nc.vector.tensor_tensor(out=scores, in0=logit_bank[:, 0:NB * E].rearrange("p (n e) -> p n e", e=E),
                                           in1=br_bc[:, :].unsqueeze(1).to_broadcast([P, NB, E]), op=ALU.add), fixed)
            landed(nc.vector.tensor_scalar(scores, scores, 0.5, None, ALU.mult), fixed)
            landed(nc.vector.tensor_reduce(out=mx, in_=scores, op=ALU.max, axis=AX.X), fixed)
            landed(nc.vector.tensor_scalar(lo, mx, -1.0, None, ALU.add), fixed)
            rowsum_of_squares(0.0)
            nc.vector.tensor_scalar(above, total, 1.0, None, ALU.is_gt)
            landed(nc.vector.tensor_scalar(step, total, 1.0, None, ALU.is_lt), fixed)
            landed(nc.vector.tensor_tensor(out=sign, in0=above, in1=step, op=ALU.subtract), fixed)
            for n in range(1, NITER + 1):
                half = SPAN * 0.5 ** n
                rowsum_of_squares(half)
                if n < NITER:
                    landed(nc.vector.tensor_tensor(out=total, in0=total, in1=sign, op=ALU.mult), fixed)
                    landed(nc.vector.tensor_tensor(out=step, in0=total, in1=sign, op=ALU.is_ge), fixed)
                    landed(nc.vector.scalar_tensor_tensor(out=lo, in0=step, scalar=half, in1=lo, op0=ALU.mult, op1=ALU.add), fixed)
            landed(nc.vector.reciprocal(tot, total), fixed)
            landed(nc.vector.tensor_tensor(out=work, in0=work, in1=each(tot), op=ALU.mult), fixed)
            landed(nc.vector.scalar_tensor_tensor(out=scores, in0=work, scalar=THRESH, in1=work, op0=ALU.is_gt, op1=ALU.mult), fixed)
            dve.wait_ge(x1_kept, B + 2)

            def add_tile(e, t, tiles, pair_e, parity_e, parity_t):
                dve.wait_ge(hid_used, (tiles + 1) * FC + RING)
                dve.wait_ge(b2_loaded[parity_e], (pair_e + 1) * DMA)
                dve.wait_ge(out_added, tiles + 1)
                for half in range(2):
                    nc.vector.tensor_tensor(out=tile_out[:, 2 * half:2 * half + 2, :],
                                            in0=out_half(parity_t, half).rearrange("p (k d) -> p k d", d=D),
                                            in1=b2_bc[:, parity_e, :].unsqueeze(1).to_broadcast([P, 2, D]),
                                            op=ALU.add).then_inc(b2_added, 1)
                dve.wait_ge(b2_added, 2 * (tiles + 1) + 2 * OUTS)
                for k in range(TB):
                    at = acc[:, bass.ds(t * TB + k, 1), :].rearrange("p o d -> p (o d)")
                    gate = gates[:, bass.ds(t * TB + k, 1), bass.ds(e, 1)].rearrange("p o d -> p (o d)")
                    ins = nc.vector.scalar_tensor_tensor(out=at, in0=tile_out[:, k, :], scalar=gate,
                                                         in1=at, op0=ALU.mult, op1=ALU.add)
                ins.then_inc(out_added, 1)

            def next_weights(e, parity):
                dve.wait_ge(raw_loaded, (e + 1) * (2 * DMA))
                for w, raw in ((w1, raw1), (w2, raw2)):
                    nc.vector.tensor_copy(w[parity][0], raw[:, :]).then_inc(w_high, 1)
                split_weights(parity, e)

            def expert(pair_e, e, parity_e):
                opening = isinstance(e, int) and e == 0
                last = isinstance(e, int) and e == E - 1

                def tile(t, out):
                    tiles = e * B + t
                    if not isinstance(tiles, int):
                        tiles = dve.snap(tiles)
                    add_tile(e, t, tiles, pair_e, parity_e, out)
                    if last:
                        dve.wait_ge(out_added, tiles + 2)
                        hold(dve, dve_held)
                        count[0] = 0
                        moments(acc, t, out, t * 2 + done)
                        normalise(lambda k: acc[:, bass.ds(t * TB + k, 1), :], acc, t, out, t + B, y_ready)

                if not last:
                    next_weights(e + 1, 1 - parity_e)
                tile(0, SPARE if opening else 0)
                with dve.Fori(0, B // 2 - 1) as pair:
                    for out in (1, 0):
                        tile(dve.snap(pair * 2 + 2 - out), out)
                tile(B - 1, 1)

            done = fixed + count[0]
            for e in range(2):
                expert(0, e, e)
            with dve.Fori(1, E // 2 - 1) as pair_e:
                for parity_e in range(2):
                    expert(pair_e, dve.snap(pair_e * 2 + parity_e), parity_e)
            for e in (E - 2, E - 1):
                expert(E // 2 - 1, e, e % 2)

        @block.tensor
        def _(pe):
            def mm3(out, w, x, first, last):
                nc.tensor.matmul(out, w[0], x[0], start=first, stop=False, skip_group_check=True)
                nc.tensor.matmul(out, w[0], x[1], start=False, stop=False, skip_group_check=True)
                return nc.tensor.matmul(out, w[1], x[0], start=False, stop=last, skip_group_check=True)

            def cols(n):
                return slice(n * P, (n + 1) * P)

            pe.sem_inc(hid_used, RING)
            pe.sem_inc(logits, 2)
            pe.sem_inc(xT_psum, 2)
            pe.wait_ge(ident_ready, 1)
            pe.wait_ge(consts_loaded, 3 * DMA)
            nc.tensor.transpose(b1_bank[:, 0:E * FC], b1_rows[:, :], ident[0:E * FC, 0:E * FC]).then_inc(b1_psum, 1)

            def transpose_x1(t, parity):
                pe.wait_ge(x1_ready, t + 1)
                pe.wait_ge(xT_full, 2 * t + 2)
                for c in range(DC):
                    for k in range(TB):
                        ins = nc.tensor.transpose(xT_bank(parity, c)[:, cols(k)], x1[parity][:, k, cols(c)], ident[:, :])
                ins.then_inc(xT_psum, 1)

            def route(t, parity):
                pe.wait_ge(xT_full, 2 * t + 6)
                for k in range(TB):
                    for c in range(DC):
                        ins = nc.tensor.matmul(logit_bank[:, bass.ds((t * TB + k) * E, E)], x1Tf[parity][:, c, cols(k)], wr[:, c, :],
                                               start=c == 0, stop=c == DC - 1)
                ins.then_inc(logits, 1)

            transpose_x1(0, 0)
            with pe.Fori(0, B // 2 - 1) as pair:
                for parity in range(2):
                    t = pe.snap(pair * 2 + parity)
                    transpose_x1(t + 1, 1 - parity)
                    route(t, parity)
            transpose_x1(B - 1, 1)
            route(B - 2, 0)
            route(B - 1, 1)
            pe.wait_ge(xT_split, B + 2)
            pe.wait_ge(b1_ready, 1)
            pe.wait_ge(w1_split, 1)
            pe.wait_ge(w2_split, 1)
            pe.wait_ge(dve_done, B * 3 + 1)

            def up(w, t, chunk, j):
                pe.wait_ge(hid_relu, chunk + j + 1)
                for c in range(DC):
                    ins = mm3(hid_bank(j), [h[:, c * F + j * P:c * F + (j + 1) * P] for h in w],
                              [h[:, c, bass.ds(t * S, S)] for h in x1T], c == 0, c == DC - 1)
                ins.then_inc(hid_psum, 1)

            def down(w, chunk, j, parity):
                pe.wait_ge(hid_split, chunk + j + 1 + FULL)
                r = j % RING
                for k in range(TB):
                    ins = mm3(out_bank(parity, k), [h[:, r, cols(k)] for h in hid],
                              [h[:, j * D:(j + 1) * D] for h in w], j == 0 and k % 2 == 0, j == FC - 1)
                ins.then_inc(hid_used, 1)

            def tile(e, parity_e, t, out, following, free=True):
                tiles = e * B + t
                chunk = tiles * FC
                if not isinstance(chunk, int):
                    tiles, chunk = pe.snap(tiles), pe.snap(chunk)
                for j in range(FC):
                    if j + AHEAD < FC:
                        up(w1[parity_e], t, chunk, j + AHEAD)
                    elif following:
                        w, t_next = following
                        if w is not w1[parity_e]:
                            pe.wait_ge(w1_split, e + 2)
                            pe.wait_ge(w2_split, e + 2)
                        up(w, t_next, chunk + FC, j + AHEAD - FC)
                    if j == 0 and free:
                        pe.wait_ge(b2_added, 2 * tiles + 2)
                    down(w2[parity_e], chunk, j, out)

            def expert(e, parity_e):
                opening = isinstance(e, int) and e == 0
                last = isinstance(e, int) and e == E - 1
                w = w1[parity_e]
                tile(e, parity_e, 0, SPARE if opening else 0, (w, 1), not opening)
                if opening:
                    tile(e, parity_e, 1, 1, (w, 2), False)
                    tile(e, parity_e, 2, 0, (w, 3), False)
                with pe.Fori(1 if opening else 0, B // 2 - 1) as pair_t:
                    for out in (1, 0):
                        t = pe.snap(pair_t * 2 + 2 - out)
                        tile(e, parity_e, t, out, (w, t + 1))
                tile(e, parity_e, B - 1, 1, None if last else (w1[1 - parity_e], 0))

            for j in range(AHEAD):
                up(w1[0], 0, 0, j)
            for e in range(2):
                expert(e, e)
            with pe.Fori(1, E // 2 - 1) as pair_e:
                for parity_e in range(2):
                    expert(pe.snap(pair_e * 2 + parity_e), parity_e)
            for e in (E - 2, E - 1):
                expert(e, e % 2)


def build(nc, x, Wkqv, Wm1, bm1, Wm2, bm2, gn_g, gn_b, Wf1, bf1, Wf2, bf2, ln_g, ln_b,
          Wr, br, W1, b1, W2, b2, score_floor, out):
    B, S, D = x.shape
    L = Wkqv.shape[0]
    pairs = B // 2
    h_store = nc.dram_tensor("h_store", ((L + 1) * pairs, 2, S, D), F32, kind="Internal").ap()
    folded = nc.dram_tensor("folded", (L, P, 6 * D), F32, kind="Internal").ap()
    with ExitStack() as ctx:
        dve_held, pool_held = (ctx.enter_context(nc.semaphore(n)) for n in ("dve_held", "pool_held"))
        h_stored = [ctx.enter_context(nc.semaphore(f"h_stored{s}")) for s in range(2)]
        retention_layers(nc, x, Wkqv, Wm1, bm1, Wm2, bm2, gn_g, gn_b, Wf1, bf1, Wf2, bf2, ln_g, ln_b,
                         score_floor, h_store, folded, h_stored, dve_held, pool_held)
        expert_mixture(nc, x, h_store[L * pairs:, :, :, :], Wr, br, W1, b1, W2, b2, out, h_stored, L * pairs + 1,
                       dve_held, pool_held)


_INS = ["L0_attn_x", "L0_attn_Wkqv", "L0_attn_Wm1", "L0_attn_bm1", "L0_attn_Wm2", "L0_attn_bm2",
        "L0_attn_gn_g", "L0_attn_gn_b", "L0_attn_Wf1", "L0_attn_bf1", "L0_attn_Wf2", "L0_attn_bf2",
        "L0_attn_ln_g", "L0_attn_ln_b", "L0_ffn_Wr", "L0_ffn_br", "L0_ffn_W1", "L0_ffn_b1", "L0_ffn_W2", "L0_ffn_b2"]


def kernel(**inputs):
    import numpy as np
    import concourse.bacc as bacc
    from concourse.bass_utils import run_bass_kernel_spmd

    arrays = {f"in_{name}": np.ascontiguousarray(inputs[name]) for name in _INS}
    B, S, D = arrays["in_L0_attn_x"].shape
    row = np.float32(np.sqrt(D)) * (1 + np.sqrt(np.arange(S, dtype=np.float32)))
    arrays["in_score_floor"] = np.ascontiguousarray(np.broadcast_to(row.astype(np.float32), (P, S)))
    nc = bacc.Bacc("TRN2", target_bir_lowering=False, num_devices=1)
    args = [nc.dram_tensor(n, a.shape, mybir.dt.from_np(a.dtype), kind="ExternalInput").ap() for n, a in arrays.items()]
    args.append(nc.dram_tensor("out", (B, S, D), F32, kind="ExternalOutput").ap())
    build(nc, *args)
    r = run_bass_kernel_spmd(nc, [arrays], core_ids=[0])
    return r.results[0]["out"]
```
